# Optimizing a Trainium2 kernel written in Bass

```python
import numpy as np
import jax
import jax.numpy as jnp

def _softmax(x, axis=-1):
    return jax.nn.softmax(x, axis=axis)

def _gelu(x):
    return jax.nn.gelu(x, approximate=True)

def _silu(x):
    return jax.nn.silu(x)

def _sigmoid(x):
    return jax.nn.sigmoid(x)

def _layernorm(x, axis=-1, eps=1e-05):
    m = jnp.mean(x, axis=axis, keepdims=True)
    v = jnp.var(x, axis=axis, keepdims=True)
    return (x - m) / jnp.sqrt(v + eps)

def _scatter_add(tgt, idx, src, axis=0):
    return tgt.at[idx].add(src)

def _segment_sum(src, seg, n):
    return jax.ops.segment_sum(src, seg, n)
kernel_name = 'mk_seq_postln_d2_jaxref_r8_738bef'

def setup_inputs(seed: int=0):
    np.random.seed(seed)
    _w = jnp.asarray

    def _L0_attn_setup():
        import jax, jax.numpy as jnp
        import numpy as np
        EPS = 1e-06
        CAP = 15.0
        NH = 8

        def soft_cap(x, cap=CAP):
            return cap * jnp.tanh(x / cap)

        def _mlstm_scan(q, k, v, i_pre, f_pre):
            B, S, nh, DQ = q.shape
            DV = v.shape[-1]
            scale = DQ ** (-0.5)

            def step(carry, xs):
                C, n, m = carry
                q_t, k_t, v_t, i_t, f_t = xs
                f_log = jax.nn.log_sigmoid(f_t)
                m_new = jnp.maximum(f_log + m, i_t)
                F = jnp.exp(f_log + m - m_new)
                I = jnp.exp(i_t - m_new)
                C_new = F[..., None, None] * C + (I[..., None] * k_t)[..., :, None] * v_t[..., None, :]
                n_new = F[..., None] * n + I[..., None] * k_t
                qs = q_t * scale
                h_num = jnp.einsum('bhd,bhdv->bhv', qs, C_new)
                qn = jnp.einsum('bhd,bhd->bh', qs, n_new)
                denom = jnp.maximum(jnp.abs(qn), jnp.exp(-m_new)) + EPS
                h = h_num / denom[..., None]
                return ((C_new, n_new, m_new), h)
            C0 = jnp.zeros((B, nh, DQ, DV), q.dtype)
            n0 = jnp.zeros((B, nh, DQ), q.dtype)
            m0 = jnp.zeros((B, nh), q.dtype)
            to_s = lambda a: jnp.moveaxis(a, 1, 0)
            (Cf, nf, mf), hs = jax.lax.scan(step, (C0, n0, m0), (to_s(q), to_s(k), to_s(v), to_s(i_pre), to_s(f_pre)))
            return (jnp.moveaxis(hs, 0, 1), (Cf, nf, mf))

        def _multihead_norm(h, gamma):
            h32 = h.astype(jnp.float32)
            mu = jnp.mean(h32, axis=-1, keepdims=True)
            var = jnp.mean((h32 - mu) ** 2, axis=-1, keepdims=True)
            hn = (h32 - mu) * jax.lax.rsqrt(var + EPS)
            return (hn * gamma).astype(h.dtype)

        def _reference_tuple_inner(x, Wq, Wk, Wv, Wog, Wig, big, Wfg, bfg, gamma, Wout):
            B, S, D = x.shape
            q = x @ Wq.T
            k = x @ Wk.T
            v = x @ Wv.T
            o_preact = x @ Wog.T
            i_pre = soft_cap(x @ Wig.T + big)
            f_pre = soft_cap(x @ Wfg.T + bfg)
            q = q.reshape(B, S, NH, -1)
            k = k.reshape(B, S, NH, -1)
            v = v.reshape(B, S, NH, -1)
            h, state = _mlstm_scan(q, k, v, i_pre, f_pre)
            h_norm = _multihead_norm(h, gamma).reshape(B, S, -1)
            h_out = jax.nn.sigmoid(o_preact) * h_norm
            y = h_out @ Wout.T
            return (y, *state)
        key = jax.random.key(seed)
        ks = jax.random.split(key, 12)
        B, S, D = (2, 256, 256)
        QK, V = (D // 2, D)
        DHV = V // NH
        s = lambda fan_in: 1.0 / np.sqrt(fan_in)
        return {'x': jax.random.normal(ks[0], (B, S, D), jnp.float32), 'Wq': jax.random.normal(ks[1], (QK, D), jnp.float32) * s(D), 'Wk': jax.random.normal(ks[2], (QK, D), jnp.float32) * s(D), 'Wv': jax.random.normal(ks[3], (V, D), jnp.float32) * s(D), 'Wog': jax.random.normal(ks[4], (V, D), jnp.float32) * s(D), 'Wig': jax.random.normal(ks[5], (NH, D), jnp.float32) * s(D), 'big': jax.random.normal(ks[6], (NH,), jnp.float32) * 0.1, 'Wfg': jax.random.normal(ks[7], (NH, D), jnp.float32) * s(D), 'bfg': jax.random.normal(ks[8], (NH,), jnp.float32) * 0.1 + 3.0, 'gamma': jnp.ones((NH, DHV), jnp.float32), 'Wout': jax.random.normal(ks[9], (D, V), jnp.float32) * s(V)}
    _L0_attn_in = _L0_attn_setup()

    def _L0_ffn_setup():
        import jax, jax.numpy as jnp
        import numpy as np
        TOP_K = 4
        NUM_EXPERTS = 16
        key = jax.random.key(seed)
        ks = jax.random.split(key, 6)
        B, S, H, I, E = (2, 128, 256, 224, NUM_EXPERTS)
        return {'x': jax.random.normal(ks[0], (B, S, H), dtype=jnp.float32), 'router_w': jax.random.normal(ks[1], (E, H), dtype=jnp.float32) * 0.02, 'expert_bias': jnp.zeros((E,), dtype=jnp.float32), 'gate_proj': jax.random.normal(ks[2], (E, H, I), dtype=jnp.float32) * 0.02, 'up_proj': jax.random.normal(ks[3], (E, H, I), dtype=jnp.float32) * 0.02, 'down_proj': jax.random.normal(ks[4], (E, I, H), dtype=jnp.float32) * 0.02}
    _L0_ffn_in = _L0_ffn_setup()

    def _L1_attn_setup():
        import jax, jax.numpy as jnp
        import numpy as np
        H = 16
        NORM = 16.0
        SCALE = 128.0 ** (-0.5)
        EPS = 1e-05

        def _gla_core(x, Wq, Wk, Wkg1, Wkg2, bkg2, Wv, Wg, bg, Wo):
            B, L, D = x.shape
            q = x @ Wq.T
            k = x @ Wk.T * SCALE
            kg = x @ Wkg1.T @ Wkg2.T + bkg2
            v = x @ Wv.T
            gproj = x @ Wg.T + bg
            dk = q.shape[-1] // H
            dv = D // H
            heads = lambda t, dh: t.reshape(B, L, H, dh).transpose(0, 2, 1, 3)
            qh = heads(q, dk)
            kh = heads(k, dk)
            vh = heads(v, dv)
            gk = jax.nn.log_sigmoid(heads(kg, dk)) / NORM
            tfirst = lambda t: t.transpose(2, 0, 1, 3)

            def step(S, inp):
                qt, kt, vt, gt = inp
                S = S * jnp.exp(gt)[..., None] + kt[..., None] * vt[..., None, :]
                ot = jnp.einsum('bhk,bhkv->bhv', qt, S)
                return (S, ot)
            S0 = jnp.zeros((B, H, dk, dv), x.dtype)
            _, os = jax.lax.scan(step, S0, (tfirst(qh), tfirst(kh), tfirst(vh), tfirst(gk)))
            o = os.transpose(1, 2, 0, 3)
            mu = o.mean(-1, keepdims=True)
            var = ((o - mu) ** 2).mean(-1, keepdims=True)
            o = (o - mu) * jax.lax.rsqrt(var + EPS)
            o = o.transpose(0, 2, 1, 3).reshape(B, L, D)
            return jax.nn.silu(gproj) * o @ Wo.T
        key = jax.random.key(seed)
        ks = jax.random.split(key, 10)
        B, L, D = (2, 256, 256)
        g = lambda k, shape, s: jax.random.normal(k, shape, jnp.float32) * s
        return {'x': g(ks[0], (B, L, D), 1.0), 'Wq': g(ks[1], (128, D), 0.02), 'Wk': g(ks[2], (128, D), 0.02), 'Wkg1': g(ks[3], (16, D), 0.02), 'Wkg2': g(ks[4], (128, 16), 0.05), 'bkg2': jnp.zeros((128,), jnp.float32), 'Wv': g(ks[5], (D, D), 0.02), 'Wg': g(ks[6], (D, D), 0.02), 'bg': jnp.zeros((D,), jnp.float32), 'Wo': g(ks[7], (D, D), 0.02)}
    _L1_attn_in = _L1_attn_setup()

    def _L1_ffn_setup():
        import jax
        import jax.numpy as jnp
        import numpy as np
        NUM_EXPERTS = 32
        HIDDEN = 256
        INTER = 96
        TOP_K = 8
        TAU = 0.05
        BATCH, SEQ = (2, 128)
        key = jax.random.key(seed)
        k1, k2, k3, k4 = jax.random.split(key, 4)
        return {'hidden_states': jax.random.normal(k1, (BATCH, SEQ, HIDDEN), dtype=jnp.float32), 'gate_weight': jax.random.normal(k2, (NUM_EXPERTS, HIDDEN), dtype=jnp.float32) * 0.02, 'gate_up_proj': jax.random.normal(k3, (NUM_EXPERTS, 2 * INTER, HIDDEN), dtype=jnp.float32) * 0.02, 'down_proj': jax.random.normal(k4, (NUM_EXPERTS, HIDDEN, INTER), dtype=jnp.float32) * 0.02, 'layer_alpha': jnp.array(1.0, dtype=jnp.float32)}
    _L1_ffn_in = _L1_ffn_setup()
    _d = {'L0_attn_x': _L0_attn_in['x'], 'L0_attn_Wq': _L0_attn_in['Wq'], 'L0_attn_Wk': _L0_attn_in['Wk'], 'L0_attn_Wv': _L0_attn_in['Wv'], 'L0_attn_Wog': _L0_attn_in['Wog'], 'L0_attn_Wig': _L0_attn_in['Wig'], 'L0_attn_big': _L0_attn_in['big'], 'L0_attn_Wfg': _L0_attn_in['Wfg'], 'L0_attn_bfg': _L0_attn_in['bfg'], 'L0_attn_gamma': _L0_attn_in['gamma'], 'L0_attn_Wout': _L0_attn_in['Wout'], 'L0_ffn_router_w': _L0_ffn_in['router_w'], 'L0_ffn_expert_bias': _L0_ffn_in['expert_bias'], 'L0_ffn_gate_proj': _L0_ffn_in['gate_proj'], 'L0_ffn_up_proj': _L0_ffn_in['up_proj'], 'L0_ffn_down_proj': _L0_ffn_in['down_proj'], 'L1_attn_Wq': _L1_attn_in['Wq'], 'L1_attn_Wk': _L1_attn_in['Wk'], 'L1_attn_Wkg1': _L1_attn_in['Wkg1'], 'L1_attn_Wkg2': _L1_attn_in['Wkg2'], 'L1_attn_bkg2': _L1_attn_in['bkg2'], 'L1_attn_Wv': _L1_attn_in['Wv'], 'L1_attn_Wg': _L1_attn_in['Wg'], 'L1_attn_bg': _L1_attn_in['bg'], 'L1_attn_Wo': _L1_attn_in['Wo'], 'L1_ffn_gate_weight': _L1_ffn_in['gate_weight'], 'L1_ffn_gate_up_proj': _L1_ffn_in['gate_up_proj'], 'L1_ffn_down_proj': _L1_ffn_in['down_proj'], 'L1_ffn_layer_alpha': _L1_ffn_in['layer_alpha']}
    _x0 = _d['L0_attn_x']
    _d['L0_attn_x'] = jax.random.normal(jax.random.fold_in(jax.random.key(seed), 1), (4, 256, 256), dtype=_x0.dtype)
    del _x0
    return _d

def reference(L0_attn_x, L0_attn_Wq, L0_attn_Wk, L0_attn_Wv, L0_attn_Wog, L0_attn_Wig, L0_attn_big, L0_attn_Wfg, L0_attn_bfg, L0_attn_gamma, L0_attn_Wout, L0_ffn_router_w, L0_ffn_expert_bias, L0_ffn_gate_proj, L0_ffn_up_proj, L0_ffn_down_proj, L1_attn_Wq, L1_attn_Wk, L1_attn_Wkg1, L1_attn_Wkg2, L1_attn_bkg2, L1_attn_Wv, L1_attn_Wg, L1_attn_bg, L1_attn_Wo, L1_ffn_gate_weight, L1_ffn_gate_up_proj, L1_ffn_down_proj, L1_ffn_layer_alpha):

    def _L0_attn_ref(x, Wq, Wk, Wv, Wog, Wig, big, Wfg, bfg, gamma, Wout):
        import jax, jax.numpy as jnp
        import numpy as np
        EPS = 1e-06
        CAP = 15.0
        NH = 8

        def soft_cap(x, cap=CAP):
            return cap * jnp.tanh(x / cap)

        def _mlstm_scan(q, k, v, i_pre, f_pre):
            B, S, nh, DQ = q.shape
            DV = v.shape[-1]
            scale = DQ ** (-0.5)

            def step(carry, xs):
                C, n, m = carry
                q_t, k_t, v_t, i_t, f_t = xs
                f_log = jax.nn.log_sigmoid(f_t)
                m_new = jnp.maximum(f_log + m, i_t)
                F = jnp.exp(f_log + m - m_new)
                I = jnp.exp(i_t - m_new)
                C_new = F[..., None, None] * C + (I[..., None] * k_t)[..., :, None] * v_t[..., None, :]
                n_new = F[..., None] * n + I[..., None] * k_t
                qs = q_t * scale
                h_num = jnp.einsum('bhd,bhdv->bhv', qs, C_new)
                qn = jnp.einsum('bhd,bhd->bh', qs, n_new)
                denom = jnp.maximum(jnp.abs(qn), jnp.exp(-m_new)) + EPS
                h = h_num / denom[..., None]
                return ((C_new, n_new, m_new), h)
            C0 = jnp.zeros((B, nh, DQ, DV), q.dtype)
            n0 = jnp.zeros((B, nh, DQ), q.dtype)
            m0 = jnp.zeros((B, nh), q.dtype)
            to_s = lambda a: jnp.moveaxis(a, 1, 0)
            (Cf, nf, mf), hs = jax.lax.scan(step, (C0, n0, m0), (to_s(q), to_s(k), to_s(v), to_s(i_pre), to_s(f_pre)))
            return (jnp.moveaxis(hs, 0, 1), (Cf, nf, mf))

        def _multihead_norm(h, gamma):
            h32 = h.astype(jnp.float32)
            mu = jnp.mean(h32, axis=-1, keepdims=True)
            var = jnp.mean((h32 - mu) ** 2, axis=-1, keepdims=True)
            hn = (h32 - mu) * jax.lax.rsqrt(var + EPS)
            return (hn * gamma).astype(h.dtype)

        def _reference_tuple_inner(x, Wq, Wk, Wv, Wog, Wig, big, Wfg, bfg, gamma, Wout):
            B, S, D = x.shape
            q = x @ Wq.T
            k = x @ Wk.T
            v = x @ Wv.T
            o_preact = x @ Wog.T
            i_pre = soft_cap(x @ Wig.T + big)
            f_pre = soft_cap(x @ Wfg.T + bfg)
            q = q.reshape(B, S, NH, -1)
            k = k.reshape(B, S, NH, -1)
            v = v.reshape(B, S, NH, -1)
            h, state = _mlstm_scan(q, k, v, i_pre, f_pre)
            h_norm = _multihead_norm(h, gamma).reshape(B, S, -1)
            h_out = jax.nn.sigmoid(o_preact) * h_norm
            y = h_out @ Wout.T
            return (y, *state)
        return _reference_tuple_inner(x, Wq, Wk, Wv, Wog, Wig, big, Wfg, bfg, gamma, Wout)[0]

    def _L0_ffn_ref(x, router_w, expert_bias, gate_proj, up_proj, down_proj):
        import jax, jax.numpy as jnp
        import numpy as np
        TOP_K = 4
        NUM_EXPERTS = 16
        logits = jnp.einsum('bsh,eh->bse', x, router_w) + expert_bias
        scores = jax.nn.softmax(logits, axis=-1)
        top_w, top_idx = jax.lax.top_k(scores, TOP_K)
        top_w = top_w / jnp.sum(top_w, axis=-1, keepdims=True)
        g = jnp.einsum('bsh,khe->bske', x, gate_proj)
        u = jnp.einsum('bsh,khe->bske', x, up_proj)
        act = jax.nn.silu(g) * u
        out = jnp.einsum('bske,keh->bskh', act, down_proj)
        sel = jnp.take_along_axis(out, top_idx[..., None], axis=2)
        return jnp.sum(sel * top_w[..., None], axis=2)

    def _L1_attn_ref(x, Wq, Wk, Wkg1, Wkg2, bkg2, Wv, Wg, bg, Wo):
        import jax, jax.numpy as jnp
        import numpy as np
        H = 16
        NORM = 16.0
        SCALE = 128.0 ** (-0.5)
        EPS = 1e-05

        def _gla_core(x, Wq, Wk, Wkg1, Wkg2, bkg2, Wv, Wg, bg, Wo):
            B, L, D = x.shape
            q = x @ Wq.T
            k = x @ Wk.T * SCALE
            kg = x @ Wkg1.T @ Wkg2.T + bkg2
            v = x @ Wv.T
            gproj = x @ Wg.T + bg
            dk = q.shape[-1] // H
            dv = D // H
            heads = lambda t, dh: t.reshape(B, L, H, dh).transpose(0, 2, 1, 3)
            qh = heads(q, dk)
            kh = heads(k, dk)
            vh = heads(v, dv)
            gk = jax.nn.log_sigmoid(heads(kg, dk)) / NORM
            tfirst = lambda t: t.transpose(2, 0, 1, 3)

            def step(S, inp):
                qt, kt, vt, gt = inp
                S = S * jnp.exp(gt)[..., None] + kt[..., None] * vt[..., None, :]
                ot = jnp.einsum('bhk,bhkv->bhv', qt, S)
                return (S, ot)
            S0 = jnp.zeros((B, H, dk, dv), x.dtype)
            _, os = jax.lax.scan(step, S0, (tfirst(qh), tfirst(kh), tfirst(vh), tfirst(gk)))
            o = os.transpose(1, 2, 0, 3)
            mu = o.mean(-1, keepdims=True)
            var = ((o - mu) ** 2).mean(-1, keepdims=True)
            o = (o - mu) * jax.lax.rsqrt(var + EPS)
            o = o.transpose(0, 2, 1, 3).reshape(B, L, D)
            return jax.nn.silu(gproj) * o @ Wo.T
        return _gla_core(x, Wq, Wk, Wkg1, Wkg2, bkg2, Wv, Wg, bg, Wo)

    def _L1_ffn_ref(hidden_states, gate_weight, gate_up_proj, down_proj, layer_alpha):
        import jax
        import jax.numpy as jnp
        import numpy as np
        NUM_EXPERTS = 32
        HIDDEN = 256
        INTER = 96
        TOP_K = 8
        TAU = 0.05
        BATCH, SEQ = (2, 128)
        B, S, H = hidden_states.shape
        x = hidden_states.reshape(-1, H)
        T = x.shape[0]
        logits = x @ gate_weight.T
        probs = jax.nn.softmax(logits.astype(jnp.float32), axis=-1).astype(logits.dtype)
        topv, topi = jax.lax.top_k(probs, TOP_K)
        topv = topv / jnp.clip(topv.sum(axis=-1, keepdims=True), 1e-12)
        scaled = topv * layer_alpha.astype(topv.dtype)
        active = scaled >= TAU
        empty = ~jnp.any(active, axis=-1)
        fallback = jnp.arange(TOP_K)[None, :] == jnp.argmax(scaled, axis=-1)[:, None]
        active = active | empty[:, None] & fallback
        routing_weights = topv * active.astype(topv.dtype)
        routing_weights = routing_weights / jnp.clip(routing_weights.sum(axis=-1, keepdims=True), 1e-12)
        combine = jnp.zeros((T, NUM_EXPERTS), dtype=x.dtype)
        combine = combine.at[jnp.arange(T)[:, None], topi].add(routing_weights)

        def expert_step(acc, xs):
            w_gu, w_d, c_e = xs
            gu = x @ w_gu.T
            g, u = jnp.split(gu, 2, axis=-1)
            h = jax.nn.silu(g) * u
            acc = acc + h @ w_d.T * c_e[:, None]
            return (acc, None)
        out, _ = jax.lax.scan(expert_step, jnp.zeros_like(x), (gate_up_proj, down_proj, combine.T))
        return out.reshape(B, S, H)
    x = L0_attn_x
    x = _layernorm(x + _L0_attn_ref(x, L0_attn_Wq, L0_attn_Wk, L0_attn_Wv, L0_attn_Wog, L0_attn_Wig, L0_attn_big, L0_attn_Wfg, L0_attn_bfg, L0_attn_gamma, L0_attn_Wout), axis=-1)
    x = _layernorm(x + _L0_ffn_ref(x, L0_ffn_router_w, L0_ffn_expert_bias, L0_ffn_gate_proj, L0_ffn_up_proj, L0_ffn_down_proj), axis=-1)
    x = _layernorm(x + _L1_attn_ref(x, L1_attn_Wq, L1_attn_Wk, L1_attn_Wkg1, L1_attn_Wkg2, L1_attn_bkg2, L1_attn_Wv, L1_attn_Wg, L1_attn_bg, L1_attn_Wo), axis=-1)
    x = _layernorm(x + _L1_ffn_ref(x, L1_ffn_gate_weight, L1_ffn_gate_up_proj, L1_ffn_down_proj, L1_ffn_layer_alpha), axis=-1)
    return x

_drawn_inputs = setup_inputs


def setup_inputs(seed=0):
    import zlib

    import numpy as np

    out = dict(_drawn_inputs(seed))
    spreads = {'L0_attn_gamma': (1.0, 0.2),
     'L0_ffn_expert_bias': (0.0, 0.8),
     'L1_attn_bkg2': (0.0, 0.8),
     'L1_attn_bg': (0.0, 0.461)}
    factors = {'L0_attn_big': 8.0,
     'L0_ffn_router_w': 8.0,
     'L0_ffn_gate_proj': 6.983,
     'L0_ffn_up_proj': 6.903,
     'L0_ffn_down_proj': 6.889,
     'L1_attn_Wkg1': 8.0,
     'L1_attn_Wkg2': 8.0,
     'L1_ffn_gate_weight': 8.0,
     'L1_ffn_gate_up_proj': 8.0,
     'L1_ffn_down_proj': 8.0}
    for name, (base, spread) in spreads.items():
        noise = np.random.default_rng([zlib.crc32(name.encode()), seed]).standard_normal(out[name].shape)
        drawn = base * np.exp(spread * noise) if base else spread * noise
        out[name] = jnp.asarray(drawn.astype(out[name].dtype))
    for name, factor in factors.items():
        out[name] = (out[name] * factor).astype(out[name].dtype)
    return out
```

```python
from contextlib import ExitStack

import concourse.bass as bass
from concourse import mybir

ALU = mybir.AluOpType
ACT = mybir.ActivationFunctionType
F32 = mybir.dt.float32
F32R = mybir.dt.float32r
BF16 = mybir.dt.bfloat16
U32 = mybir.dt.uint32
AX_X = mybir.AxisListType.X

P = 128
BANK = 512


def build_kernel(nc, a, out):
    B, S, D = a["x"].shape
    T = B * S
    NT = T // P
    KD = D // P
    TB = S // P
    NH0 = 8
    DV0 = D // NH0
    DQ0 = P // NH0
    CAP = 15.0
    EPS_M = 1e-6
    NH1 = 16
    DV1 = D // NH1
    DK1 = P // NH1
    GATE_NORM = 16.0
    KSCALE = 128.0 ** -0.5
    EPS_G = 1e-5
    EPS_LN = 1e-5
    TAU = 0.05
    E0, I0 = a["gate0"].shape[0], a["gate0"].shape[2]
    E1, I1 = a["gateup1"].shape[0], a["gateup1"].shape[2] // 2

    V0, O0, Q0, K0, IG0, FG0 = 0, D, 2 * D, 2 * D + P, 2 * D + 2 * P, 2 * D + 2 * P + 32
    W0C = FG0 + 32
    V1, G1, Q1, K1, Z1 = 0, D, 2 * D, 2 * D + P, 2 * D + 2 * P
    W1C = Z1 + P

    with ExitStack() as ctx:
        def sb(name, shape, dt=F32):
            return ctx.enter_context(nc.sbuf_tensor(name, shape, dt))

        def sem(name):
            return ctx.enter_context(nc.semaphore(name))

        PS = ctx.enter_context(nc.psum_tensor("PS", [P, 8, BANK], F32))

        def bank(n):
            return PS[:, n, :]

        ident = sb("ident", [P, P])
        identb = sb("identb", [P, P], BF16)
        futb = sb("futb", [P, P], BF16)
        zb = sb("zb", [P, BANK], BF16)
        head_masks = sb("head_masks", [P, 4])
        gate_b = sb("gate_b", [P, 2])
        gate_bs = sb("gate_bs", [P, 2])
        gamma = sb("gamma", [P, KD])
        bias_r0 = sb("bias_r0", [P, E0])
        alpha = sb("alpha", [P, 1])
        bkg = sb("bkg", [P, 1])
        bg = sb("bg", [P, D])
        wkg2 = sb("wkg2", [16, P])
        iota_e = sb("iota_e", [P, E1])
        first8 = sb("first8", [P, 8])
        block1 = sb("block1", [P, NH1])
        sel0 = sb("sel0", [P, B * NH0], F32R)
        rep1 = sb("rep1", [P, 8, P], F32R)

        XA = sb("XA", [P, NT, D])
        XB = sb("XB", [P, NT, D])
        XH = sb("XH", [P, KD, T], F32R)
        XL = sb("XL", [P, KD, T], F32R)
        HTH, HTL = XH, XL
        OGATE = sb("OGATE", [P, NT, D])
        HC = sb("HC", [P, NT, D])
        QT = sb("QT", [P, T])

        FA = sb("FA", [P, 10240])
        at = 0

        def take(n):
            nonlocal at
            at += n
            return FA[:, at - n:at]
        XT = take(KD * T).rearrange("p (k t) -> p k t", k=KD)
        W0T = take(KD * W0C).rearrange("p (k n) -> p k n", k=KD)
        VX = take(NT * NH0 * (DV0 + 1)).rearrange("p (t h v) -> p t h v", t=NT, h=NH0)
        KTE = take(T)
        KTO = take(T)
        WO0T = take(KD * D).rearrange("p (k n) -> p k n", k=KD)
        assert at <= 10240
        at = 0
        DEC = take(T)
        KT = take(T)
        DATA1 = take(2 * T).rearrange("p (s t) -> p s t", s=2)
        STATE = take(2 * T).rearrange("p (s t) -> p s t", s=2)
        QS = take(2 * T).rearrange("p (s t) -> p s t", s=2)
        KG = take(T)
        KGL = take(T)
        RA = sb("RA", [P, max(2 * KD * W0C, 2 * KD * T)], F32R)
        W0H = RA[:, 0:KD * W0C].rearrange("p (k n) -> p k n", k=KD)
        W0L = RA[:, KD * W0C:2 * KD * W0C].rearrange("p (k n) -> p k n", k=KD)
        VTH = RA[:, 0:KD * T].rearrange("p (k t) -> p k t", k=KD)
        VTL = RA[:, KD * T:2 * KD * T].rearrange("p (k t) -> p k t", k=KD)
        WO0H = sb("WO0H", [P, KD, D], F32R)
        WO0L = sb("WO0L", [P, KD, D], F32R)
        W1T = XB[:, :, :].rearrange("p t d -> p (t d)")[:, 0:KD * W1C].rearrange("p (k n) -> p k n", k=KD)
        W1H = sb("W1H", [P, KD, W1C], F32R)
        W1L = sb("W1L", [P, KD, W1C], F32R)
        WO1T = HC[:, 0:KD, :]
        WO1H = sb("WO1H", [P, KD, D], F32R)
        WO1L = sb("WO1L", [P, KD, D], F32R)
        WRT = sb("WRT", [P, KD, E0 + E1])
        WRH = sb("WRH", [P, KD, E0 + E1], F32R)
        WRL = sb("WRL", [P, KD, E0 + E1], F32R)

        GI = sb("GI", [P, S])
        GF = sb("GF", [P, S])
        NL = sb("NL", [P, S])
        AS = sb("AS", [P, S])
        MX = sb("MX", [P, S])
        NMH = sb("NMH", [P, S], F32R)
        NML = sb("NML", [P, S])
        NMD = sb("NMD", [P, S], F32R)
        ATF = sb("ATF", [P, 2, TB, P])
        EW = sb("EW", [P, 2, 3 * P])
        WW = sb("WW", [P, 2, 3 * P])

        st = sb("st", [P, NT, 6])
        mv = sb("mv", [P, NT, 2])
        rstd = sb("rstd", [P, NT])
        rv = sb("rv", [P, NT])
        hn = sb("hn", [P, NT, 16])
        hr = sb("hr", [P, NT, 16])
        hs = sb("hs", [P, NT, 16])
        SQ = sb("SQ", [P, 2, D])
        den = sb("den", [P, 4, NH0])
        LG = sb("LG", [P, NT, E1])
        PR = sb("PR", [P, NT, E1])
        EQ = sb("EQ", [P, NT, E1])
        rsum = sb("rsum", [P, NT])
        top = sb("top", [P, NT, 8])
        tix = sb("tix", [P, NT, 8], U32)
        tif = sb("tif", [P, NT, 8])
        t1 = sb("t1", [P, NT, 8])
        t2 = sb("t2", [P, NT, 8])
        t3 = sb("t3", [P, NT, 8])
        CW = sb("CW", [P, NT, E1])

        MG = KD * 2 * I0
        MD = 2 * D
        EG = sb("EG", [P, 2, MG])
        ED = sb("ED", [P, 2, MD])
        EGH = sb("EGH", [P, 2, MG], F32R)
        EGL = sb("EGL", [P, 2, MG], F32R)
        EDH = sb("EDH", [P, 2, MD], F32R)
        EDL = sb("EDL", [P, 2, MD], F32R)
        round_mark = sb("round_mark", [P, 3])
        SIL = sb("SIL", [P, 2, 256])
        HH = sb("HH", [P, 2, 256])
        EHH = sb("EHH", [P, 2, 256], F32R)
        EHL = sb("EHL", [P, 2, 256], F32R)

        ld_const = sem("ld_const")
        ld_sel = sem("ld_sel")
        ld_x = sem("ld_x")
        ld_xt = sem("ld_xt")
        ld_w0 = sem("ld_w0")
        ld_wo0 = sem("ld_wo0")
        ld_w1 = sem("ld_w1")
        ld_wo1 = sem("ld_wo1")
        ld_wr = sem("ld_wr")
        ld_exp = [sem("ld_exp0"), sem("ld_exp1")]
        stored = sem("stored")
        zb_set = sem("zb_set")
        ones_set = sem("ones_set")
        xt_hi = sem("xt_hi")
        w0_hi = sem("w0_hi")
        x0_split = sem("x0_split")
        pool_chain = sem("pool_chain")
        w_split = sem("w_split")
        gate_mm = sem("gate_mm")
        gate_bias = sem("gate_bias")
        qk_mm = sem("qk_mm")
        tanh_done = sem("tanh_done")
        soft_done = sem("soft_done")
        act_chain = sem("act_chain")
        dve_chain = sem("dve_chain")
        nl_ready = sem("nl_ready")
        floor_ready = sem("floor_ready")
        a_ready = sem("a_ready")
        nm_ready = sem("nm_ready")
        gt_mm = sem("gt_mm")
        at_ready = sem("at_ready")
        q_ready = sem("q_ready")
        k_ready = sem("k_ready")
        vo_mm = sem("vo_mm")
        vo_done = sem("vo_done")
        r_ready = sem("r_ready")
        qk_ready = sem("qk_ready")
        e_ready = sem("e_ready")
        w_ready = sem("w_ready")
        av_done = sem("av_done")
        ao_read = sem("ao_read")
        var_ready = sem("var_ready")
        rstd_ready = sem("rstd_ready")
        gated = sem("gated")
        tp_done = sem("tp_done")
        hi_done = sem("hi_done")
        lo_done = sem("lo_done")
        y_done = sem("y_done")
        y_read = sem("y_read")
        ln_var = sem("ln_var")
        ln_rstd = sem("ln_rstd")
        x_ready = sem("x_ready")
        rt_mm = sem("rt_mm")
        rt_read = sem("rt_read")
        rt_max = sem("rt_max")
        rt_exp = sem("rt_exp")
        cw_ready = sem("cw_ready")
        exp_split = sem("exp_split")
        gu_done = sem("gu_done")
        sil_done = sem("sil_done")
        h_ready = sem("h_ready")
        ht_done = sem("ht_done")
        hhi_done = sem("hhi_done")
        hlo_done = sem("hlo_done")
        dn_done = sem("dn_done")
        g_mm = sem("g_mm")
        g_read = sem("g_read")
        dec_ready = sem("dec_ready")
        z_ready = sem("z_ready")
        vt_mm = sem("vt_mm")
        vt_hi = sem("vt_hi")
        vt_lo = sem("vt_lo")
        og_mm = sem("og_mm")
        og_pre = sem("og_pre")
        og_silu = sem("og_silu")
        vr_mm = sem("vr_mm")
        d1_done = sem("d1_done")
        s_done = sem("s_done")
        qs_done = sem("qs_done")
        o_mm = sem("o_mm")

        class Counter:
            def __init__(self, eng, s):
                self.eng, self.s, self.n = eng, s, 0

            def link(self, ins):
                ins.then_inc(self.s, 1)
                self.n += 1
                self.eng.wait_ge(self.s, self.n)

        def col(ap, n):
            return ap.unsqueeze(2).broadcast_to([P, ap.shape[1], n])

        def wait_past(eng, s, count):
            if not isinstance(count, int) or count > 0:
                eng.wait_ge(s, count)

        class Moe:
            def __init__(self, n, E, I, tiles):
                self.n, self.E, self.I, self.tiles = n, E, I, tiles
                self.units = NT // tiles
                self.total = E * self.units
                self.body = 2 * self.units
                self.IC = 2 if I > P else 1
                self.IP = I // self.IC
                self.gcols = KD * 2 * I
                self.dcols = self.IC * D
        MOES = [Moe(0, E0, I0, 1), Moe(1, E1, I1, 2)]
        UB = [0, MOES[0].total, MOES[0].total + MOES[1].total]
        EB = [0, E0, E0 + E1]

        xd = a["x"].rearrange("b (n p) d -> p (b n) d", p=P)
        outd = out.rearrange("b (n p) d -> p (b n) d", p=P)

        def run_units(eng, m, now, later):
            base = UB[m.n]

            def step(pos, u, have_past):
                if now is not None:
                    now(pos, u)
                for fn, lag in later:
                    if have_past or pos >= lag:
                        fn((pos - lag) % m.body, u - lag)
            for pos in range(m.body):
                step(pos, base + pos, False)
            with eng.Fori(1, m.total // m.body) as i:
                for pos in range(m.body):
                    step(pos, i * m.body + (base + pos), True)
            for pos in range(max(lag for _, lag in later)):
                for fn, lag in later:
                    if pos < lag:
                        fn((pos - lag) % m.body, base + m.total + pos - lag)

        block = ctx.enter_context(nc.Block())

        @block.sync
        def _(sp):
            sp.dma_start(XT, a["xT"].rearrange("(k p) t -> p k t", p=P)).then_inc(ld_xt, 16)
            sp.dma_start(W0T, a["w0T"].rearrange("(k p) n -> p k n", p=P)).then_inc(ld_w0, 16)
            consts = [(ident[:], a["ident"]), (identb[:], a["identb"]), (futb[:], a["futb"]),
                      (head_masks[:], a["head_masks"]), (gate_b[:], a["gate_b"]), (gamma[:], a["gamma"]),
                      (bias_r0[:], a["bias_r0"]), (alpha[:], a["alpha"]), (bkg[:], a["bkg"]), (bg[:], a["bg"]),
                      (wkg2[:], a["wkg2T"]), (iota_e[:], a["iota_e"]), (first8[:], a["first8"]),
                      (block1[:], a["block1"])]
            for dst, src in consts:
                sp.dma_start(dst, src).then_inc(ld_const, 16)
            sp.dma_start(WO0T, a["wo0T"].rearrange("(k p) n -> p k n", p=P)).then_inc(ld_wo0, 16)
            sp.dma_start(WRT[:], a["wrT"].rearrange("(k p) n -> p k n", p=P)).then_inc(ld_wr, 16)
            sp.dma_start(W1T, a["w1T"].rearrange("(k p) n -> p k n", p=P)).then_inc(ld_w1, 16)
            sp.dma_start(WO1T, a["wo1T"].rearrange("(k p) n -> p k n", p=P)).then_inc(ld_wo1, 16)
            sp.dma_start(XA[:], xd).then_inc(ld_x, 16)

            def load_expert(m, e, par, free_at):
                if free_at is not None:
                    sp.wait_ge(exp_split, free_at)
                if m.n == 0:
                    gu = EG[:, par, 0:m.gcols].rearrange("p (k c i) -> p k c i", k=KD, c=2)
                    sp.dma_start(gu[:, :, 0, :], a["gate0"][bass.ds(e, 1)].rearrange("o (k p) i -> p (o k) i", p=P)
                                 ).then_inc(ld_exp[par], 16)
                    sp.dma_start(gu[:, :, 1, :], a["up0"][bass.ds(e, 1)].rearrange("o (k p) i -> p (o k) i", p=P)
                                 ).then_inc(ld_exp[par], 16)
                    src = a["down0"]
                else:
                    sp.dma_start(EG[:, par, 0:m.gcols].rearrange("p (k c) -> p k c", k=KD),
                                 a["gateup1"][bass.ds(e, 1)].rearrange("o (k p) i -> p (o k) i", p=P)
                                 ).then_inc(ld_exp[par], 16)
                    src = a["down1"]
                sp.dma_start(ED[0:m.IP, par, 0:m.dcols].rearrange("p (c d) -> p c d", d=D),
                             src[bass.ds(e, 1)].rearrange("o (c p) d -> p (o c) d", p=m.IP)
                             ).then_inc(ld_exp[par], 16)

            for m in MOES:
                for par in range(2):
                    base = EB[m.n] + par
                    load_expert(m, par, par, base - 1 if base >= 2 else None)
                with sp.Fori(1, m.E // 2) as i:
                    for par in range(2):
                        load_expert(m, i * 2 + par, par, i * 2 + (EB[m.n] + par - 1))
            for t in range(NT):
                sp.wait_ge(x_ready, 3 * NT + t + 1)
                sp.dma_start(outd[:, t, :], XA[:, t, :]).then_inc(stored, 16)
            sp.wait_ge(stored, 16 * NT)

        @block.gpsimd
        def _(pool):
            ch = Counter(pool, pool_chain)
            pool.dma_start(sel0[:], a["sel0"]).then_inc(ld_sel, 16)
            pool.dma_start(rep1[:], a["rep1"]).then_inc(ld_sel, 16)

            def split(hi, lo, src):
                ch.link(pool.tensor_scalar(hi, src, 1.0, 0.0, ALU.mult, ALU.add))
                return pool.tensor_tensor(lo, src, hi.bitcast(F32), ALU.subtract)

            ch.link(pool.memset(round_mark[:], 0.0))
            pool.wait_ge(ld_const, 16 * 14)
            pool.wait_ge(ld_wo0, 16)
            for k in range(KD):
                ch.link(pool.tensor_scalar(WO0T[:, k, :], WO0T[:, k, :], gamma[:, k:k + 1], 0.0, ALU.mult, ALU.add))
            split(WO0H[:], WO0L[:], WO0T).then_inc(w_split, 1)
            pool.wait_ge(ld_wr, 16)
            split(WRH[:], WRL[:], WRT[:]).then_inc(w_split, 1)
            pool.wait_ge(ld_w1, 16)
            split(W1H[:], W1L[:], W1T).then_inc(w_split, 1)
            pool.wait_ge(ld_wo1, 16)
            split(WO1H[:], WO1L[:], WO1T).then_inc(w_split, 1)

            def split_expert(m, par, loads, free_at, ordinal):
                pool.wait_ge(ld_exp[par], loads)
                if free_at is not None:
                    pool.wait_ge(dn_done, free_at)
                pool.tensor_tensor(round_mark[:, 0:1], round_mark[:, 1:2], round_mark[:, 2:3], ALU.add)
                gh, gl = EGH[:, par, 0:m.gcols], EGL[:, par, 0:m.gcols]
                dh, dl = EDH[0:m.IP, par, 0:m.dcols], EDL[0:m.IP, par, 0:m.dcols]
                pool.tensor_scalar(gh, EG[:, par, 0:m.gcols], 1.0, 0.0, ALU.mult, ALU.add).then_inc(pool_chain, 1)
                pool.tensor_scalar(dh, ED[0:m.IP, par, 0:m.dcols], 1.0, 0.0, ALU.mult, ALU.add).then_inc(pool_chain, 1)
                pool.wait_ge(pool_chain, ordinal * 2 + (chained + 2))
                pool.tensor_tensor(gl, EG[:, par, 0:m.gcols], gh.bitcast(F32), ALU.subtract)
                pool.tensor_tensor(dl, ED[0:m.IP, par, 0:m.dcols], dh.bitcast(F32), ALU.subtract
                                   ).then_inc(exp_split, 1)

            chained = ch.n
            per0, per1 = 16 * 3, 16 * 2
            m = MOES[0]
            for e in range(2):
                split_expert(m, e % 2, per0, None, e)
            with pool.Fori(1, m.E // 2) as i:
                for par in range(2):
                    split_expert(m, par, i * per0 + per0, i * m.body + (par + 1) * m.units - m.body, i * 2 + par)
            m = MOES[1]
            had = per0 * (E0 // 2)
            for e in range(2):
                split_expert(m, e % 2, had + per1, UB[1] - (1 - e) * MOES[0].units, E0 + e)
            pool.wait_ge(q_ready, 2)
            for v in range(DV1):
                pool.wait_ge(s_done, v + 1)
                if v >= 2:
                    pool.wait_ge(o_mm, v - 1)
                pool.tensor_tensor(QS[:, v % 2, :], STATE[:, v % 2, :], QT[:], ALU.mult).then_inc(qs_done, 1)
            with pool.Fori(1, m.E // 2) as i:
                for par in range(2):
                    split_expert(m, par, i * per1 + (had + per1),
                                 i * m.body + (UB[1] + (par + 1) * m.units - m.body), i * 2 + (E0 + par))

        @block.scalar
        def _(act):
            ch = Counter(act, act_chain)

            act.wait_ge(ld_w0, 16)
            act.activation(W0H, W0T, ACT.Copy).then_inc(w0_hi, 1)
            act.wait_ge(ld_xt, 16)
            act.activation(XH[:], XT, ACT.Copy).then_inc(xt_hi, 1)
            act.wait_ge(gate_bias, 1)
            act.wait_ge(gate_mm, 1)
            act.activation(GI[:], bank(0)[:, 0:S], ACT.Tanh, bias=gate_bs[:, 0:1], scale=1.0 / CAP).then_inc(tanh_done, 1)
            ch.link(act.activation(GF[:], bank(1)[:, 0:S], ACT.Tanh, bias=gate_bs[:, 1:2], scale=1.0 / CAP))
            ch.link(act.activation(GF[:], GF[:], ACT.Exp, scale=-CAP))
            act.activation(GF[:], GF[:], ACT.Ln, bias=1.0).then_inc(soft_done, 1)
            act.wait_ge(qk_mm, 2)
            for hf in range(2):
                act.activation(QT[:, hf * BANK:(hf + 1) * BANK], bank(2 + hf), ACT.Copy).then_inc(q_ready, 1)
            act.wait_ge(ones_set, 1)
            for t in range(NT):
                act.wait_ge(vo_mm, t + 1)
                act.activation(VX[:, t, :, 0:DV0], bank(6 + t % 2)[:, 0:D].rearrange("p (h v) -> p h v", h=NH0), ACT.Copy)
                act.activation(OGATE[:, t, :], bank(6 + t % 2)[:, D:2 * D], ACT.Sigmoid).then_inc(vo_done, 1)
            act.wait_ge(nl_ready, 1)
            act.activation(NL[:], NL[:], ACT.Exp).then_inc(floor_ready, 1)
            act.wait_ge(at_ready, 1)
            for u in range(B * NH0):
                b, h = u // NH0, u % NH0
                act.wait_ge(r_ready, u + 1)
                if u >= 2:
                    act.wait_ge(w_ready, u - 1)
                c = 32 * b + h
                act.activation(EW[:, u % 2, 0:S], bank(u % 2)[:, 0:S], ACT.Exp, bias=ATF[:, 0, 0, c:c + 1])
                act.activation(EW[:, u % 2, S:S + P], bank(u % 2)[:, S:S + P], ACT.Exp,
                               bias=ATF[:, 0, 1, c:c + 1]).then_inc(e_ready, 1)

            def head_rstd(n, nh):
                act.wait_ge(var_ready, (n + 1) * NT)
                act.activation(hr[:, :, 0:nh], hr[:, :, 0:nh], ACT.Sqrt).then_inc(rstd_ready, 1)

            def hi_parts(n, dst):
                for p in range(NT // 2):
                    act.wait_ge(tp_done, n * (NT // 2) + p + 1)
                    act.activation(dst[:, :, p * 2 * P:(p + 1) * 2 * P].rearrange("p k (t c) -> p t k c", t=2),
                                   bank(p).rearrange("p (t k c) -> p t k c", t=2, k=KD), ACT.Copy).then_inc(hi_done, 1)

            def ln_sqrt(n):
                act.wait_ge(ln_var, n + 1)
                act.activation(rstd[:], rv[:], ACT.Sqrt).then_inc(ln_rstd, 1)

            def router_exp(n, E):
                act.wait_ge(rt_max, n + 1)
                act.activation(PR[:, :, 0:E], LG[:, :, 0:E], ACT.Exp).then_inc(rt_exp, 1)

            def moe_act(m):
                IC, IP, I, tl = m.IC, m.IP, m.I, m.tiles

                def silu(pos, u):
                    s = pos % 2
                    act.wait_ge(gu_done, u + 1)
                    wait_past(act, h_ready, u - 1)
                    act.activation(SIL[:, s, 0:tl * I].rearrange("p (t i) -> p t i", t=tl),
                                   bank(s)[:, 0:tl * 2 * I].rearrange("p (t c) -> p t c", t=tl)[:, :, 0:I],
                                   ACT.Silu).then_inc(sil_done, 1)

                def hi(pos, u):
                    s = pos % 2
                    act.wait_ge(ht_done, u + 1)
                    wait_past(act, dn_done, u - 1)
                    act.activation(EHH[0:IP, s, :], bank(2 + s)[0:IP, 0:256], ACT.Copy).then_inc(hhi_done, 1)

                run_units(act, m, silu, [(hi, 1)])

            head_rstd(0, NH0)
            hi_parts(0, HTH)
            ln_sqrt(0)
            hi_parts(1, XH)
            router_exp(0, E0)
            moe_act(MOES[0])
            ln_sqrt(1)
            hi_parts(2, XH)

            act.wait_ge(g_mm, 1)
            for hf in range(2):
                act.activation(QT[:, hf * BANK:(hf + 1) * BANK], bank(hf), ACT.Copy).then_inc(q_ready, 1)
            act.wait_ge(g_mm, 2)
            for hf in range(2):
                act.activation(KT[:, hf * BANK:(hf + 1) * BANK], bank(2 + hf), ACT.Copy, scale=KSCALE).then_inc(k_ready, 1)
            act.wait_ge(g_mm, 3)
            for hf in range(2):
                act.activation(KGL[0:16, hf * BANK:(hf + 1) * BANK], bank(4 + hf)[0:16, :], ACT.Copy).then_inc(z_ready, 1)
            act.wait_ge(dec_ready, 1)
            ch.link(act.activation(KGL, KGL, ACT.Exp, scale=-1.0))
            act.activation(KGL, KGL, ACT.Ln, bias=1.0).then_inc(dec_ready, 1)
            act.wait_ge(dec_ready, 3)
            act.activation(DEC, KG, ACT.Exp, scale=1.0 / GATE_NORM).then_inc(dec_ready, 1)
            for n in range(4):
                act.wait_ge(vt_mm, n + 1)
                act.activation(VTH[:, n // 2, (n % 2) * BANK:(n % 2 + 1) * BANK], bank(n), ACT.Copy).then_inc(vt_hi, 1)
            for p in range(NT // 2):
                act.wait_ge(og_pre, p + 1)
                act.activation(OGATE[:, 2 * p:2 * p + 2, :], OGATE[:, 2 * p:2 * p + 2, :], ACT.Silu).then_inc(og_silu, 1)
            head_rstd(1, NH1)
            hi_parts(3, HTH)
            ln_sqrt(2)
            hi_parts(4, XH)
            router_exp(1, E1)
            moe_act(MOES[1])
            ln_sqrt(3)

        @block.vector
        def _(dve):
            ch = Counter(dve, dve_chain)
            dve.memset(zb[:], 0.0).then_inc(zb_set, 1)
            dve.wait_ge(ld_xt, 16)
            dve.wait_ge(ld_w0, 16)
            dve.memset(VX[:, :, :, DV0:DV0 + 1], 1.0).then_inc(ones_set, 1)
            dve.wait_ge(ld_const, 16 * 14)
            dve.tensor_scalar(gate_bs[:], gate_b[:], 1.0 / CAP, None, ALU.mult).then_inc(gate_bias, 1)
            dve.wait_ge(w0_hi, 1)
            dve.tensor_tensor(W0L, W0T, W0H.bitcast(F32), ALU.subtract).then_inc(x0_split, 1)
            dve.wait_ge(xt_hi, 1)
            dve.tensor_tensor(XL[:], XT, XH[:].bitcast(F32), ALU.subtract).then_inc(x0_split, 1)

            dve.wait_ge(soft_done, 1)
            ch.link(dve.tensor_tensor_scan(NL[:], GF[:], GF[:], 0.0, ALU.add, ALU.max))
            dve.wait_ge(tanh_done, 1)
            ch.link(dve.scalar_tensor_tensor(out=AS[:], in0=GI[:], scalar=CAP, in1=NL[:], op0=ALU.mult, op1=ALU.add))
            ch.link(dve.tensor_tensor_scan(MX[:], AS[:], AS[:], 0.0, ALU.max, ALU.max))
            dve.tensor_tensor(NL[:], NL[:], MX[:], ALU.subtract).then_inc(nl_ready, 1)
            ch.link(dve.tensor_scalar(MX[:], MX[:], -1.0, None, ALU.mult))
            ch.link(dve.tensor_copy(NMH[:], MX[:]))
            ch.link(dve.tensor_tensor(NML[:], MX[:], NMH[:].bitcast(F32), ALU.subtract))
            ch.link(dve.tensor_scalar(NML[:], NML[:], head_masks[:, 3:4], None, ALU.mult))
            dve.scalar_tensor_tensor(out=NMD[:], in0=NMH[:].bitcast(F32), scalar=head_masks[:, 2:3], in1=NML[:],
                                     op0=ALU.mult, op1=ALU.add).then_inc(nm_ready, 1)
            dve.wait_ge(qk_mm, 4)
            for hf in range(2):
                dve.tensor_scalar(KTE[:, hf * BANK:(hf + 1) * BANK], bank(4 + hf), head_masks[:, 0:1], None, ALU.mult)
                dve.tensor_scalar(KTO[:, hf * BANK:(hf + 1) * BANK], bank(4 + hf), head_masks[:, 1:2], None,
                                  ALU.mult).then_inc(k_ready, 1)
            dve.wait_ge(gt_mm, 1)
            ch.link(dve.tensor_copy(ATF[:].rearrange("p a t c -> p (a t c)"), bank(4)))
            dve.sem_inc(at_ready, 1) if False else dve.tensor_copy(den[:, 3, 0:1], head_masks[:, 0:1]).then_inc(at_ready, 1)

            def centre(view, g, nh, n_tile, count, eps, gate, out_view, sq_view):
                ch.link(dve.tensor_reduce(hs[:, n_tile, 0:nh], view, AX_X, ALU.add))
                ch.link(dve.tensor_scalar(hn[:, n_tile, 0:nh], hs[:, n_tile, 0:nh], -1.0 / count, None, ALU.mult))
                ch.link(dve.tensor_tensor(out_view, view, col(hn[:, n_tile, 0:nh], count), ALU.add))
                ch.link(dve.tensor_tensor(sq_view, out_view, out_view, ALU.mult))
                ch.link(dve.tensor_reduce(hs[:, n_tile, 0:nh], sq_view, AX_X, ALU.add))
                ch.link(dve.tensor_scalar(hs[:, n_tile, 0:nh], hs[:, n_tile, 0:nh], 1.0 / count, eps, ALU.mult, ALU.add))
                dve.reciprocal(hr[:, n_tile, 0:nh], hs[:, n_tile, 0:nh]).then_inc(var_ready, 1)
                ch.link(dve.tensor_tensor(out_view, out_view, gate, ALU.mult))

            def mlstm_heads(b):
                for tt in range(TB):
                    t = b * TB + tt
                    ao = bank(4 + 2 * (b % 2) + tt)[:, 0:NH0 * (DV0 + 1)].rearrange("p (h v) -> p h v", h=NH0)
                    qn = ao[:, :, DV0]
                    dve.wait_ge(av_done, (b + 1) * NH0)
                    ch.link(dve.scalar_tensor_tensor(out=den[:, 0, :], in0=qn, scalar=-1.0,
                                                     in1=ATF[:, 1, tt, 32 * b:32 * b + NH0], op0=ALU.mult, op1=ALU.max))
                    ch.link(dve.tensor_tensor(den[:, 1, :], qn, den[:, 0, :], ALU.max))
                    ch.link(dve.tensor_scalar(den[:, 1, :], den[:, 1, :], EPS_M, None, ALU.add))
                    ch.link(dve.reciprocal(den[:, 2, :], den[:, 1, :]))
                    hv = HC[:, t, :].rearrange("p (h v) -> p h v", h=NH0)
                    ins = dve.tensor_tensor(SQ[:, 0, :].rearrange("p (h v) -> p h v", h=NH0), ao[:, :, 0:DV0],
                                            col(den[:, 2, :], DV0), ALU.mult)
                    ch.link(ins)
                    centre(SQ[:, 0, :].rearrange("p (h v) -> p h v", h=NH0), None, NH0, t, DV0, EPS_M,
                           OGATE[:, t, :].rearrange("p (h v) -> p h v", h=NH0), hv,
                           SQ[:, 1, :].rearrange("p (h v) -> p h v", h=NH0))
                dve.tensor_copy(den[:, 3, 1:2], head_masks[:, 0:1]).then_inc(ao_read, 1)

            dve.wait_ge(vo_done, NT)
            dve.wait_ge(w_split, 4)
            for u in range(B * NH0):
                dve.wait_ge(e_ready, u + 1)
                dve.wait_ge(qk_ready, u + 1)
                if u >= 2:
                    dve.wait_ge(av_done, u - 1)
                dve.tensor_tensor(WW[:, u % 2, :], EW[:, u % 2, :], bank(2 + u % 2)[:, 0:3 * P],
                                  ALU.mult).then_inc(w_ready, 1)
                if u % NH0 == 2 and u > NH0:
                    mlstm_heads(u // NH0 - 1)
            mlstm_heads(B - 1)

            def apply_rstd(n, nh):
                dve.wait_ge(rstd_ready, n + 1)
                for t in range(NT):
                    v = HC[:, t, :].rearrange("p (h v) -> p h v", h=nh)
                    dve.tensor_tensor(v, v, col(hr[:, t, 0:nh], D // nh), ALU.mult).then_inc(gated, 1)

            def lo_parts(n, dst, hi):
                for p in range(NT // 2):
                    dve.wait_ge(hi_done, n * (NT // 2) + p + 1)
                    ap = lambda x: x[:, :, p * 2 * P:(p + 1) * 2 * P].rearrange("p k (t c) -> p t k c", t=2)
                    for t in range(2):
                        ins = dve.tensor_tensor(ap(dst)[:, t], bank(p).rearrange("p (t k c) -> p t k c", t=2, k=KD)[:, t],
                                                ap(hi).bitcast(F32)[:, t], ALU.subtract)
                    ins.then_inc(lo_done, 1)

            def layernorm(n, res, dst):
                for t in range(NT):
                    dve.wait_ge(y_done, n * NT + 2 * (t // 2) + 2)
                    y = bank(4 + t // 2)[:, (t % 2) * D:(t % 2 + 1) * D]
                    ins = dve.tensor_tensor(dst[:, t, :], y, res[:, t, :], ALU.add)
                    ch.link(ins)
                    ch.link(dve.bn_stats(st[:, t, :], dst[:, t, :]))
                    ch.link(dve.bn_aggr(mv[:, t, :], st[:, t, :]))
                ch.link(dve.tensor_scalar(rv[:], mv[:, :, 1], EPS_LN, None, ALU.add))
                dve.reciprocal(rv[:], rv[:]).then_inc(ln_var, 1)
                dve.wait_ge(ln_rstd, n + 1)
                for t in range(NT):
                    dve.tensor_scalar(dst[:, t, :], dst[:, t, :], mv[:, t, 0:1], rstd[:, t:t + 1],
                                      ALU.subtract, ALU.mult).then_inc(x_ready, 1)

            def softmax(n, E, bias):
                lg, pr = LG[:, :, 0:E], PR[:, :, 0:E]
                dve.wait_ge(rt_mm, n + 1)
                src = bank(3)[:, 0:NT * E].rearrange("p (t e) -> p t e", t=NT)
                if bias is None:
                    ins = dve.tensor_copy(lg, src)
                else:
                    ins = dve.tensor_tensor(lg, src, bias.unsqueeze(1).broadcast_to([P, NT, E]), ALU.add)
                ins.then_inc(rt_read, 1)
                dve.wait_ge(rt_read, n + 1)
                ch.link(dve.tensor_reduce(rsum[:], lg, AX_X, ALU.max))
                dve.tensor_tensor(lg, lg, col(rsum[:], E), ALU.subtract).then_inc(rt_max, 1)
                dve.wait_ge(rt_exp, n + 1)
                ch.link(dve.tensor_reduce(rsum[:], pr, AX_X, ALU.add))
                ch.link(dve.reciprocal(rsum[:], rsum[:]))
                ch.link(dve.tensor_tensor(pr, pr, col(rsum[:], E), ALU.mult))
                for t in range(NT):
                    ins = dve.max(top[:, t, :], PR[:, t, 0:E])
                ch.link(ins)
                for t in range(NT):
                    ins = dve.max_index(tix[:, t, :], top[:, t, :], PR[:, t, 0:E])
                ch.link(ins)
                ch.link(dve.tensor_copy(tif[:], tix[:]))

            def normalise(dst, src, k, floor):
                ch.link(dve.tensor_reduce(rsum[:], src[:, :, 0:k], AX_X, ALU.add))
                if floor is not None:
                    ch.link(dve.tensor_scalar(rsum[:], rsum[:], floor, None, ALU.max))
                ch.link(dve.reciprocal(rsum[:], rsum[:]))
                ch.link(dve.tensor_tensor(dst[:, :, 0:k], src[:, :, 0:k], col(rsum[:], k), ALU.mult))

            def combine(E, k, w):
                io = iota_e[:, 0:E].unsqueeze(1).broadcast_to([P, NT, E])
                eq, cw = EQ[:, :, 0:E], CW[:, :, 0:E]
                for j in range(k):
                    dst = cw if j == 0 else eq
                    ch.link(dve.tensor_tensor(eq, io, col(tif[:, :, j], E), ALU.is_equal))
                    ch.link(dve.tensor_tensor(dst, eq, col(w[:, :, j], E), ALU.mult))
                    if j:
                        ins = dve.tensor_tensor(cw, cw, eq, ALU.add)
                        if j < k - 1:
                            ch.link(ins)
                ins.then_inc(cw_ready, 1)
                dve.wait_ge(cw_ready, 1 if E == E0 else 2)

            def route1():
                normalise(t1, top, 8, 1e-12)
                ch.link(dve.tensor_scalar(t2[:], t1[:], alpha[:, 0:1], None, ALU.mult))
                ch.link(dve.tensor_reduce(rsum[:], t2[:], AX_X, ALU.max))
                ch.link(dve.tensor_tensor(t3[:], t2[:], col(rsum[:], 8), ALU.is_equal))
                f8 = first8[:].unsqueeze(1).broadcast_to([P, NT, 8])
                ch.link(dve.tensor_tensor(t3[:], t3[:], f8, ALU.mult))
                ch.link(dve.tensor_reduce(rsum[:], t3[:], AX_X, ALU.max))
                ch.link(dve.tensor_tensor(t3[:], f8, col(rsum[:], 8), ALU.is_equal))
                ch.link(dve.tensor_scalar(t2[:], t2[:], TAU, None, ALU.is_ge))
                ch.link(dve.tensor_reduce(rsum[:], t2[:], AX_X, ALU.max))
                ch.link(dve.tensor_scalar(rsum[:], rsum[:], -1.0, 1.0, ALU.mult, ALU.add))
                ch.link(dve.tensor_tensor(t3[:], t3[:], col(rsum[:], 8), ALU.mult))
                ch.link(dve.tensor_tensor(t2[:], t2[:], t3[:], ALU.max))
                ch.link(dve.tensor_tensor(t1[:], t1[:], t2[:], ALU.mult))
                normalise(t2, t1, 8, 1e-12)

            def moe_dve(m):
                I, IP, tl = m.I, m.IP, m.tiles

                def gate_up(pos, u):
                    s = pos % 2
                    dve.wait_ge(sil_done, u + 1)
                    wait_past(dve, ht_done, u - 1)
                    e = pos // m.units + ((u - (UB[m.n] + pos)) // m.units if not isinstance(u, int)
                                          else (u - UB[m.n] - pos) // m.units)
                    for j in range(tl):
                        t = (pos % m.units) * tl + j
                        if isinstance(e, int):
                            c = CW[:, t, e:e + 1]
                        else:
                            c = CW[:, t, bass.ds(e, 1)]
                        ins = dve.scalar_tensor_tensor(
                            out=HH[:, s, j * I:(j + 1) * I], in0=SIL[:, s, j * I:(j + 1) * I], scalar=c,
                            in1=bank(s)[:, j * 2 * I + I:(j + 1) * 2 * I], op0=ALU.mult, op1=ALU.mult)
                    ins.then_inc(h_ready, 1)

                def lo(pos, u):
                    s = pos % 2
                    dve.wait_ge(hhi_done, u + 1)
                    dve.tensor_tensor(EHL[0:IP, s, :], bank(2 + s)[0:IP, 0:256], EHH[0:IP, s, :].bitcast(F32),
                                      ALU.subtract).then_inc(hlo_done, 1)

                run_units(dve, m, gate_up, [(lo, 1)])

            apply_rstd(0, NH0)
            lo_parts(0, HTL, HTH)
            dve.wait_ge(ld_x, 16)
            dve.wait_ge(w_split, 3)
            layernorm(0, XA, XB)
            lo_parts(1, XL, XH)
            softmax(0, E0, bias_r0[:])
            normalise(t2, top, 4, None)
            combine(E0, 4, t2)
            moe_dve(MOES[0])
            layernorm(1, XB, XA)
            lo_parts(2, XL, XH)

            for hf in range(2):
                dve.wait_ge(g_mm, 4 + hf)
                dve.tensor_scalar(KG[:, hf * BANK:(hf + 1) * BANK], bank(6 + hf), bkg[:, 0:1], None,
                                  ALU.add).then_inc(g_read, 1)
            dve.wait_ge(g_read, 2)
            dve.scalar_tensor_tensor(out=KGL, in0=KG, scalar=-1.0, in1=KG, op0=ALU.mult, op1=ALU.max
                                     ).then_inc(dec_ready, 1)
            dve.wait_ge(dec_ready, 2)
            dve.scalar_tensor_tensor(out=KG, in0=KG, scalar=0.0, in1=KGL, op0=ALU.min, op1=ALU.subtract
                                     ).then_inc(dec_ready, 1)
            for n in range(4):
                dve.wait_ge(vt_hi, n + 1)
                dve.tensor_tensor(VTL[:, n // 2, (n % 2) * BANK:(n % 2 + 1) * BANK], bank(n),
                                  VTH[:, n // 2, (n % 2) * BANK:(n % 2 + 1) * BANK].bitcast(F32),
                                  ALU.subtract).then_inc(vt_lo, 1)
            for p in range(NT // 2):
                dve.wait_ge(og_mm, p + 1)
                dve.tensor_tensor(OGATE[:, 2 * p:2 * p + 2, :], bank(4 + p).rearrange("p (t d) -> p t d", t=2),
                                  bg[:].unsqueeze(1).broadcast_to([P, 2, D]), ALU.add).then_inc(og_pre, 1)
            dve.wait_ge(dec_ready, 4)
            ch.link(dve.memset(DEC.rearrange("p (b s) -> p b s", b=B)[:, :, 0:1], 0.0))
            dve.wait_ge(k_ready, 4)
            for v in range(DV1):
                s = v % 2
                dve.wait_ge(vr_mm, v + 1)
                dve.tensor_tensor(DATA1[:, s, :], KT,
                                  PS[:, 2 * s:2 * s + 2, :].rearrange("p k c -> p (k c)"), ALU.mult).then_inc(d1_done, 1)
                dve.wait_ge(d1_done, v + 1)
                if v >= 2:
                    dve.wait_ge(qs_done, v - 1)
                dve.tensor_tensor_scan(STATE[:, s, :], DEC, DATA1[:, s, :], 0.0, ALU.mult, ALU.add).then_inc(s_done, 1)
            dve.wait_ge(o_mm, DV1)
            dve.wait_ge(og_silu, NT // 2)
            for t in range(NT):
                o = bank(4 + t // 2)[:, (t % 2) * D:(t % 2 + 1) * D].rearrange("p (v h) -> p h v", h=NH1)
                centre(o, None, NH1, t, DV1, EPS_G, OGATE[:, t, :].rearrange("p (h v) -> p h v", h=NH1),
                       HC[:, t, :].rearrange("p (h v) -> p h v", h=NH1),
                       SQ[:, 1, :].rearrange("p (h v) -> p h v", h=NH1))
            apply_rstd(1, NH1)
            lo_parts(3, HTL, HTH)
            layernorm(2, XA, XB)
            lo_parts(4, XL, XH)
            softmax(1, E1, None)
            route1()
            combine(E1, 8, t2)
            moe_dve(MOES[1])
            layernorm(3, XB, XA)

        @block.tensor
        def _(pe):
            def mm3(o, lhs, rhs, start, stop):
                n = 3 * len(lhs)
                i = 0
                for (lh, ll), (rh, rl) in zip(lhs, rhs):
                    for l, r in ((lh, rh), (lh, rl), (ll, rh)):
                        ins = pe.matmul(o, l, r, start=start and i == 0, stop=stop and i == n - 1,
                                        skip_group_check=True)
                        i += 1
                return ins

            def xs(t):
                return [(XH[:, k, t * P:(t + 1) * P], XL[:, k, t * P:(t + 1) * P]) for k in range(KD)]

            def xm(hf):
                return [(XH[:, k, hf * BANK:(hf + 1) * BANK], XL[:, k, hf * BANK:(hf + 1) * BANK]) for k in range(KD)]

            def ws(wh, wl, c, n):
                return [(wh[:, k, c:c + n], wl[:, k, c:c + n]) for k in range(KD)]

            pe.wait_ge(ld_xt, 16)
            pe.wait_ge(ld_w0, 16)
            for g, c in ((0, IG0), (1, FG0)):
                for b in range(B):
                    for k in range(KD):
                        ins = pe.matmul(bank(g)[32 * b:32 * b + 32, 0:S], W0T[:, k, c:c + 32],
                                        XT[:, k, b * S:(b + 1) * S], start=(k == 0), stop=(k == KD - 1))
            ins.then_inc(gate_mm, 1)
            pe.wait_ge(x0_split, 2)
            for g, c in ((2, Q0), (4, K0)):
                for hf in range(2):
                    mm3(bank(g + hf), ws(W0H, W0L, c, P), xm(hf), True, True).then_inc(qk_mm, 1)
            for t in range(NT):
                if t >= 2:
                    pe.wait_ge(vo_done, t - 1)
                mm3(bank(6 + t % 2), xs(t), ws(W0H, W0L, 0, 2 * D), True, True).then_inc(vo_mm, 1)
            pe.wait_ge(ld_const, 16 * 14)
            pe.wait_ge(k_ready, 2)
            pe.wait_ge(nm_ready, 1)
            pe.wait_ge(floor_ready, 1)
            for i, src in enumerate((AS, NL)):
                for tt in range(TB):
                    ins = pe.transpose(bank(4)[:, (2 * i + tt) * P:(2 * i + tt + 1) * P],
                                       src[:, tt * P:(tt + 1) * P], ident[:])
            ins.then_inc(gt_mm, 1)

            def scores(u):
                b, h = u // NH0, u % NH0
                r, q = bank(u % 2), bank(2 + u % 2)
                if u >= 2:
                    pe.wait_ge(e_ready, u - 1)
                sel = sel0[:, u:u + 1].broadcast_to([P, P])
                pe.matmul(r[:, 0:S], sel, NMD[:], start=True, stop=False, skip_group_check=True)
                pe.matmul(r[:, S:S + P], sel, NMD[:, P:S], start=False, stop=False, skip_group_check=True)
                pe.matmul(r[:, 0:P], identb[:], futb[:], start=False, stop=False, skip_group_check=True)
                pe.matmul(r[:, S:S + P], identb[:], futb[:], start=False, stop=True, skip_group_check=True
                          ).then_inc(r_ready, 1)
                if u >= 2:
                    pe.wait_ge(w_ready, u - 1)
                rows = slice(32 * (h // 2), 32 * (h // 2) + 32)
                kt = KTE if h % 2 == 0 else KTO
                pe.matmul(q[:, 0:S], kt[rows, b * S:b * S + P], QT[rows, b * S:(b + 1) * S],
                          start=True, stop=False, skip_group_check=True)
                pe.matmul(q[:, S:S + P], kt[rows, b * S + P:b * S + 2 * P], QT[rows, b * S + P:b * S + 2 * P],
                          start=False, stop=True, skip_group_check=True).then_inc(qk_ready, 1)

            def values(u):
                b, h = u // NH0, u % NH0
                if h == 0:
                    if b == 0:
                        pe.wait_ge(at_ready, 1)
                    if b >= 2:
                        pe.wait_ge(ao_read, b - 1)
                pe.wait_ge(w_ready, u + 1)
                c = slice(h * (DV0 + 1), (h + 1) * (DV0 + 1))
                w = WW[:, u % 2, :]
                v0, v1 = VX[:, TB * b, h, :], VX[:, TB * b + 1, h, :]
                o0, o1 = bank(4 + 2 * (b % 2))[:, c], bank(5 + 2 * (b % 2))[:, c]
                pe.matmul(o0, w[:, 0:P], v0, start=(h == 0), stop=True, skip_group_check=True)
                pe.matmul(o1, w[:, P:2 * P], v0, start=(h == 0), stop=False, skip_group_check=True)
                pe.matmul(o1, w[:, 2 * P:3 * P], v1, start=False, stop=True, skip_group_check=True
                          ).then_inc(av_done, 1)

            pe.wait_ge(ld_sel, 32)
            pe.wait_ge(q_ready, 2)
            pe.wait_ge(tanh_done, 1)
            pe.wait_ge(vo_done, NT)
            for u in range(B * NH0 + 1):
                if u < B * NH0:
                    scores(u)
                if u >= 1:
                    values(u - 1)

            def transposes(n, src, ready, base):
                for p in range(NT // 2):
                    pe.wait_ge(ready, base + 2 * (p + 1))
                    for t in range(2):
                        for k in range(KD):
                            ins = pe.transpose(bank(p)[:, (2 * t + k) * P:(2 * t + k + 1) * P],
                                               src[:, 2 * p + t, k * P:(k + 1) * P], ident[:])
                    ins.then_inc(tp_done, 1)

            def project(n, wh, wl):
                for t in range(NT):
                    if t % 2 == 0:
                        pe.wait_ge(lo_done, n * (NT // 2) + t // 2 + 1)
                    lhs = [(HTH[:, k, t * P:(t + 1) * P], HTL[:, k, t * P:(t + 1) * P]) for k in range(KD)]
                    mm3(bank(4 + t // 2)[:, (t % 2) * D:(t % 2 + 1) * D], lhs, ws(wh, wl, 0, D),
                        t % 2 == 0, True).then_inc(y_done, 1)

            def router(n, tp, c, E):
                pe.wait_ge(lo_done, (tp + 1) * (NT // 2))
                for t in range(NT):
                    for i in range(4 * KD):
                        k, part = i // 4, i % 4
                        l = (XH, XL)[part // 2][:, k, t * P:(t + 1) * P]
                        r = (WRH, WRL)[part % 2][:, k, c:c + E]
                        ins = pe.matmul(bank(3)[:, t * E:(t + 1) * E], l, r, start=(t == 0 and i == 0),
                                        stop=(i == 4 * KD - 1), skip_group_check=True)
                ins.then_inc(rt_mm, 1)

            def moe_pe(m):
                I, IP, IC, tl = m.I, m.IP, m.IC, m.tiles
                base = UB[m.n]
                for n in range(4):
                    pe.matmul(bank(4 + n), zb[:, 0:P], zb[:], start=True, stop=True, skip_group_check=True)
                pe.wait_ge(rt_read, m.n + 1)

                def gate_up(pos, u):
                    s, par = pos % 2, pos // m.units
                    if pos % m.units == 0:
                        first = (u - (base + pos)) // m.units if not isinstance(u, int) else 0
                        pe.wait_ge(exp_split, first + (EB[m.n] + par + 1))
                    wait_past(pe, h_ready, u - 1)
                    w = [EG_.rearrange("p (k c) -> p k c", k=KD) for EG_ in (EGH[:, par, 0:m.gcols], EGL[:, par, 0:m.gcols])]
                    for j in range(tl):
                        t = (pos % m.units) * tl + j
                        ins = mm3(bank(s)[:, j * 2 * I:(j + 1) * 2 * I], xs(t), [(w[0][:, k, :], w[1][:, k, :]) for k in range(KD)],
                                  j == 0, j == tl - 1)
                    ins.then_inc(gu_done, 1)

                def turn(pos, u):
                    s = pos % 2
                    pe.wait_ge(h_ready, u + 1)
                    wait_past(pe, hlo_done, u - 1)
                    for j in range(2):
                        ins = pe.transpose(bank(2 + s)[0:IP, j * P:(j + 1) * P], HH[:, s, j * IP:(j + 1) * IP], ident[:])
                    ins.then_inc(ht_done, 1)

                def down(pos, u):
                    s, par = pos % 2, pos // m.units
                    pe.wait_ge(hlo_done, u + 1)
                    for j in range(tl):
                        t = (pos % m.units) * tl + j
                        y = bank(4 + t // 2)[:, (t % 2) * D:(t % 2 + 1) * D]
                        ks = [(c if IC == 2 else j) for c in range(IC)]
                        lhs = [(EHH[0:IP, s, q * P:(q + 1) * P], EHL[0:IP, s, q * P:(q + 1) * P]) for q in ks]
                        rhs = [(EDH[0:IP, par, c * D:(c + 1) * D], EDL[0:IP, par, c * D:(c + 1) * D]) for c in range(IC)]
                        ins = mm3(y, lhs, rhs, False, True)
                    ins.then_inc(dn_done, 1)

                run_units(pe, m, gate_up, [(turn, 1), (down, 2)])
                pe.wait_ge(dn_done, base + m.total)

            def release_y(n):
                for t in range(NT):
                    pe.matmul(bank(0)[:, 0:2], zb[:, 0:P], zb[:, 0:2], start=True, stop=True,
                              skip_group_check=True).then_inc(y_done, 1)

            transposes(0, HC, gated, 0)
            pe.wait_ge(w_split, 1)
            project(0, WO0H, WO0L)
            transposes(1, XB, x_ready, 0)
            pe.wait_ge(w_split, 2)
            router(0, 1, 0, E0)
            pe.wait_ge(zb_set, 1)
            moe_pe(MOES[0])
            release_y(1)
            transposes(2, XA, x_ready, NT)

            pe.wait_ge(lo_done, 3 * (NT // 2))
            pe.wait_ge(w_split, 4)
            for g, c in ((0, Q1), (2, K1), (4, Z1)):
                for hf in range(2):
                    ins = mm3(bank(g + hf), ws(W1H, W1L, c, P), xm(hf), True, True)
                ins.then_inc(g_mm, 1)
            for hf in range(2):
                pe.wait_ge(z_ready, hf + 1)
                pe.matmul(bank(6 + hf), wkg2[:], KGL[0:16, hf * BANK:(hf + 1) * BANK], start=True, stop=True
                          ).then_inc(g_mm, 1)
            pe.wait_ge(q_ready, 4)
            pe.wait_ge(k_ready, 4)
            for n in range(4):
                mm3(bank(n), ws(W1H, W1L, V1 + (n // 2) * P, P), xm(n % 2), True, True).then_inc(vt_mm, 1)
            pe.wait_ge(g_read, 2)
            for t in range(NT):
                ins = mm3(bank(4 + t // 2)[:, (t % 2) * D:(t % 2 + 1) * D], xs(t), ws(W1H, W1L, G1, D), t % 2 == 0, True)
                if t % 2:
                    ins.then_inc(og_mm, 1)

            def spread(v):
                s = v % 2
                if v >= 2:
                    pe.wait_ge(d1_done, v - 1)
                for hf in range(2):
                    for i, part in enumerate((VTH, VTL)):
                        ins = pe.matmul(bank(2 * s + hf), rep1[:, v % 8, :], part[:, v // 8, hf * BANK:(hf + 1) * BANK],
                                        start=(i == 0), stop=(i == 1))
                ins.then_inc(vr_mm, 1)

            def gather_o(v):
                pe.wait_ge(qs_done, v + 1)
                for t in range(NT):
                    c = (t % 2) * D + v * NH1
                    ins = pe.matmul(bank(4 + t // 2)[:, c:c + NH1], QS[:, v % 2, t * P:(t + 1) * P], block1[:],
                                    start=(v == 0 and t % 2 == 0), stop=True, skip_group_check=True)
                ins.then_inc(o_mm, 1)

            pe.wait_ge(vt_lo, 4)
            spread(0)
            spread(1)
            pe.wait_ge(og_pre, NT // 2)
            for v in range(DV1):
                if v + 2 < DV1:
                    spread(v + 2)
                gather_o(v)
            transposes(3, HC, gated, NT)
            project(3, WO1H, WO1L)
            transposes(4, XB, x_ready, 2 * NT)
            router(1, 4, E0, E1)
            moe_pe(MOES[1])
            release_y(3)


def kernel(**inputs):
    import numpy as np
    import concourse.bacc as bacc
    from concourse.bass_utils import run_bass_kernel_spmd

    g = {k: np.asarray(v) for k, v in inputs.items()}
    B, S, D = g["L0_attn_x"].shape
    P = 128
    NH0, NH1 = 8, 16
    DV1, DK1 = D // NH1, P // NH1
    f32 = np.float32
    eye = np.eye(P, dtype=f32)
    rows = np.arange(P)

    odd = (rows // (P // NH0)) % 2
    rep = (rows % 32) // NH0
    sc = f32((P // NH0) ** -0.5)
    head_masks = np.stack([(odd == 0) * sc, (odd == 1) * sc, rep == 0, rep == 1], 1).astype(f32)
    sel0 = np.zeros((P, B * NH0), f32)
    for b in range(B):
        for h in range(NH0):
            sel0[32 * b + h, b * NH0 + h] = 1
            sel0[32 * b + NH0 + h, b * NH0 + h] = 1
    rep1 = np.zeros((P, 8, P), f32)
    for v in range(8):
        for h in range(NH1):
            rep1[v * NH1 + h, v, h * DK1:(h + 1) * DK1] = 1
    import ml_dtypes
    bf = ml_dtypes.bfloat16
    futb = np.where(rows[:, None] > rows[None, :], -1e30, 0.0).astype(bf)

    def rowsof(v):
        return np.ascontiguousarray(np.broadcast_to(v, (P,) + v.shape))
    wv1 = g["L1_attn_Wv"].reshape(NH1, DV1, D).transpose(1, 0, 2).reshape(D, D)
    arrays = {
        "x": g["L0_attn_x"],
        "xT": g["L0_attn_x"].reshape(B * S, D).T,
        "w0T": np.concatenate([g["L0_attn_Wv"], g["L0_attn_Wog"], g["L0_attn_Wq"], g["L0_attn_Wk"],
                               np.tile(g["L0_attn_Wig"], (4, 1)), np.tile(g["L0_attn_Wfg"], (4, 1))]).T,
        "wo0T": g["L0_attn_Wout"].T,
        "w1T": np.concatenate([wv1, g["L1_attn_Wg"], g["L1_attn_Wq"], g["L1_attn_Wk"],
                               np.tile(g["L1_attn_Wkg1"], (8, 1))]).T,
        "wo1T": g["L1_attn_Wo"].T,
        "wrT": np.concatenate([g["L0_ffn_router_w"], g["L1_ffn_gate_weight"]]).T,
        "gate_b": np.stack([np.tile(g["L0_attn_big"], P // NH0), np.tile(g["L0_attn_bfg"], P // NH0)], 1),
        "gamma": g["L0_attn_gamma"].reshape(D // P, P).T,
        "bias_r0": rowsof(g["L0_ffn_expert_bias"]),
        "alpha": rowsof(g["L1_ffn_layer_alpha"].reshape(1)),
        "bkg": g["L1_attn_bkg2"].reshape(P, 1),
        "bg": rowsof(g["L1_attn_bg"]),
        "wkg2T": g["L1_attn_Wkg2"].T,
        "gate0": g["L0_ffn_gate_proj"],
        "up0": g["L0_ffn_up_proj"],
        "down0": g["L0_ffn_down_proj"],
        "gateup1": g["L1_ffn_gate_up_proj"].transpose(0, 2, 1),
        "down1": g["L1_ffn_down_proj"].transpose(0, 2, 1),
        "ident": eye,
        "identb": eye.astype(bf),
        "futb": futb,
        "head_masks": head_masks,
        "sel0": sel0,
        "rep1": rep1,
        "iota_e": rowsof(np.arange(32, dtype=f32)),
        "first8": rowsof(np.arange(8, 0, -1).astype(f32)),
        "block1": (rows[:, None] // DK1 == np.arange(NH1)[None, :]).astype(f32),
    }
    nc = bacc.Bacc("TRN2", target_bir_lowering=False, num_devices=1)
    feeds, aps = {}, {}
    for name, v in arrays.items():
        v = np.ascontiguousarray(v)
        feeds[f"in_{name}"] = v
        aps[name] = nc.dram_tensor(f"in_{name}", v.shape, mybir.dt.from_np(v.dtype), kind="ExternalInput").ap()
    out = nc.dram_tensor("out_y", (B, S, D), F32, kind="ExternalOutput").ap()
    build_kernel(nc, aps, out)
    r = run_bass_kernel_spmd(nc, [feeds], core_ids=[0])
    return r.results[0]["out_y"]
```

```python
import itertools
from contextlib import ExitStack

import concourse.bass as bass
from concourse import mybir

ALU = mybir.AluOpType
ACT = mybir.ActivationFunctionType
F32 = mybir.dt.float32
F32R = mybir.dt.float32r
BF16 = mybir.dt.bfloat16
U32 = mybir.dt.uint32
AX_X = mybir.AxisListType.X

P = 128
BANK = 512


def build_kernel(nc, a, out):
    B, S, D = a["x"].shape
    T = B * S
    NT = T // P
    KD = D // P
    TB = S // P
    NH0 = 8
    DV0 = D // NH0
    DQ0 = P // NH0
    CAP = 15.0
    EPS_M = 1e-6
    NH1 = 16
    DV1 = D // NH1
    DK1 = P // NH1
    GATE_NORM = 16.0
    KSCALE = 128.0 ** -0.5
    EPS_G = 1e-5
    EPS_LN = 1e-5
    TAU = 0.05
    E0, I0 = a["gateup0"].shape[0], a["gateup0"].shape[2] // 2
    PAIR = 2
    E1, I1 = a["gateup1"].shape[0] * PAIR, a["gateup1"].shape[2] // 2 // PAIR

    V0, O0, Q0, K0, IG0, FG0 = 0, D, 2 * D, 2 * D + P, 2 * D + 2 * P, 2 * D + 2 * P + 32
    W0C = FG0 + 32
    V1, G1, Q1, K1, Z1 = 0, D, 2 * D, 2 * D + P, 2 * D + 2 * P
    W1C = Z1 + P

    with ExitStack() as ctx:
        def sb(name, shape, dt=F32):
            return ctx.enter_context(nc.sbuf_tensor(name, shape, dt))

        def sem(name):
            return ctx.enter_context(nc.semaphore(name))

        PS = ctx.enter_context(nc.psum_tensor("PS", [P, 8, BANK], F32))

        def bank(n):
            return PS[:, n, :]

        ident = sb("ident", [P, P])
        identb = sb("identb", [P, P], BF16)
        futb = sb("futb", [P, P], BF16)
        zb = sb("zb", [P, BANK], BF16)
        head_masks = sb("head_masks", [P, 4])
        gate_b = sb("gate_b", [P, 2])
        gate_bs = sb("gate_bs", [P, 2])
        gamma = sb("gamma", [P, KD])
        bias_r0 = sb("bias_r0", [P, E0])
        alpha = sb("alpha", [P, 1])
        bkg = sb("bkg", [P, 1])
        bg = sb("bg", [P, D])
        wkg2 = sb("wkg2", [16, P])
        iota_e = sb("iota_e", [P, E1])
        first8 = sb("first8", [P, 8])
        block2 = sb("block2", [P, 2, 2 * NH1])
        sel0 = sb("sel0", [P, B * NH0], F32R)
        rep1 = sb("rep1", [P, 8, P], F32R)

        XA = sb("XA", [P, NT, D])
        XB = sb("XB", [P, NT, D])
        XH = sb("XH", [P, KD, T], F32R)
        XL = sb("XL", [P, KD, T], F32R)
        HTH, HTL = XH, XL
        OGATE = sb("OGATE", [P, NT, D])
        HC = sb("HC", [P, NT, D])
        QT = sb("QT", [P, T])

        FA_WORDS = KD * T + KD * W0C + NT * NH0 * (DV0 + 1) + 2 * T + KD * D
        FA = sb("FA", [P, FA_WORDS])
        at = 0

        def take(n):
            nonlocal at
            at += n
            return FA[:, at - n:at]
        XT = take(KD * T).rearrange("p (k t) -> p k t", k=KD)
        W0T = take(KD * W0C).rearrange("p (k n) -> p k n", k=KD)
        VX = take(NT * NH0 * (DV0 + 1)).rearrange("p (t h v) -> p t h v", t=NT, h=NH0)
        KTE = take(T)
        KTO = take(T)
        WO0T = take(KD * D).rearrange("p (k n) -> p k n", k=KD)
        at = 0
        DEC = take(T)
        KT = take(T)
        STATE = take(2 * T).rearrange("p (s t) -> p s t", s=2)
        QS = take(2 * T).rearrange("p (s t) -> p s t", s=2)
        OT = take(KD * T).rearrange("p (k t) -> p k t", k=KD)
        KG, KGL = OT[:, 0, :], OT[:, 1, :]
        RA = sb("RA", [P, max(2 * KD * W0C, 2 * KD * T)], F32R)
        W0H = RA[:, 0:KD * W0C].rearrange("p (k n) -> p k n", k=KD)
        W0L = RA[:, KD * W0C:2 * KD * W0C].rearrange("p (k n) -> p k n", k=KD)
        VTH = RA[:, 0:KD * T].rearrange("p (k t) -> p k t", k=KD)
        VTL = RA[:, KD * T:2 * KD * T].rearrange("p (k t) -> p k t", k=KD)
        WO0H = sb("WO0H", [P, KD, D], F32R)
        WO0L = sb("WO0L", [P, KD, D], F32R)
        W1T = XB[:, :, :].rearrange("p t d -> p (t d)")[:, 0:KD * W1C].rearrange("p (k n) -> p k n", k=KD)
        W1H = sb("W1H", [P, KD, W1C], F32R)
        W1L = sb("W1L", [P, KD, W1C], F32R)
        WO1T = HC[:, 0:KD, :]
        WO1H = sb("WO1H", [P, KD, D], F32R)
        WO1L = sb("WO1L", [P, KD, D], F32R)
        WRT = sb("WRT", [P, KD, E0 + E1])
        WRH = sb("WRH", [P, KD, E0 + E1], F32R)
        WRL = sb("WRL", [P, KD, E0 + E1], F32R)

        GI = sb("GI", [P, S])
        GF = sb("GF", [P, S])
        NL = sb("NL", [P, S])
        AS = sb("AS", [P, S])
        MX = sb("MX", [P, S])
        NMH = sb("NMH", [P, S], F32R)
        NML = sb("NML", [P, S])
        NMD = sb("NMD", [P, S], F32R)
        ATF = sb("ATF", [P, 2, TB, P])
        EW = sb("EW", [P, 2, 3 * P])
        WW = sb("WW", [P, 2, 3 * P])

        st = sb("st", [P, NT, 6])
        mv = sb("mv", [P, NT, 2])
        rstd = sb("rstd", [P, NT])
        rv = sb("rv", [P, NT])
        hn = sb("hn", [P, NT, 16])
        hr = sb("hr", [P, NT, 16])
        hs = sb("hs", [P, NT, 16])
        SQ = sb("SQ", [P, 4, D])
        act_scratch = sb("act_scratch", [P, 16])
        den = sb("den", [P, 3, NH0])
        LG = sb("LG", [P, NT, E1])
        PR = sb("PR", [P, NT, E1])
        EQ = sb("EQ", [P, NT, E1])
        rsum = sb("rsum", [P, NT])
        top = sb("top", [P, NT, 8])
        tix = sb("tix", [P, NT, 8], U32)
        tif = sb("tif", [P, NT, 8])
        t1 = sb("t1", [P, NT, 8])
        t2 = sb("t2", [P, NT, 8])
        t3 = sb("t3", [P, NT, 8])
        CW = sb("CW", [P, NT, E1])

        MG = KD * 2 * I0
        MD = 2 * D
        EG = sb("EG", [P, 2, MG])
        ED = sb("ED", [P, 2, MD])
        EGH = sb("EGH", [P, 2, MG], F32R)
        EGL = sb("EGL", [P, 2, MG], F32R)
        EDH = sb("EDH", [P, 2, MD], F32R)
        EDL = sb("EDL", [P, 2, MD], F32R)
        round_mark = sb("round_mark", [P, 3])
        SIL = sb("SIL", [P, 2, 256])
        HH = sb("HH", [P, 2, 256])
        EHH = sb("EHH", [P, 2, 256], F32R)
        EHL = sb("EHL", [P, 2, 256], F32R)

        ld_const = sem("ld_const")
        ld_sel = sem("ld_sel")
        ld_x = sem("ld_x")
        ld_xt = sem("ld_xt")
        ld_w0 = sem("ld_w0")
        ld_wo0 = sem("ld_wo0")
        ld_w1 = sem("ld_w1")
        ld_wo1 = sem("ld_wo1")
        ld_wr = sem("ld_wr")
        ld_exp = [sem("ld_exp0"), sem("ld_exp1")]
        stored = sem("stored")
        zb_set = sem("zb_set")
        ones_set = sem("ones_set")
        xt_hi = sem("xt_hi")
        w0_hi = sem("w0_hi")
        x0_split = sem("x0_split")
        pool_chain = sem("pool_chain")
        v_centred = sem("v_centred")
        hc_ready = sem("hc_ready")
        sq_done = sem("sq_done")
        sq_read = sem("sq_read")
        og_ready = sem("og_ready")
        ot_evac = sem("ot_evac")
        w_split = sem("w_split")
        gate_mm = sem("gate_mm")
        gate_bias = sem("gate_bias")
        qk_mm = sem("qk_mm")
        tanh_done = sem("tanh_done")
        soft_done = sem("soft_done")
        act_chain = sem("act_chain")
        dve_chain = sem("dve_chain")
        nl_ready = sem("nl_ready")
        floor_ready = sem("floor_ready")
        a_ready = sem("a_ready")
        nm_ready = sem("nm_ready")
        gt_mm = sem("gt_mm")
        at_ready = sem("at_ready")
        q_ready = sem("q_ready")
        k_ready = sem("k_ready")
        vo_mm = sem("vo_mm")
        vo_done = sem("vo_done")
        r_ready = sem("r_ready")
        qk_ready = sem("qk_ready")
        e_ready = sem("e_ready")
        w_ready = sem("w_ready")
        av_done = sem("av_done")
        var_ready = sem("var_ready")
        rstd_ready = sem("rstd_ready")
        gated = sem("gated")
        tp_done = sem("tp_done")
        hi_done = sem("hi_done")
        lo_done = sem("lo_done")
        y_done = sem("y_done")
        y_read = sem("y_read")
        ln_var = sem("ln_var")
        ln_rstd = sem("ln_rstd")
        x_ready = sem("x_ready")
        rt_mm = sem("rt_mm")
        rt_read = sem("rt_read")
        rt_max = sem("rt_max")
        rt_exp = sem("rt_exp")
        cw_ready = sem("cw_ready")
        exp_split = sem("exp_split")
        gu_done = sem("gu_done")
        sil_done = sem("sil_done")
        h_ready = sem("h_ready")
        ht_done = sem("ht_done")
        hhi_done = sem("hhi_done")
        hlo_done = sem("hlo_done")
        dn_done = sem("dn_done")
        g_mm = sem("g_mm")
        g_read = sem("g_read")
        dec_ready = sem("dec_ready")
        z_ready = sem("z_ready")
        vt_mm = sem("vt_mm")
        vt_hi = sem("vt_hi")
        vt_lo = sem("vt_lo")
        og_mm = sem("og_mm")
        og_pre = sem("og_pre")
        og_silu = sem("og_silu")
        vr_mm = sem("vr_mm")
        d1_done = sem("d1_done")
        s_done = sem("s_done")
        qs_done = sem("qs_done")
        o_mm = sem("o_mm")
        qs_used = sem("qs_used")

        class Counter:
            def __init__(self, eng, s):
                self.eng, self.s, self.n = eng, s, 0

            def link(self, ins):
                ins.then_inc(self.s, 1)
                self.n += 1
                self.eng.wait_ge(self.s, self.n)

            def mark(self, ins):
                ins.then_inc(self.s, 1)
                self.n += 1
                return self.n

            def need(self, n):
                self.eng.wait_ge(self.s, n)

        def col(ap, n):
            return ap.unsqueeze(2).broadcast_to([P, ap.shape[1], n])

        def wait_past(eng, s, count):
            if not isinstance(count, int) or count > 0:
                eng.wait_ge(s, count)

        class Moe:
            def __init__(self, n, E, I, pair):
                self.n, self.E, self.I, self.pair = n, E // pair, I * pair, pair
                self.units = NT
                self.total = self.E * self.units
                self.body = 2 * self.units
                self.IC = 2
                self.IP = self.I // self.IC
                self.gcols = KD * 2 * self.I
                self.dcols = self.IC * D
        MOES = [Moe(0, E0, I0, 1), Moe(1, E1, I1, PAIR)]
        UB = [0, MOES[0].total, MOES[0].total + MOES[1].total]
        EB = [0, MOES[0].E, MOES[0].E + MOES[1].E]

        xd = a["x"].rearrange("b (n p) d -> p (b n) d", p=P)
        outd = out.rearrange("b (n p) d -> p (b n) d", p=P)

        def run_units(eng, m, now, later):
            base = UB[m.n]

            def step(pos, u, have_past):
                if now is not None:
                    now(pos, u)
                for fn, lag in later:
                    if have_past or pos >= lag:
                        fn((pos - lag) % m.body, u - lag)
            for pos in range(m.body):
                step(pos, base + pos, False)
            with eng.Fori(1, m.total // m.body) as i:
                for pos in range(m.body):
                    step(pos, i * m.body + (base + pos), True)
            for pos in range(max(lag for _, lag in later)):
                for fn, lag in later:
                    if pos < lag:
                        fn((pos - lag) % m.body, base + m.total + pos - lag)

        block = ctx.enter_context(nc.Block())

        @block.sync
        def _(sp):
            sp.dma_start(XT, a["xT"].rearrange("(k p) t -> p k t", p=P)).then_inc(ld_xt, 16)
            sp.dma_start(W0T, a["w0T"].rearrange("(k p) n -> p k n", p=P)).then_inc(ld_w0, 16)
            consts = [(ident[:], a["ident"]), (identb[:], a["identb"]), (futb[:], a["futb"]),
                      (head_masks[:], a["head_masks"]), (gate_b[:], a["gate_b"]), (gamma[:], a["gamma"]),
                      (bias_r0[:], a["bias_r0"]), (alpha[:], a["alpha"]), (bkg[:], a["bkg"]), (bg[:], a["bg"]),
                      (wkg2[:], a["wkg2T"]), (iota_e[:], a["iota_e"]), (first8[:], a["first8"]),
                      (block2[:], a["block2"])]
            for dst, src in consts:
                sp.dma_start(dst, src).then_inc(ld_const, 16)
            sp.dma_start(WO0T, a["wo0T"].rearrange("(k p) n -> p k n", p=P)).then_inc(ld_wo0, 16)
            sp.dma_start(WRT[:], a["wrT"].rearrange("(k p) n -> p k n", p=P)).then_inc(ld_wr, 16)
            sp.dma_start(W1T, a["w1T"].rearrange("(k p) n -> p k n", p=P)).then_inc(ld_w1, 16)
            sp.dma_start(WO1T, a["wo1T"].rearrange("(k p) n -> p k n", p=P)).then_inc(ld_wo1, 16)
            sp.dma_start(XA[:], xd).then_inc(ld_x, 16)

            def load_expert(m, e, par, free_at):
                if free_at is not None:
                    sp.wait_ge(exp_split, free_at)
                gate_up, src = (a["gateup0"], a["down0"]) if m.n == 0 else (a["gateup1"], a["down1"])
                sp.dma_start(EG[:, par, 0:m.gcols].rearrange("p (k c) -> p k c", k=KD),
                             gate_up[bass.ds(e, 1)].rearrange("o (k p) i -> p (o k) i", p=P)
                             ).then_inc(ld_exp[par], 16)
                sp.dma_start(ED[0:m.IP, par, 0:m.dcols].rearrange("p (c d) -> p c d", d=D),
                             src[bass.ds(e, 1)].rearrange("o (c p) d -> p (o c) d", p=m.IP)
                             ).then_inc(ld_exp[par], 16)

            for m in MOES:
                for par in range(2):
                    base = EB[m.n] + par
                    load_expert(m, par, par, base - 1 if base >= 2 else None)
                with sp.Fori(1, m.E // 2) as i:
                    for par in range(2):
                        load_expert(m, i * 2 + par, par, i * 2 + (EB[m.n] + par - 1))
            for t in range(NT):
                sp.wait_ge(x_ready, 3 * NT + t + 1)
                sp.dma_start(outd[:, t, :], XA[:, t, :]).then_inc(stored, 16)
            sp.wait_ge(stored, 16 * NT)

        @block.gpsimd
        def _(pool):
            ch = Counter(pool, pool_chain)
            pool.dma_start(sel0[:], a["sel0"]).then_inc(ld_sel, 16)
            pool.dma_start(rep1[:], a["rep1"]).then_inc(ld_sel, 16)

            def split(hi, lo, src):
                ch.link(pool.tensor_scalar(hi, src, 1.0, 0.0, ALU.mult, ALU.add))
                return pool.tensor_tensor(lo, src, hi.bitcast(F32), ALU.subtract)

            ch.link(pool.memset(round_mark[:], 0.0))
            pool.wait_ge(ld_const, 16 * 14)
            pool.wait_ge(ld_wo0, 16)
            for k in range(KD):
                ch.link(pool.tensor_scalar(WO0T[:, k, :], WO0T[:, k, :], gamma[:, k:k + 1], 0.0, ALU.mult, ALU.add))
            split(WO0H[:], WO0L[:], WO0T).then_inc(w_split, 1)
            pool.wait_ge(ld_wr, 16)
            split(WRH[:], WRL[:], WRT[:]).then_inc(w_split, 1)
            pool.wait_ge(v_centred, 2)
            split(W1H[:], W1L[:], W1T).then_inc(w_split, 1)
            pool.wait_ge(ld_wo1, 16)
            split(WO1H[:], WO1L[:], WO1T).then_inc(w_split, 1)

            for t in range(NT):
                pool.wait_ge(hc_ready, t + 1)
                pool.tensor_tensor(OGATE[:, t, :], OGATE[:, t, :], HC[:, t, :], ALU.mult).then_inc(og_ready, 1)

            def split_expert(m, par, loads, free_at, ordinal):
                pool.wait_ge(ld_exp[par], loads)
                if free_at is not None:
                    pool.wait_ge(dn_done, free_at)
                pool.tensor_tensor(round_mark[:, 0:1], round_mark[:, 1:2], round_mark[:, 2:3], ALU.add)
                gh, gl = EGH[:, par, 0:m.gcols], EGL[:, par, 0:m.gcols]
                dh, dl = EDH[0:m.IP, par, 0:m.dcols], EDL[0:m.IP, par, 0:m.dcols]
                pool.tensor_scalar(gh, EG[:, par, 0:m.gcols], 1.0, 0.0, ALU.mult, ALU.add).then_inc(pool_chain, 1)
                pool.tensor_scalar(dh, ED[0:m.IP, par, 0:m.dcols], 1.0, 0.0, ALU.mult, ALU.add).then_inc(pool_chain, 1)
                pool.wait_ge(pool_chain, ordinal * 2 + (chained + 2))
                pool.tensor_tensor(gl, EG[:, par, 0:m.gcols], gh.bitcast(F32), ALU.subtract)
                pool.tensor_tensor(dl, ED[0:m.IP, par, 0:m.dcols], dh.bitcast(F32), ALU.subtract
                                   ).then_inc(exp_split, 1)

            chained = ch.n
            per0 = per1 = 16 * 2
            m = MOES[0]
            for e in range(2):
                split_expert(m, e % 2, per0, None, e)
            with pool.Fori(1, m.E // 2) as i:
                for par in range(2):
                    split_expert(m, par, i * per0 + per0, i * m.body + (par + 1) * m.units - m.body, i * 2 + par)
            m = MOES[1]
            had = per0 * (EB[1] // 2)
            for e in range(2):
                split_expert(m, e % 2, had + per1, UB[1] - (1 - e) * MOES[0].units, EB[1] + e)
            pool.wait_ge(q_ready, 2)
            for v in range(DV1):
                pool.wait_ge(s_done, v + 1)
                if v >= 2:
                    pool.wait_ge(qs_used, v - 1)
                pool.tensor_tensor(QS[:, v % 2, :], STATE[:, v % 2, :], QT[:], ALU.mult).then_inc(qs_done, 1)
            with pool.Fori(1, m.E // 2) as i:
                for par in range(2):
                    split_expert(m, par, i * per1 + (had + per1),
                                 i * m.body + (UB[1] + (par + 1) * m.units - m.body), i * 2 + (EB[1] + par))

        @block.scalar
        def _(act):
            ch = Counter(act, act_chain)

            warmed = itertools.count()

            def warm(func):
                c = next(warmed)
                act.activation(act_scratch[:, c:c + 1], ident[:, 0:1], func)

            act.wait_ge(v_centred, 1)
            act.activation(W0H, W0T, ACT.Copy).then_inc(w0_hi, 1)
            act.wait_ge(ld_xt, 16)
            act.activation(XH[:], XT, ACT.Copy).then_inc(xt_hi, 1)
            act.wait_ge(gate_bias, 1)
            act.wait_ge(gate_mm, 1)
            act.activation(GI[:], bank(0)[:, 0:S], ACT.Tanh, bias=gate_bs[:, 0:1], scale=1.0 / CAP).then_inc(tanh_done, 1)
            ch.link(act.activation(GF[:], bank(1)[:, 0:S], ACT.Tanh, bias=gate_bs[:, 1:2], scale=1.0 / CAP))
            ch.link(act.activation(GF[:], GF[:], ACT.Exp, scale=-CAP))
            act.activation(GF[:], GF[:], ACT.Ln, bias=1.0).then_inc(soft_done, 1)
            act.wait_ge(qk_mm, 2)
            for hf in range(2):
                act.activation(QT[:, hf * BANK:(hf + 1) * BANK], bank(2 + hf), ACT.Copy).then_inc(q_ready, 1)
            act.wait_ge(ones_set, 1)
            for t in range(NT):
                act.wait_ge(vo_mm, t + 1)
                act.activation(VX[:, t, :, 0:DV0], bank(6 + t % 2)[:, 0:D].rearrange("p (h v) -> p h v", h=NH0), ACT.Copy)
                act.activation(OGATE[:, t, :], bank(6 + t % 2)[:, D:2 * D], ACT.Sigmoid).then_inc(vo_done, 1)
            act.wait_ge(nl_ready, 1)
            act.activation(NL[:], NL[:], ACT.Exp).then_inc(floor_ready, 1)
            act.wait_ge(at_ready, 1)

            def square(t):
                act.wait_ge(hc_ready, t + 1)
                if t >= 4:
                    act.wait_ge(sq_read, t - 3)
                act.activation(SQ[:, t % 4, :], HC[:, t, :], ACT.Square).then_inc(sq_done, 1)

            for u in range(B * NH0):
                b, h = u // NH0, u % NH0
                act.wait_ge(r_ready, u + 1)
                if u >= 2:
                    act.wait_ge(w_ready, u - 1)
                c = 32 * b + h
                act.activation(EW[:, u % 2, 0:S], bank(u % 2)[:, 0:S], ACT.Exp, bias=ATF[:, 0, 0, c:c + 1])
                act.activation(EW[:, u % 2, S:S + P], bank(u % 2)[:, S:S + P], ACT.Exp,
                               bias=ATF[:, 0, 1, c:c + 1]).then_inc(e_ready, 1)
                if u >= NH0 and u % NH0 in (3, 6):
                    square((u // NH0 - 1) * TB + (u % NH0 - 3) // 3)

            for tt in range(TB):
                square((B - 1) * TB + tt)

            def head_rstd(n, nh):
                warm(ACT.Sqrt)
                act.wait_ge(var_ready, n + 1)
                act.activation(hr[:, :, 0:nh], hr[:, :, 0:nh], ACT.Sqrt).then_inc(rstd_ready, 1)

            def hi_parts(n, dst):
                for p in range(NT // 2):
                    act.wait_ge(tp_done, n * (NT // 2) + p + 1)
                    act.activation(dst[:, :, p * 2 * P:(p + 1) * 2 * P].rearrange("p k (t c) -> p t k c", t=2),
                                   bank(p).rearrange("p (t k c) -> p t k c", t=2, k=KD), ACT.Copy).then_inc(hi_done, 1)

            def ln_sqrt(n):
                warm(ACT.Sqrt)
                act.wait_ge(ln_var, n + 1)
                act.activation(rstd[:], rv[:], ACT.Sqrt).then_inc(ln_rstd, 1)
                warm(ACT.Exp)

            def router_exp(n, E):
                act.wait_ge(rt_max, n + 1)
                act.activation(PR[:, :, 0:E], LG[:, :, 0:E], ACT.Exp).then_inc(rt_exp, 1)
                warm(ACT.Silu)

            def moe_act(m):
                IP, I = m.IP, m.I

                def silu(pos, u):
                    s = pos % 2
                    act.wait_ge(gu_done, u + 1)
                    wait_past(act, h_ready, u - 1)
                    act.activation(SIL[:, s, 0:I], bank(s)[:, 0:I], ACT.Silu).then_inc(sil_done, 1)

                def hi(pos, u):
                    s = pos % 2
                    act.wait_ge(ht_done, u + 1)
                    wait_past(act, dn_done, u - 1)
                    act.activation(EHH[0:IP, s, :], bank(2 + s)[0:IP, 0:256], ACT.Copy).then_inc(hhi_done, 1)

                run_units(act, m, silu, [(hi, 1)])

            head_rstd(0, NH0)
            hi_parts(0, HTH)
            ln_sqrt(0)
            hi_parts(1, XH)
            router_exp(0, E0)
            moe_act(MOES[0])
            ln_sqrt(1)
            hi_parts(2, XH)

            act.wait_ge(g_mm, 1)
            for hf in range(2):
                act.activation(QT[:, hf * BANK:(hf + 1) * BANK], bank(hf), ACT.Copy).then_inc(q_ready, 1)
            act.wait_ge(g_mm, 2)
            for hf in range(2):
                act.activation(KT[:, hf * BANK:(hf + 1) * BANK], bank(2 + hf), ACT.Copy, scale=KSCALE).then_inc(k_ready, 1)
            act.wait_ge(g_mm, 3)
            for hf in range(2):
                act.activation(KGL[0:16, hf * BANK:(hf + 1) * BANK], bank(4 + hf)[0:16, :], ACT.Copy).then_inc(z_ready, 1)
            act.wait_ge(dec_ready, 1)
            ch.link(act.activation(KGL, KGL, ACT.Exp, scale=-1.0))
            act.activation(KGL, KGL, ACT.Ln, bias=1.0).then_inc(dec_ready, 1)
            act.wait_ge(dec_ready, 3)
            act.activation(DEC, KG, ACT.Exp, scale=1.0 / GATE_NORM).then_inc(dec_ready, 1)
            for n in range(4):
                act.wait_ge(vt_mm, n + 1)
                act.activation(VTH[:, n // 2, (n % 2) * BANK:(n % 2 + 1) * BANK], bank(n), ACT.Copy).then_inc(vt_hi, 1)
            for p in range(NT // 2):
                act.wait_ge(og_pre, p + 1)
                act.activation(OGATE[:, 2 * p:2 * p + 2, :], OGATE[:, 2 * p:2 * p + 2, :], ACT.Silu).then_inc(og_silu, 1)
            for n in range(2):
                act.wait_ge(qs_used, DV1)
                act.activation(OT[:, 1, n * BANK:(n + 1) * BANK], bank(6 + n), ACT.Copy).then_inc(ot_evac, 1)
            for p in range(NT // 2):
                act.wait_ge(o_mm, p + 1)
                if 2 * p >= 4:
                    act.wait_ge(sq_read, NT + 2 * p - 2)
                o = bank(p).rearrange("p (t v h) -> p t h v", t=2, v=DV1)
                for t in range(2):
                    act.activation(SQ[:, (2 * p + t) % 4, :].rearrange("p (h v) -> p h v", h=NH1), o[:, t],
                                   ACT.Square).then_inc(sq_done, 1)
            head_rstd(1, NH1)
            hi_parts(3, HTH)
            ln_sqrt(2)
            hi_parts(4, XH)
            router_exp(1, E1)
            moe_act(MOES[1])
            ln_sqrt(3)

        @block.vector
        def _(dve):
            ch = Counter(dve, dve_chain)
            dve.memset(zb[:], 0.0).then_inc(zb_set, 1)
            dve.wait_ge(ld_xt, 16)
            dve.wait_ge(ld_w0, 16)
            dve.memset(VX[:, :, :, DV0:DV0 + 1], 1.0).then_inc(ones_set, 1)
            dve.wait_ge(ld_const, 16 * 14)
            dve.tensor_scalar(gate_bs[:], gate_b[:], 1.0 / CAP, None, ALU.mult).then_inc(gate_bias, 1)
            def centre_values(view, shape):
                nh = shape[1]
                acc = hn[:, 0:KD, 0:nh]
                for k in range(KD):
                    ins = dve.tensor_reduce(hn[:, k, 0:nh], view(k), AX_X, ALU.add)
                ch.link(ins)
                ch.link(dve.tensor_scalar(acc, acc, -1.0 / (D // nh), None, ALU.mult))
                for k in range(KD):
                    ins = dve.tensor_tensor(view(k), view(k), col(hn[:, k, 0:nh], D // nh), ALU.add)
                return ins
            centre_values(lambda k: W0T[:, k, V0:V0 + D].rearrange("p (h v) -> p h v", h=NH0), (P, NH0)
                          ).then_inc(v_centred, 1)
            dve.wait_ge(w0_hi, 1)
            dve.tensor_tensor(W0L, W0T, W0H.bitcast(F32), ALU.subtract).then_inc(x0_split, 1)
            dve.wait_ge(xt_hi, 1)
            dve.tensor_tensor(XL[:], XT, XH[:].bitcast(F32), ALU.subtract).then_inc(x0_split, 1)
            dve.wait_ge(ld_w1, 16)
            centre_values(lambda k: W1T[:, k, V1:V1 + D].rearrange("p (v h) -> p h v", h=NH1), (P, NH1)
                          ).then_inc(v_centred, 1)

            dve.wait_ge(soft_done, 1)
            ch.link(dve.tensor_tensor_scan(NL[:], GF[:], GF[:], 0.0, ALU.add, ALU.max))
            dve.wait_ge(tanh_done, 1)
            ch.link(dve.scalar_tensor_tensor(out=AS[:], in0=GI[:], scalar=CAP, in1=NL[:], op0=ALU.mult, op1=ALU.add))
            ch.link(dve.tensor_tensor_scan(MX[:], AS[:], AS[:], 0.0, ALU.max, ALU.max))
            dve.tensor_tensor(NL[:], NL[:], MX[:], ALU.subtract).then_inc(nl_ready, 1)
            ch.link(dve.tensor_scalar(MX[:], MX[:], -1.0, None, ALU.mult))
            ch.link(dve.tensor_copy(NMH[:], MX[:]))
            ch.link(dve.tensor_tensor(NML[:], MX[:], NMH[:].bitcast(F32), ALU.subtract))
            ch.link(dve.tensor_scalar(NML[:], NML[:], head_masks[:, 3:4], None, ALU.mult))
            dve.scalar_tensor_tensor(out=NMD[:], in0=NMH[:].bitcast(F32), scalar=head_masks[:, 2:3], in1=NML[:],
                                     op0=ALU.mult, op1=ALU.add).then_inc(nm_ready, 1)
            dve.wait_ge(qk_mm, 4)
            for hf in range(2):
                dve.tensor_scalar(KTE[:, hf * BANK:(hf + 1) * BANK], bank(4 + hf), head_masks[:, 0:1], None, ALU.mult)
                dve.tensor_scalar(KTO[:, hf * BANK:(hf + 1) * BANK], bank(4 + hf), head_masks[:, 1:2], None,
                                  ALU.mult).then_inc(k_ready, 1)
            dve.wait_ge(gt_mm, 1)
            dve.tensor_copy(ATF[:].rearrange("p a t c -> p (a t c)"), bank(4)).then_inc(at_ready, 1)

            def mlstm_heads(t):
                b, tt = t // TB, t % TB
                if t == 0:
                    dve.wait_ge(at_ready, 1)
                ao = bank(4 + 2 * (b % 2) + tt)[:, 0:NH0 * (DV0 + 1)].rearrange("p (h v) -> p h v", h=NH0)
                qn = ao[:, :, DV0]
                dve.wait_ge(av_done, (b + 1) * NH0)
                ch.link(dve.scalar_tensor_tensor(out=den[:, 0, :], in0=qn, scalar=-1.0,
                                                 in1=ATF[:, 1, tt, 32 * b:32 * b + NH0], op0=ALU.mult, op1=ALU.max))
                ch.link(dve.tensor_tensor(den[:, 1, :], qn, den[:, 0, :], ALU.max))
                ch.link(dve.tensor_scalar(den[:, 1, :], den[:, 1, :], EPS_M, None, ALU.add))
                ch.link(dve.reciprocal(den[:, 2, :], den[:, 1, :]))
                dve.tensor_tensor(HC[:, t, :].rearrange("p (h v) -> p h v", h=NH0), ao[:, :, 0:DV0],
                                  col(den[:, 2, :], DV0), ALU.mult).then_inc(hc_ready, 1)

            def head_sums(n, t, nh):
                dve.wait_ge(sq_done, n * NT + t + 1)
                dve.tensor_reduce(hs[:, t, 0:nh], SQ[:, t % 4, :].rearrange("p (h v) -> p h v", h=nh), AX_X, ALU.add
                                  ).then_inc(sq_read, 1)

            def head_var(n, nh, eps):
                dve.wait_ge(sq_read, (n + 1) * NT)
                ch.link(dve.tensor_scalar(hs[:, :, 0:nh], hs[:, :, 0:nh], nh / D, eps, ALU.mult, ALU.add))
                dve.reciprocal(hr[:, :, 0:nh], hs[:, :, 0:nh]).then_inc(var_ready, 1)

            dve.wait_ge(vo_done, NT)
            dve.wait_ge(w_split, 4)
            for u in range(B * NH0):
                dve.wait_ge(e_ready, u + 1)
                dve.wait_ge(qk_ready, u + 1)
                if u >= 2:
                    dve.wait_ge(av_done, u - 1)
                dve.tensor_tensor(WW[:, u % 2, :], EW[:, u % 2, :], bank(2 + u % 2)[:, 0:3 * P],
                                  ALU.mult).then_inc(w_ready, 1)
                done = u // NH0 - 1
                if done >= 0:
                    for tt in range(TB):
                        if u % NH0 == 1 + 3 * tt:
                            mlstm_heads(done * TB + tt)
                        if u % NH0 == 3 + 3 * tt:
                            head_sums(0, done * TB + tt, NH0)
            for tt in range(TB):
                mlstm_heads((B - 1) * TB + tt)
            for tt in range(TB):
                head_sums(0, (B - 1) * TB + tt, NH0)
            head_var(0, NH0, EPS_M)

            def apply_rstd(n, nh):
                dve.wait_ge(rstd_ready, n + 1)
                dve.wait_ge(og_ready, (n + 1) * NT)
                for t in range(NT):
                    dve.tensor_tensor(HC[:, t, :].rearrange("p (h v) -> p h v", h=nh),
                                      OGATE[:, t, :].rearrange("p (h v) -> p h v", h=nh),
                                      col(hr[:, t, 0:nh], D // nh), ALU.mult).then_inc(gated, 1)

            def lo_parts(n, dst, hi):
                for p in range(NT // 2):
                    dve.wait_ge(hi_done, n * (NT // 2) + p + 1)
                    ap = lambda x: x[:, :, p * 2 * P:(p + 1) * 2 * P].rearrange("p k (t c) -> p t k c", t=2)
                    for t in range(2):
                        ins = dve.tensor_tensor(ap(dst)[:, t], bank(p).rearrange("p (t k c) -> p t k c", t=2, k=KD)[:, t],
                                                ap(hi).bitcast(F32)[:, t], ALU.subtract)
                    ins.then_inc(lo_done, 1)

            def layernorm(n, res, dst):
                added = []
                for p in range(NT // 2 + 1):
                    if p < NT // 2:
                        dve.wait_ge(y_done, n * NT + 2 * p + 2)
                        added.append(ch.mark(dve.tensor_tensor(
                            dst[:, 2 * p:2 * p + 2, :], bank(4 + p).rearrange("p (t d) -> p t d", t=2),
                            res[:, 2 * p:2 * p + 2, :], ALU.add)))
                    if p >= 1:
                        ch.need(added[p - 1])
                        for t in (2 * p - 2, 2 * p - 1):
                            stats = ch.mark(dve.bn_stats(st[:, t, :], dst[:, t, :]))
                ch.need(stats)
                for t in range(NT):
                    ins = dve.bn_aggr(mv[:, t, :], st[:, t, :])
                ch.link(ins)
                ch.link(dve.tensor_scalar(rv[:], mv[:, :, 1], EPS_LN, None, ALU.add))
                dve.reciprocal(rv[:], rv[:]).then_inc(ln_var, 1)
                dve.wait_ge(ln_rstd, n + 1)
                for t in range(NT):
                    dve.tensor_scalar(dst[:, t, :], dst[:, t, :], mv[:, t, 0:1], rstd[:, t:t + 1],
                                      ALU.subtract, ALU.mult).then_inc(x_ready, 1)

            def softmax(n, E, bias):
                lg, pr = LG[:, :, 0:E], PR[:, :, 0:E]
                dve.wait_ge(rt_mm, n + 1)
                src = bank(4)[:, 0:NT * E].rearrange("p (t e) -> p t e", t=NT)
                if bias is None:
                    ins = dve.tensor_copy(lg, src)
                else:
                    ins = dve.tensor_tensor(lg, src, bias.unsqueeze(1).broadcast_to([P, NT, E]), ALU.add)
                ins.then_inc(rt_read, 1)
                dve.wait_ge(rt_read, n + 1)
                ch.link(dve.tensor_reduce(rsum[:], lg, AX_X, ALU.max))
                dve.tensor_tensor(lg, lg, col(rsum[:], E), ALU.subtract).then_inc(rt_max, 1)
                dve.wait_ge(rt_exp, n + 1)
                ch.link(dve.tensor_reduce(rsum[:], pr, AX_X, ALU.add))
                ch.link(dve.reciprocal(rsum[:], rsum[:]))
                ch.link(dve.tensor_tensor(pr, pr, col(rsum[:], E), ALU.mult))
                for t in range(NT):
                    ins = dve.max(top[:, t, :], PR[:, t, 0:E])
                ch.link(ins)
                for t in range(NT):
                    ins = dve.max_index(tix[:, t, :], top[:, t, :], PR[:, t, 0:E])
                ch.link(ins)
                ch.link(dve.tensor_copy(tif[:], tix[:]))

            def normalise(dst, src, k, floor):
                ch.link(dve.tensor_reduce(rsum[:], src[:, :, 0:k], AX_X, ALU.add))
                if floor is not None:
                    ch.link(dve.tensor_scalar(rsum[:], rsum[:], floor, None, ALU.max))
                ch.link(dve.reciprocal(rsum[:], rsum[:]))
                ch.link(dve.tensor_tensor(dst[:, :, 0:k], src[:, :, 0:k], col(rsum[:], k), ALU.mult))

            def combine(E, k, w):
                io = iota_e[:, 0:E].unsqueeze(1).broadcast_to([P, NT, E])
                eq, cw = EQ[:, :, 0:E], CW[:, :, 0:E]
                for j in range(k):
                    dst = cw if j == 0 else eq
                    ch.link(dve.tensor_tensor(eq, io, col(tif[:, :, j], E), ALU.is_equal))
                    ch.link(dve.tensor_tensor(dst, eq, col(w[:, :, j], E), ALU.mult))
                    if j:
                        ins = dve.tensor_tensor(cw, cw, eq, ALU.add)
                        if j < k - 1:
                            ch.link(ins)
                ins.then_inc(cw_ready, 1)
                dve.wait_ge(cw_ready, 1 if E == E0 else 2)

            def route1():
                normalise(t1, top, 8, 1e-12)
                ch.link(dve.tensor_scalar(t2[:], t1[:], alpha[:, 0:1], None, ALU.mult))
                ch.link(dve.tensor_reduce(rsum[:], t2[:], AX_X, ALU.max))
                ch.link(dve.tensor_tensor(t3[:], t2[:], col(rsum[:], 8), ALU.is_equal))
                f8 = first8[:].unsqueeze(1).broadcast_to([P, NT, 8])
                ch.link(dve.tensor_tensor(t3[:], t3[:], f8, ALU.mult))
                ch.link(dve.tensor_reduce(rsum[:], t3[:], AX_X, ALU.max))
                ch.link(dve.tensor_tensor(t3[:], f8, col(rsum[:], 8), ALU.is_equal))
                ch.link(dve.tensor_scalar(t2[:], t2[:], TAU, None, ALU.is_ge))
                ch.link(dve.tensor_reduce(rsum[:], t2[:], AX_X, ALU.max))
                ch.link(dve.tensor_scalar(rsum[:], rsum[:], -1.0, 1.0, ALU.mult, ALU.add))
                ch.link(dve.tensor_tensor(t3[:], t3[:], col(rsum[:], 8), ALU.mult))
                ch.link(dve.tensor_tensor(t2[:], t2[:], t3[:], ALU.max))
                ch.link(dve.tensor_tensor(t1[:], t1[:], t2[:], ALU.mult))
                normalise(t2, t1, 8, 1e-12)

            def moe_dve(m):
                I, IP = m.I, m.IP
                W = I // m.pair

                def gate_up(pos, u):
                    s = pos % 2
                    dve.wait_ge(sil_done, u + 1)
                    wait_past(dve, ht_done, u - 1)
                    t, first = pos % m.units, pos // m.units
                    for j in range(m.pair):
                        if isinstance(u, int):
                            c = CW[:, t, first * m.pair + j:first * m.pair + j + 1]
                        else:
                            round_ = (u - (UB[m.n] + pos)) // m.units
                            c = CW[:, t, bass.ds(round_ * m.pair + (first * m.pair + j), 1)]
                        ins = dve.scalar_tensor_tensor(
                            out=HH[:, s, j * W:(j + 1) * W], in0=SIL[:, s, j * W:(j + 1) * W], scalar=c,
                            in1=bank(s)[:, I + j * W:I + (j + 1) * W], op0=ALU.mult, op1=ALU.mult)
                    ins.then_inc(h_ready, 1)

                def lo(pos, u):
                    s = pos % 2
                    dve.wait_ge(hhi_done, u + 1)
                    dve.tensor_tensor(EHL[0:IP, s, :], bank(2 + s)[0:IP, 0:256], EHH[0:IP, s, :].bitcast(F32),
                                      ALU.subtract).then_inc(hlo_done, 1)

                run_units(dve, m, gate_up, [(lo, 1)])

            apply_rstd(0, NH0)
            lo_parts(0, HTL, HTH)
            dve.wait_ge(ld_x, 16)
            dve.wait_ge(w_split, 3)
            layernorm(0, XA, XB)
            lo_parts(1, XL, XH)
            softmax(0, E0, bias_r0[:])
            normalise(t2, top, 4, None)
            combine(E0, 4, t2)
            moe_dve(MOES[0])
            layernorm(1, XB, XA)
            lo_parts(2, XL, XH)

            for hf in range(2):
                dve.wait_ge(g_mm, 4 + hf)
                dve.tensor_scalar(KG[:, hf * BANK:(hf + 1) * BANK], bank(6 + hf), bkg[:, 0:1], None,
                                  ALU.add).then_inc(g_read, 1)
            dve.wait_ge(g_read, 2)
            dve.scalar_tensor_tensor(out=KGL, in0=KG, scalar=-1.0, in1=KG, op0=ALU.mult, op1=ALU.max
                                     ).then_inc(dec_ready, 1)
            dve.wait_ge(dec_ready, 2)
            dve.scalar_tensor_tensor(out=KG, in0=KG, scalar=0.0, in1=KGL, op0=ALU.min, op1=ALU.subtract
                                     ).then_inc(dec_ready, 1)
            for n in range(4):
                dve.wait_ge(vt_hi, n + 1)
                dve.tensor_tensor(VTL[:, n // 2, (n % 2) * BANK:(n % 2 + 1) * BANK], bank(n),
                                  VTH[:, n // 2, (n % 2) * BANK:(n % 2 + 1) * BANK].bitcast(F32),
                                  ALU.subtract).then_inc(vt_lo, 1)
            for p in range(NT // 2):
                dve.wait_ge(og_mm, p + 1)
                dve.tensor_tensor(OGATE[:, 2 * p:2 * p + 2, :], bank(4 + p).rearrange("p (t d) -> p t d", t=2),
                                  bg[:].unsqueeze(1).broadcast_to([P, 2, D]), ALU.add).then_inc(og_pre, 1)
            dve.wait_ge(dec_ready, 4)
            ch.link(dve.memset(DEC.rearrange("p (b s) -> p b s", b=B)[:, :, 0:1], 0.0))
            dve.wait_ge(k_ready, 4)
            for v in range(DV1):
                s = v % 2
                dve.wait_ge(vr_mm, v + 1)
                kv = PS[:, 2 * s:2 * s + 2, :].rearrange("p k c -> p (k c)")
                dve.tensor_tensor(kv, KT, kv, ALU.mult).then_inc(d1_done, 1)
                dve.wait_ge(d1_done, v + 1)
                if v >= 2:
                    dve.wait_ge(qs_done, v - 1)
                dve.tensor_tensor_scan(STATE[:, s, :], DEC, kv, 0.0, ALU.mult, ALU.add).then_inc(s_done, 1)
            for n in range(2):
                dve.wait_ge(qs_used, DV1 // 2)
                dve.tensor_copy(OT[:, 0, n * BANK:(n + 1) * BANK], bank(4 + n)).then_inc(ot_evac, 1)
            for p in range(NT // 2):
                dve.wait_ge(o_mm, p + 1)
                dve.wait_ge(sq_done, NT + 2 * p + 2)
                o = bank(p).rearrange("p (t v h) -> p t h v", t=2, v=DV1)
                for t in range(2):
                    ins = dve.tensor_tensor(OGATE[:, 2 * p + t, :].rearrange("p (h v) -> p h v", h=NH1), o[:, t],
                                            OGATE[:, 2 * p + t, :].rearrange("p (h v) -> p h v", h=NH1), ALU.mult)
                    ins.then_inc(og_ready, 1)
                for t in range(2):
                    head_sums(1, 2 * p + t, NH1)
            head_var(1, NH1, EPS_G)
            apply_rstd(1, NH1)
            lo_parts(3, HTL, HTH)
            layernorm(2, XA, XB)
            lo_parts(4, XL, XH)
            softmax(1, E1, None)
            route1()
            combine(E1, 8, t2)
            moe_dve(MOES[1])
            layernorm(3, XB, XA)

        @block.tensor
        def _(pe):
            def mm3(o, lhs, rhs, start, stop):
                n = 3 * len(lhs)
                i = 0
                for (lh, ll), (rh, rl) in zip(lhs, rhs):
                    for l, r in ((lh, rh), (lh, rl), (ll, rh)):
                        ins = pe.matmul(o, l, r, start=start and i == 0, stop=stop and i == n - 1,
                                        skip_group_check=True)
                        i += 1
                return ins

            def xs(t):
                return [(XH[:, k, t * P:(t + 1) * P], XL[:, k, t * P:(t + 1) * P]) for k in range(KD)]

            def xm(hf):
                return [(XH[:, k, hf * BANK:(hf + 1) * BANK], XL[:, k, hf * BANK:(hf + 1) * BANK]) for k in range(KD)]

            def ws(wh, wl, c, n):
                return [(wh[:, k, c:c + n], wl[:, k, c:c + n]) for k in range(KD)]

            pe.wait_ge(ld_xt, 16)
            pe.wait_ge(ld_w0, 16)
            for g, c in ((0, IG0), (1, FG0)):
                for b in range(B):
                    for k in range(KD):
                        ins = pe.matmul(bank(g)[32 * b:32 * b + 32, 0:S], W0T[:, k, c:c + 32],
                                        XT[:, k, b * S:(b + 1) * S], start=(k == 0), stop=(k == KD - 1))
            ins.then_inc(gate_mm, 1)
            pe.wait_ge(x0_split, 2)
            for g, c in ((2, Q0), (4, K0)):
                for hf in range(2):
                    mm3(bank(g + hf), ws(W0H, W0L, c, P), xm(hf), True, True).then_inc(qk_mm, 1)
            for t in range(NT):
                if t >= 2:
                    pe.wait_ge(vo_done, t - 1)
                mm3(bank(6 + t % 2), xs(t), ws(W0H, W0L, 0, 2 * D), True, True).then_inc(vo_mm, 1)
            pe.wait_ge(ld_const, 16 * 14)
            pe.wait_ge(k_ready, 2)
            pe.wait_ge(nm_ready, 1)
            pe.wait_ge(floor_ready, 1)
            for i, src in enumerate((AS, NL)):
                for tt in range(TB):
                    ins = pe.transpose(bank(4)[:, (2 * i + tt) * P:(2 * i + tt + 1) * P],
                                       src[:, tt * P:(tt + 1) * P], ident[:])
            ins.then_inc(gt_mm, 1)

            def scores(u):
                b, h = u // NH0, u % NH0
                r, q = bank(u % 2), bank(2 + u % 2)
                if u >= 2:
                    pe.wait_ge(e_ready, u - 1)
                sel = sel0[:, u:u + 1].broadcast_to([P, P])
                pe.matmul(r[:, 0:S], sel, NMD[:], start=True, stop=False, skip_group_check=True)
                pe.matmul(r[:, S:S + P], sel, NMD[:, P:S], start=False, stop=False, skip_group_check=True)
                pe.matmul(r[:, 0:P], identb[:], futb[:], start=False, stop=False, skip_group_check=True)
                pe.matmul(r[:, S:S + P], identb[:], futb[:], start=False, stop=True, skip_group_check=True
                          ).then_inc(r_ready, 1)
                if u >= 2:
                    pe.wait_ge(w_ready, u - 1)
                rows = slice(32 * (h // 2), 32 * (h // 2) + 32)
                kt = KTE if h % 2 == 0 else KTO
                pe.matmul(q[:, 0:S], kt[rows, b * S:b * S + P], QT[rows, b * S:(b + 1) * S],
                          start=True, stop=False, skip_group_check=True)
                pe.matmul(q[:, S:S + P], kt[rows, b * S + P:b * S + 2 * P], QT[rows, b * S + P:b * S + 2 * P],
                          start=False, stop=True, skip_group_check=True).then_inc(qk_ready, 1)

            def values(u):
                b, h = u // NH0, u % NH0
                if h == 0:
                    if b == 0:
                        pe.wait_ge(at_ready, 1)
                    if b >= 2:
                        pe.wait_ge(hc_ready, (b - 1) * TB)
                pe.wait_ge(w_ready, u + 1)
                c = slice(h * (DV0 + 1), (h + 1) * (DV0 + 1))
                w = WW[:, u % 2, :]
                v0, v1 = VX[:, TB * b, h, :], VX[:, TB * b + 1, h, :]
                o0, o1 = bank(4 + 2 * (b % 2))[:, c], bank(5 + 2 * (b % 2))[:, c]
                pe.matmul(o0, w[:, 0:P], v0, start=(h == 0), stop=True, skip_group_check=True)
                pe.matmul(o1, w[:, P:2 * P], v0, start=(h == 0), stop=False, skip_group_check=True)
                pe.matmul(o1, w[:, 2 * P:3 * P], v1, start=False, stop=True, skip_group_check=True
                          ).then_inc(av_done, 1)

            pe.wait_ge(ld_sel, 32)
            pe.wait_ge(q_ready, 2)
            pe.wait_ge(tanh_done, 1)
            pe.wait_ge(vo_done, NT)
            for u in range(B * NH0 + 1):
                if u < B * NH0:
                    scores(u)
                if u >= 1:
                    values(u - 1)

            def transposes(n, src, ready, base):
                for p in range(NT // 2):
                    pe.wait_ge(ready, base + 2 * (p + 1))
                    for t in range(2):
                        for k in range(KD):
                            ins = pe.transpose(bank(p)[:, (2 * t + k) * P:(2 * t + k + 1) * P],
                                               src[:, 2 * p + t, k * P:(k + 1) * P], ident[:])
                    ins.then_inc(tp_done, 1)

            def project(n, wh, wl):
                for t in range(NT):
                    if t % 2 == 0:
                        pe.wait_ge(lo_done, n * (NT // 2) + t // 2 + 1)
                    lhs = [(HTH[:, k, t * P:(t + 1) * P], HTL[:, k, t * P:(t + 1) * P]) for k in range(KD)]
                    mm3(bank(4 + t // 2)[:, (t % 2) * D:(t % 2 + 1) * D], lhs, ws(wh, wl, 0, D),
                        t % 2 == 0, True).then_inc(y_done, 1)

            def router(n, tp, c, E):
                for t in range(NT):
                    if t % 2 == 0:
                        pe.wait_ge(lo_done, tp * (NT // 2) + t // 2 + 1)
                    for i in range(4 * KD):
                        k, part = i // 4, i % 4
                        l = (XH, XL)[part // 2][:, k, t * P:(t + 1) * P]
                        r = (WRH, WRL)[part % 2][:, k, c:c + E]
                        ins = pe.matmul(bank(4)[:, t * E:(t + 1) * E], l, r, start=(t == 0 and i == 0),
                                        stop=(i == 4 * KD - 1), skip_group_check=True)
                ins.then_inc(rt_mm, 1)

            def moe_pe(m):
                I, IP, IC = m.I, m.IP, m.IC
                base = UB[m.n]
                for n in (3, 2, 1, 0):
                    if n == 0:
                        pe.wait_ge(rt_read, m.n + 1)
                    pe.matmul(bank(4 + n), zb[:, 0:P], zb[:], start=True, stop=True, skip_group_check=True)

                def gate_up(pos, u):
                    s, par = pos % 2, pos // m.units
                    if pos % m.units == 0:
                        first = (u - (base + pos)) // m.units if not isinstance(u, int) else 0
                        pe.wait_ge(exp_split, first + (EB[m.n] + par + 1))
                    wait_past(pe, h_ready, u - 1)
                    w = [EG_.rearrange("p (k c) -> p k c", k=KD) for EG_ in (EGH[:, par, 0:m.gcols], EGL[:, par, 0:m.gcols])]
                    ins = mm3(bank(s)[:, 0:2 * I], xs(pos % m.units), [(w[0][:, k, :], w[1][:, k, :]) for k in range(KD)],
                              True, True)
                    ins.then_inc(gu_done, 1)

                def turn(pos, u):
                    s = pos % 2
                    pe.wait_ge(h_ready, u + 1)
                    wait_past(pe, hlo_done, u - 1)
                    for j in range(2):
                        ins = pe.transpose(bank(2 + s)[0:IP, j * P:(j + 1) * P], HH[:, s, j * IP:(j + 1) * IP], ident[:])
                    ins.then_inc(ht_done, 1)

                def down(pos, u):
                    s, par = pos % 2, pos // m.units
                    pe.wait_ge(hlo_done, u + 1)
                    t = pos % m.units
                    lhs = [(EHH[0:IP, s, c * P:(c + 1) * P], EHL[0:IP, s, c * P:(c + 1) * P]) for c in range(IC)]
                    rhs = [(EDH[0:IP, par, c * D:(c + 1) * D], EDL[0:IP, par, c * D:(c + 1) * D]) for c in range(IC)]
                    ins = mm3(bank(4 + t // 2)[:, (t % 2) * D:(t % 2 + 1) * D], lhs, rhs, False, True)
                    ins.then_inc(dn_done, 1)

                run_units(pe, m, gate_up, [(turn, 1), (down, 2)])
                pe.wait_ge(dn_done, base + m.total)

            def release_y(n):
                for t in range(NT):
                    pe.matmul(bank(0)[:, 0:2], zb[:, 0:P], zb[:, 0:2], start=True, stop=True,
                              skip_group_check=True).then_inc(y_done, 1)

            transposes(0, HC, gated, 0)
            pe.wait_ge(w_split, 1)
            project(0, WO0H, WO0L)
            transposes(1, XB, x_ready, 0)
            pe.wait_ge(w_split, 2)
            router(0, 1, 0, E0)
            pe.wait_ge(zb_set, 1)
            moe_pe(MOES[0])
            release_y(1)
            transposes(2, XA, x_ready, NT)

            pe.wait_ge(lo_done, 3 * (NT // 2))
            pe.wait_ge(w_split, 4)
            for g, c in ((0, Q1), (2, K1), (4, Z1)):
                for hf in range(2):
                    ins = mm3(bank(g + hf), ws(W1H, W1L, c, P), xm(hf), True, True)
                ins.then_inc(g_mm, 1)
            for hf in range(2):
                pe.wait_ge(z_ready, hf + 1)
                pe.matmul(bank(6 + hf), wkg2[:], KGL[0:16, hf * BANK:(hf + 1) * BANK], start=True, stop=True
                          ).then_inc(g_mm, 1)
            pe.wait_ge(q_ready, 4)
            pe.wait_ge(k_ready, 4)
            for n in range(4):
                mm3(bank(n), ws(W1H, W1L, V1 + (n // 2) * P, P), xm(n % 2), True, True).then_inc(vt_mm, 1)
            pe.wait_ge(g_read, 2)
            for t in range(NT):
                ins = mm3(bank(4 + t // 2)[:, (t % 2) * D:(t % 2 + 1) * D], xs(t), ws(W1H, W1L, G1, D), t % 2 == 0, True)
                if t % 2:
                    ins.then_inc(og_mm, 1)

            def spread(v):
                s = v % 2
                if v >= 2:
                    pe.wait_ge(s_done, v - 1)
                for hf in range(2):
                    for i, part in enumerate((VTH, VTL)):
                        ins = pe.matmul(bank(2 * s + hf), rep1[:, v % 8, :], part[:, v // 8, hf * BANK:(hf + 1) * BANK],
                                        start=(i == 0), stop=(i == 1))
                ins.then_inc(vr_mm, 1)

            def gather_o(v):
                pe.wait_ge(qs_done, v + 1)
                q = 32 * ((v % 8) // 2)
                for hf in range(2):
                    ins = pe.matmul(bank(4 + 2 * (v // 8) + hf)[q:q + 32, :], block2[:, v % 2, :],
                                    QS[:, v % 2, hf * BANK:(hf + 1) * BANK], start=(v % 2 == 0), stop=(v % 2 == 1))
                ins.then_inc(qs_used, 1)

            pe.wait_ge(vt_lo, 4)
            spread(0)
            spread(1)
            pe.wait_ge(og_pre, NT // 2)
            for v in range(DV1):
                if v + 2 < DV1:
                    spread(v + 2)
                gather_o(v)
            pe.wait_ge(ot_evac, 4)
            for p in range(NT // 2):
                for t in range(2):
                    for k in range(KD):
                        ins = pe.transpose(bank(p)[:, (2 * t + k) * P:(2 * t + k + 1) * P],
                                           OT[:, k, (2 * p + t) * P:(2 * p + t + 1) * P], ident[:])
                ins.then_inc(o_mm, 1)
            transposes(3, HC, gated, NT)
            project(3, WO1H, WO1L)
            transposes(4, XB, x_ready, 2 * NT)
            router(1, 4, E0, E1)
            moe_pe(MOES[1])
            release_y(3)


def kernel(**inputs):
    import numpy as np
    import concourse.bacc as bacc
    from concourse.bass_utils import run_bass_kernel_spmd

    g = {k: np.asarray(v) for k, v in inputs.items()}
    B, S, D = g["L0_attn_x"].shape
    P = 128
    NH0, NH1 = 8, 16
    DV1, DK1 = D // NH1, P // NH1
    f32 = np.float32
    eye = np.eye(P, dtype=f32)
    rows = np.arange(P)

    odd = (rows // (P // NH0)) % 2
    rep = (rows % 32) // NH0
    sc = f32((P // NH0) ** -0.5)
    head_masks = np.stack([(odd == 0) * sc, (odd == 1) * sc, rep == 0, rep == 1], 1).astype(f32)
    sel0 = np.zeros((P, B * NH0), f32)
    for b in range(B):
        for h in range(NH0):
            sel0[32 * b + h, b * NH0 + h] = 1
            sel0[32 * b + NH0 + h, b * NH0 + h] = 1
    rep1 = np.zeros((P, 8, P), f32)
    for v in range(8):
        for h in range(NH1):
            rep1[v * NH1 + h, v, h * DK1:(h + 1) * DK1] = 1
    import ml_dtypes
    bf = ml_dtypes.bfloat16
    futb = np.where(rows[:, None] > rows[None, :], -1e30, 0.0).astype(bf)

    block2 = np.zeros((P, 2, 2 * NH1), f32)
    for i in range(2):
        block2[rows, i, i * NH1 + rows // DK1] = 1

    def rowsof(v):
        return np.ascontiguousarray(np.broadcast_to(v, (P,) + v.shape))
    wv1 = g["L1_attn_Wv"].reshape(NH1, DV1, D).transpose(1, 0, 2).reshape(D, D)
    arrays = {
        "x": g["L0_attn_x"],
        "xT": g["L0_attn_x"].reshape(B * S, D).T,
        "w0T": np.concatenate([g["L0_attn_Wv"], g["L0_attn_Wog"], g["L0_attn_Wq"], g["L0_attn_Wk"],
                               np.tile(g["L0_attn_Wig"], (4, 1)), np.tile(g["L0_attn_Wfg"], (4, 1))]).T,
        "wo0T": g["L0_attn_Wout"].T,
        "w1T": np.concatenate([wv1, g["L1_attn_Wg"], g["L1_attn_Wq"], g["L1_attn_Wk"],
                               np.tile(g["L1_attn_Wkg1"], (8, 1))]).T,
        "wo1T": g["L1_attn_Wo"].T,
        "wrT": np.concatenate([g["L0_ffn_router_w"], g["L1_ffn_gate_weight"]]).T,
        "gate_b": np.stack([np.tile(g["L0_attn_big"], P // NH0), np.tile(g["L0_attn_bfg"], P // NH0)], 1),
        "gamma": g["L0_attn_gamma"].reshape(D // P, P).T,
        "bias_r0": rowsof(g["L0_ffn_expert_bias"]),
        "alpha": rowsof(g["L1_ffn_layer_alpha"].reshape(1)),
        "bkg": g["L1_attn_bkg2"].reshape(P, 1),
        "bg": rowsof(g["L1_attn_bg"]),
        "wkg2T": g["L1_attn_Wkg2"].T,
        "gateup0": np.concatenate([g["L0_ffn_gate_proj"], g["L0_ffn_up_proj"]], 2),
        "down0": g["L0_ffn_down_proj"],
        "gateup1": g["L1_ffn_gate_up_proj"].reshape(16, 2, 2, 96, D).transpose(0, 4, 2, 1, 3).reshape(16, D, 384),
        "down1": g["L1_ffn_down_proj"].transpose(0, 2, 1).reshape(16, 192, D),
        "ident": eye,
        "identb": eye.astype(bf),
        "futb": futb,
        "head_masks": head_masks,
        "sel0": sel0,
        "rep1": rep1,
        "iota_e": rowsof(np.arange(32, dtype=f32)),
        "first8": rowsof(np.arange(8, 0, -1).astype(f32)),
        "block2": block2,
    }
    nc = bacc.Bacc("TRN2", target_bir_lowering=False, num_devices=1)
    feeds, aps = {}, {}
    for name, v in arrays.items():
        v = np.ascontiguousarray(v)
        feeds[f"in_{name}"] = v
        aps[name] = nc.dram_tensor(f"in_{name}", v.shape, mybir.dt.from_np(v.dtype), kind="ExternalInput").ap()
    out = nc.dram_tensor("out_y", (B, S, D), F32, kind="ExternalOutput").ap()
    build_kernel(nc, aps, out)
    r = run_bass_kernel_spmd(nc, [feeds], core_ids=[0])
    return r.results[0]["out_y"]
```

```python
import itertools
from contextlib import ExitStack

import concourse.bass as bass
from concourse import mybir

ALU = mybir.AluOpType
ACT = mybir.ActivationFunctionType
F32 = mybir.dt.float32
F32R = mybir.dt.float32r
BF16 = mybir.dt.bfloat16
U32 = mybir.dt.uint32
AX_X = mybir.AxisListType.X

P = 128
BANK = 512


def build_kernel(nc, a, out):
    B, S, D = a["x"].shape
    T = B * S
    NT = T // P
    KD = D // P
    TB = S // P
    NH0 = 8
    DV0 = D // NH0
    DQ0 = P // NH0
    CAP = 15.0
    EPS_M = 1e-6
    NH1 = 16
    DV1 = D // NH1
    DK1 = P // NH1
    GATE_NORM = 16.0
    KSCALE = 128.0 ** -0.5
    EPS_G = 1e-5
    EPS_LN = 1e-5
    TAU = 0.05
    E0, I0 = a["gateup0"].shape[0], a["gateup0"].shape[2] // 2
    PAIR = 2
    E1, I1 = a["gateup1"].shape[0] * PAIR, a["gateup1"].shape[2] // 2 // PAIR

    V0, O0, Q0, K0, IG0, FG0 = 0, D, 2 * D, 2 * D + P, 2 * D + 2 * P, 2 * D + 2 * P + 32
    W0C = FG0 + 32
    V1, G1, Q1, K1, Z1 = 0, D, 2 * D, 2 * D + P, 2 * D + 2 * P
    W1C = Z1 + P

    with ExitStack() as ctx:
        def sb(name, shape, dt=F32):
            return ctx.enter_context(nc.sbuf_tensor(name, shape, dt))

        def sem(name):
            return ctx.enter_context(nc.semaphore(name))

        PS = ctx.enter_context(nc.psum_tensor("PS", [P, 8, BANK], F32))

        def bank(n):
            return PS[:, n, :]

        ident = sb("ident", [P, P])
        identb = sb("identb", [P, P], BF16)
        futb = sb("futb", [P, P], BF16)
        zb = sb("zb", [P, BANK], BF16)
        head_masks = sb("head_masks", [P, 4])
        gate_b = sb("gate_b", [P, 2])
        gate_bs = sb("gate_bs", [P, 2])
        gamma = sb("gamma", [P, KD])
        bias_r0 = sb("bias_r0", [P, E0])
        alpha = sb("alpha", [P, 1])
        bkg = sb("bkg", [P, 1])
        bg = sb("bg", [1, D])
        wkg2 = sb("wkg2", [16, P])
        iota_e = sb("iota_e", [P, E1])
        first8 = sb("first8", [P, 8])
        wr_sum = sb("wr_sum", [P, E0 + E1])
        block2 = sb("block2", [P, 2, 2 * NH1])
        sel0 = sb("sel0", [P, B * NH0], F32R)
        rep1 = sb("rep1", [P, 8, P], F32R)

        XA = sb("XA", [P, NT, D])
        XB = sb("XB", [P, NT, D])
        XH = sb("XH", [P, KD, T], F32R)
        XL = sb("XL", [P, KD, T], F32R)
        HTH, HTL = XH, XL
        OGATE = sb("OGATE", [P, NT, D])
        HC = sb("HC", [P, NT, D])
        QT = sb("QT", [P, T])
        LT = QT[0:2 * (E0 + E1), :]

        VXC = NT * NH0 * (DV0 + 1)
        FA_WORDS = KD * T + KD * W0C + VXC + DV0 + 2 * T + KD * D + 2 * BANK
        FA = sb("FA", [P, FA_WORDS])
        at = 0

        def take(n):
            nonlocal at
            at += n
            return FA[:, at - n:at]
        XT = take(KD * T).rearrange("p (k t) -> p k t", k=KD)
        W0T = take(KD * W0C).rearrange("p (k n) -> p k n", k=KD)
        VXF = take(VXC + DV0)
        VX = VXF[:, 0:VXC].rearrange("p (t h v) -> p t h v", t=NT, h=NH0)
        KTE = take(T)
        KTO = take(T)
        AOT = take(2 * BANK).rearrange("p (n c) -> p n c", n=2)
        WO0T = take(KD * D).rearrange("p (k n) -> p k n", k=KD)
        at = 0
        DEC = take(T)
        KT = take(T)
        STATE = take(2 * T).rearrange("p (s t) -> p s t", s=2)
        QS = take(2 * T).rearrange("p (s t) -> p s t", s=2)
        OT = take(KD * T).rearrange("p (k t) -> p k t", k=KD)
        KG, KGL = OT[:, 0, :], OT[:, 1, :]
        RA = sb("RA", [P, max(2 * KD * W0C, 2 * KD * T)], F32R)
        W0H = RA[:, 0:KD * W0C].rearrange("p (k n) -> p k n", k=KD)
        W0L = RA[:, KD * W0C:2 * KD * W0C].rearrange("p (k n) -> p k n", k=KD)
        VTH = RA[:, 0:KD * T].rearrange("p (k t) -> p k t", k=KD)
        VTL = RA[:, KD * T:2 * KD * T].rearrange("p (k t) -> p k t", k=KD)
        WO0H = sb("WO0H", [P, KD, D], F32R)
        WO0L = sb("WO0L", [P, KD, D], F32R)
        W1T = XB[:, :, :].rearrange("p t d -> p (t d)")[:, 0:KD * W1C].rearrange("p (k n) -> p k n", k=KD)
        W1H = sb("W1H", [P, KD, W1C], F32R)
        W1L = sb("W1L", [P, KD, W1C], F32R)
        WO1T = HC[:, 0:KD, :]
        WO1H = sb("WO1H", [P, KD, D], F32R)
        WO1L = sb("WO1L", [P, KD, D], F32R)
        WRT = sb("WRT", [P, KD, E0 + E1])
        WRC = E0 + E1
        WRS = sb("WRS", [P, KD, 2 * WRC], F32R)

        GI = sb("GI", [P, S])
        GF = sb("GF", [P, S])
        NL = sb("NL", [P, S])
        AS = sb("AS", [P, S])
        MX = sb("MX", [P, S])
        NMH = sb("NMH", [P, S], F32R)
        NML = sb("NML", [P, S])
        NMD = sb("NMD", [P, 3 * P], F32R)
        BGH, BGL = NMH[0:1, 0:D], NMD[0:1, 0:D]
        ATF = sb("ATF", [P, 2, TB, P])
        EW = sb("EW", [P, 2, 3 * P])
        WW = sb("WW", [P, 3, 3 * P])

        st = sb("st", [P, NT, 6])
        mv = sb("mv", [P, NT, 2])
        rstd = sb("rstd", [P, NT])
        rv = sb("rv", [P, NT])
        nb = sb("nb", [P, NT])
        hn = sb("hn", [P, NT, 16])
        hr = sb("hr", [P, NT, 16])
        hs = sb("hs", [P, NT, 16])
        SQ = sb("SQ", [P, 4, D])
        act_scratch = sb("act_scratch", [P, 16])
        den = sb("den", [P, 3, NH0])
        LG = sb("LG", [P, NT, E1])
        PR = sb("PR", [P, NT, E1])
        EQ = sb("EQ", [P, NT, E1])
        rsum = sb("rsum", [P, NT])
        rbest = sb("rbest", [P, NT])
        top = sb("top", [P, NT, 8])
        tix = sb("tix", [P, NT, 8], U32)
        tif = sb("tif", [P, NT, 8])
        t1 = sb("t1", [P, NT, 8])
        t2 = sb("t2", [P, NT, 8])
        t3 = sb("t3", [P, NT, 8])
        CW = sb("CW", [P, NT, E1])

        MG = KD * 2 * I0
        MD = 2 * D
        EG = sb("EG", [P, 2, MG])
        ED = sb("ED", [P, 2, MD])
        EGH = sb("EGH", [P, 2, MG], F32R)
        EGL = sb("EGL", [P, 2, MG], F32R)
        EDH = sb("EDH", [P, 2, MD], F32R)
        EDL = sb("EDL", [P, 2, MD], F32R)
        round_mark = sb("round_mark", [P, 3])
        SIL = sb("SIL", [P, 2, 256])
        HH = sb("HH", [P, 2, 256])
        EHH = sb("EHH", [P, 2, 256], F32R)
        EHL = sb("EHL", [P, 2, 256], F32R)

        ld_const = sem("ld_const")
        ld_sel = sem("ld_sel")
        ld_x = sem("ld_x")
        ld_xt = sem("ld_xt")
        ld_w0 = sem("ld_w0")
        ld_wo0 = sem("ld_wo0")
        ld_w1 = sem("ld_w1")
        ld_wo1 = sem("ld_wo1")
        ld_wr = sem("ld_wr")
        ld_exp = [sem("ld_exp0"), sem("ld_exp1")]
        stored = sem("stored")
        zb_set = sem("zb_set")
        ones_set = sem("ones_set")
        xt_hi = sem("xt_hi")
        w0_hi = sem("w0_hi")
        w0v_hi = sem("w0v_hi")
        x0_split = sem("x0_split")
        pool_chain = sem("pool_chain")
        v_centred = sem("v_centred")
        ao_evac = sem("ao_evac")
        ao_tokens = sem("ao_tokens")
        hc_ready = sem("hc_ready")
        sq_done = sem("sq_done")
        sq_read = sem("sq_read")
        og_ready = sem("og_ready")
        ot_evac = sem("ot_evac")
        w_split = sem("w_split")
        gate_mm = sem("gate_mm")
        gate_bias = sem("gate_bias")
        qk_mm = sem("qk_mm")
        tanh_done = sem("tanh_done")
        soft_done = sem("soft_done")
        act_chain = sem("act_chain")
        dve_chain = sem("dve_chain")
        nl_ready = sem("nl_ready")
        floor_ready = sem("floor_ready")
        a_ready = sem("a_ready")
        nm_ready = sem("nm_ready")
        gt_mm = sem("gt_mm")
        at_ready = sem("at_ready")
        q_ready = sem("q_ready")
        k_ready = sem("k_ready")
        vo_mm = sem("vo_mm")
        vo_done = sem("vo_done")
        r_ready = sem("r_ready")
        qk_ready = sem("qk_ready")
        e_ready = sem("e_ready")
        w_ready = sem("w_ready")
        av_done = sem("av_done")
        var_ready = sem("var_ready")
        rstd_ready = sem("rstd_ready")
        gated = sem("gated")
        tp_done = sem("tp_done")
        hi_done = sem("hi_done")
        lo_done = sem("lo_done")
        y_done = sem("y_done")
        ln_var = sem("ln_var")
        ln_rstd = sem("ln_rstd")
        ln_bias = sem("ln_bias")
        x_dve = sem("x_dve")
        x_act = sem("x_act")
        lt_read = sem("lt_read")
        rt_mm = sem("rt_mm")
        rt_max = sem("rt_max")
        rt_exp = sem("rt_exp")
        weights_ready = sem("weights_ready")
        exp_split = sem("exp_split")
        gu_done = sem("gu_done")
        sil_done = sem("sil_done")
        h_ready = sem("h_ready")
        ht_done = sem("ht_done")
        hhi_done = sem("hhi_done")
        hlo_done = sem("hlo_done")
        dn_done = sem("dn_done")
        g_mm = sem("g_mm")
        g_read = sem("g_read")
        kg_abs = sem("kg_abs")
        kg_ln = sem("kg_ln")
        kg_log_sigmoid = sem("kg_log_sigmoid")
        dec_ready = sem("dec_ready")
        z_ready = sem("z_ready")
        vt_mm = sem("vt_mm")
        vt_hi = sem("vt_hi")
        vt_lo = sem("vt_lo")
        og_mm = sem("og_mm")
        og_silu = sem("og_silu")
        vr_mm = sem("vr_mm")
        d1_done = sem("d1_done")
        s_done = sem("s_done")
        qs_done = sem("qs_done")
        qs_last = sem("qs_last")
        o_mm = sem("o_mm")
        qs_used = sem("qs_used")

        class Counter:
            def __init__(self, eng, s):
                self.eng, self.s, self.n = eng, s, 0

            def link(self, ins):
                ins.then_inc(self.s, 1)
                self.n += 1
                self.eng.wait_ge(self.s, self.n)

            def mark(self, ins):
                ins.then_inc(self.s, 1)
                self.n += 1
                return self.n

            def need(self, n):
                self.eng.wait_ge(self.s, n)

        def col(ap, n):
            return ap.unsqueeze(2).broadcast_to([P, ap.shape[1], n])

        def wait_past(eng, s, count):
            if not isinstance(count, int) or count > 0:
                eng.wait_ge(s, count)

        def wait_x(eng, n, t):
            eng.wait_ge(x_act if t // 2 % 2 else x_dve, n * (NT // 2) + 2 * (t // 4) + t % 2 + 1)

        class Moe:
            def __init__(self, n, E, I, pair, top):
                self.top = top
                self.n, self.E, self.I, self.pair = n, E // pair, I * pair, pair
                self.units = NT
                self.total = self.E * self.units
                self.body = 2 * self.units
                self.IC = 2
                self.IP = self.I // self.IC
                self.gcols = KD * 2 * self.I
                self.dcols = self.IC * D
        MOES = [Moe(0, E0, I0, 1, 4), Moe(1, E1, I1, PAIR, 8)]
        UB = [0, MOES[0].total, MOES[0].total + MOES[1].total]
        EB = [0, MOES[0].E, MOES[0].E + MOES[1].E]

        xd = a["x"].rearrange("b (n p) d -> p (b n) d", p=P)
        outd = out.rearrange("b (n p) d -> p (b n) d", p=P)

        def run_units(eng, m, now, later, between=None):
            base = UB[m.n]

            def step(pos, u, have_past):
                now(pos, u)
                if between is not None and not have_past:
                    between(2 * pos)
                for fn, lag in later:
                    if have_past or pos >= lag:
                        fn((pos - lag) % m.body, u - lag)
                if between is not None and not have_past:
                    between(2 * pos + 1)
            for pos in range(m.body):
                step(pos, base + pos, False)
            with eng.Fori(1, m.total // m.body) as i:
                for pos in range(m.body):
                    step(pos, i * m.body + (base + pos), True)
            for pos in range(max(lag for _, lag in later)):
                for fn, lag in later:
                    if pos < lag:
                        fn((pos - lag) % m.body, base + m.total + pos - lag)

        LATE_VALUES_AT = 1
        FLOOR_AT, EVAC_AT, TOKENS_AT = 2, 1, 4
        HEADS_AT, SQUARE_AT, SUMS_AT = (4, 5), (5, 6), (6, 7)

        block = ctx.enter_context(nc.Block())

        @block.sync
        def _(sp):
            sp.dma_start(XT, a["xT"].rearrange("(k p) t -> p k t", p=P)).then_inc(ld_xt, 16)
            sp.dma_start(W0T, a["w0T"].rearrange("(k p) n -> p k n", p=P)).then_inc(ld_w0, 16)
            consts = [(ident[:], a["ident"]), (identb[:], a["identb"]), (futb[:], a["futb"]),
                      (head_masks[:], a["head_masks"]), (gate_b[:], a["gate_b"]), (gamma[:], a["gamma"]),
                      (bias_r0[:], a["bias_r0"]), (alpha[:], a["alpha"]), (bkg[:], a["bkg"]), (bg[:], a["bg"]),
                      (wkg2[:], a["wkg2T"]), (iota_e[:], a["iota_e"]), (first8[:], a["first8"]),
                      (block2[:], a["block2"]), (wr_sum[:], a["wr_sum"])]
            for dst, src in consts:
                sp.dma_start(dst, src).then_inc(ld_const, 16)
            sp.dma_start(WO0T, a["wo0T"].rearrange("(k p) n -> p k n", p=P)).then_inc(ld_wo0, 16)
            sp.dma_start(WRT[:], a["wrT"].rearrange("(k p) n -> p k n", p=P)).then_inc(ld_wr, 16)
            sp.dma_start(W1T, a["w1T"].rearrange("(k p) n -> p k n", p=P)).then_inc(ld_w1, 16)
            sp.dma_start(WO1T, a["wo1T"].rearrange("(k p) n -> p k n", p=P)).then_inc(ld_wo1, 16)
            sp.dma_start(XA[:], xd).then_inc(ld_x, 16)

            def load_expert(m, e, par, free_at):
                if free_at is not None:
                    sp.wait_ge(exp_split, free_at)
                gate_up, src = (a["gateup0"], a["down0"]) if m.n == 0 else (a["gateup1"], a["down1"])
                sp.dma_start(EG[:, par, 0:m.gcols].rearrange("p (k c) -> p k c", k=KD),
                             gate_up[bass.ds(e, 1)].rearrange("o (k p) i -> p (o k) i", p=P)
                             ).then_inc(ld_exp[par], 16)
                sp.dma_start(ED[0:m.IP, par, 0:m.dcols].rearrange("p (c d) -> p c d", d=D),
                             src[bass.ds(e, 1)].rearrange("o (c p) d -> p (o c) d", p=m.IP)
                             ).then_inc(ld_exp[par], 16)

            for m in MOES:
                for par in range(2):
                    base = EB[m.n] + par
                    load_expert(m, par, par, base - 1 if base >= 2 else None)
                with sp.Fori(1, m.E // 2) as i:
                    for par in range(2):
                        load_expert(m, i * 2 + par, par, i * 2 + (EB[m.n] + par - 1))
            for t in range(NT):
                wait_x(sp, 3, t)
                sp.dma_start(outd[:, t, :], XA[:, t, :]).then_inc(stored, 16)
            sp.wait_ge(stored, 16 * NT)

        @block.gpsimd
        def _(pool):
            ch = Counter(pool, pool_chain)
            pool.dma_start(sel0[:], a["sel0"]).then_inc(ld_sel, 16)
            pool.dma_start(rep1[:], a["rep1"]).then_inc(ld_sel, 16)

            def split(hi, lo, src):
                ch.link(pool.tensor_scalar(hi, src, 1.0, 0.0, ALU.mult, ALU.add))
                return pool.tensor_tensor(lo, src, hi.bitcast(F32), ALU.subtract)

            pool.wait_ge(ld_w0, 16)
            pool.tensor_scalar(W0H[:, :, Q0:Q0 + 2 * P], W0T[:, :, Q0:Q0 + 2 * P], 1.0, 0.0, ALU.mult, ALU.add
                               ).then_inc(w0_hi, 1)
            pool.tensor_scalar(W0H[:, :, O0:O0 + D], W0T[:, :, O0:O0 + D], 1.0, 0.0, ALU.mult, ALU.add
                               ).then_inc(w0_hi, 1)
            ch.link(pool.memset(round_mark[:], 0.0))
            pool.wait_ge(ld_const, 16 * 15)
            pool.wait_ge(ld_wo0, 16)
            for k in range(KD):
                ch.link(pool.tensor_scalar(WO0T[:, k, :], WO0T[:, k, :], gamma[:, k:k + 1], 0.0, ALU.mult, ALU.add))
            split(WO0H[:], WO0L[:], WO0T).then_inc(w_split, 1)
            pool.wait_ge(ld_wr, 16)
            split(WRS[:, :, 0:WRC], WRS[:, :, WRC:2 * WRC], WRT[:]).then_inc(w_split, 1)
            pool.wait_ge(v_centred, 2)
            split(W1H[:], W1L[:], W1T).then_inc(w_split, 1)
            pool.wait_ge(ld_wo1, 16)
            split(WO1H[:], WO1L[:], WO1T).then_inc(w_split, 1)

            for t in range(NT):
                pool.wait_ge(hc_ready, t + 1)
                pool.tensor_tensor(OGATE[:, t, :], OGATE[:, t, :], HC[:, t, :], ALU.mult).then_inc(og_ready, 1)

            def split_expert(m, par, loads, free_at, ordinal):
                pool.wait_ge(ld_exp[par], loads)
                if free_at is not None:
                    pool.wait_ge(dn_done, free_at)
                pool.tensor_tensor(round_mark[:, 0:1], round_mark[:, 1:2], round_mark[:, 2:3], ALU.add)
                gh, gl = EGH[:, par, 0:m.gcols], EGL[:, par, 0:m.gcols]
                dh, dl = EDH[0:m.IP, par, 0:m.dcols], EDL[0:m.IP, par, 0:m.dcols]
                pool.tensor_scalar(gh, EG[:, par, 0:m.gcols], 1.0, 0.0, ALU.mult, ALU.add).then_inc(pool_chain, 1)
                pool.tensor_scalar(dh, ED[0:m.IP, par, 0:m.dcols], 1.0, 0.0, ALU.mult, ALU.add).then_inc(pool_chain, 1)
                pool.wait_ge(pool_chain, ordinal * 2 + (chained + 2))
                pool.tensor_tensor(gl, EG[:, par, 0:m.gcols], gh.bitcast(F32), ALU.subtract)
                pool.tensor_tensor(dl, ED[0:m.IP, par, 0:m.dcols], dh.bitcast(F32), ALU.subtract
                                   ).then_inc(exp_split, 1)

            split(BGH, BGL, bg[:]).then_inc(w_split, 1)
            chained = ch.n
            per0 = per1 = 16 * 2
            m = MOES[0]
            for e in range(2):
                split_expert(m, e % 2, per0, None, e)
            with pool.Fori(1, m.E // 2) as i:
                for par in range(2):
                    split_expert(m, par, i * per0 + per0, i * m.body + (par + 1) * m.units - m.body, i * 2 + par)
            m = MOES[1]
            had = per0 * (EB[1] // 2)
            for e in range(2):
                split_expert(m, e % 2, had + per1, UB[1] - (1 - e) * MOES[0].units, EB[1] + e)
            pool.wait_ge(q_ready, 4)
            for v in range(DV1):
                pool.wait_ge(s_done, v + 1)
                if v >= 2:
                    pool.wait_ge(qs_used, v - 1)
                c = slice(BANK if v == DV1 - 1 else 0, T)
                pool.tensor_tensor(QS[:, v % 2, c], STATE[:, v % 2, c], QT[:, c], ALU.mult).then_inc(qs_done, 1)
            with pool.Fori(1, m.E // 2) as i:
                for par in range(2):
                    split_expert(m, par, i * per1 + (had + per1),
                                 i * m.body + (UB[1] + (par + 1) * m.units - m.body), i * 2 + (EB[1] + par))

        @block.scalar
        def _(act):
            ch = Counter(act, act_chain)

            warmed = itertools.count()

            def warm(func):
                c = next(warmed)
                act.activation(act_scratch[:, c:c + 1], ident[:, 0:1], func)

            act.wait_ge(ld_xt, 16)
            for k in range(KD):
                act.activation(XH[:, k, :], XT[:, k, :], ACT.Copy).then_inc(xt_hi, 1)
            act.wait_ge(v_centred, 1)
            act.activation(W0H[:, :, V0:V0 + D], W0T[:, :, V0:V0 + D], ACT.Copy).then_inc(w0v_hi, 1)
            act.wait_ge(gate_bias, 1)
            act.wait_ge(gate_mm, 1)
            act.activation(GI[:], bank(0)[:, 0:S], ACT.Tanh, bias=gate_bs[:, 0:1], scale=1.0 / CAP).then_inc(tanh_done, 1)
            ch.link(act.activation(GF[:], bank(1)[:, 0:S], ACT.Tanh, bias=gate_bs[:, 1:2], scale=1.0 / CAP))
            ch.link(act.activation(GF[:], GF[:], ACT.Exp, scale=-CAP))
            act.activation(GF[:], GF[:], ACT.Ln, bias=1.0).then_inc(soft_done, 1)
            act.wait_ge(qk_mm, 2)
            for hf in range(2):
                act.activation(QT[:, hf * BANK:(hf + 1) * BANK], bank(2 + hf), ACT.Copy).then_inc(q_ready, 1)
            act.wait_ge(ones_set, 1)
            for t in range(NT):
                act.wait_ge(vo_mm, t + 1)
                act.activation(VX[:, t, :, 0:DV0], bank(6 + t % 2)[:, 0:D].rearrange("p (h v) -> p h v", h=NH0), ACT.Copy)
                act.activation(OGATE[:, t, :], bank(6 + t % 2)[:, D:2 * D], ACT.Sigmoid).then_inc(vo_done, 1)
            act.wait_ge(nl_ready, 1)
            act.activation(NL[:], NL[:], ACT.Exp).then_inc(floor_ready, 1)
            act.wait_ge(at_ready, 1)

            def square(t):
                act.wait_ge(hc_ready, t + 1)
                if t >= 4:
                    act.wait_ge(sq_read, t - 3)
                act.activation(SQ[:, t % 4, :], HC[:, t, :], ACT.Square).then_inc(sq_done, 1)

            for u in range((B + 1) * NH0):
                b, h = u // NH0, u % NH0
                if b < B:
                    act.wait_ge(r_ready, u + 1)
                    if u >= 2:
                        act.wait_ge(w_ready, u - 1)
                    c = 32 * b + h
                    act.activation(EW[:, u % 2, 0:S], bank(u % 2)[:, 0:S], ACT.Exp, bias=ATF[:, 0, 0, c:c + 1])
                    act.activation(EW[:, u % 2, S:S + P], bank(u % 2)[:, S:S + P], ACT.Exp,
                                   bias=ATF[:, 0, 1, c:c + 1]).then_inc(e_ready, 1)
                if b >= 1 and h == EVAC_AT:
                    act.wait_ge(av_done, b * NH0)
                    if b >= 2:
                        act.wait_ge(ao_tokens, (b - 1) * TB)
                    act.activation(AOT[:, 0, :], bank(4), ACT.Copy).then_inc(ao_evac, 1)
                if b >= 1 and h in SQUARE_AT:
                    square((b - 1) * TB + SQUARE_AT.index(h))

            def head_rstd(n, nh):
                warm(ACT.Sqrt)
                act.wait_ge(var_ready, n + 1)
                act.activation(hr[:, :, 0:nh], hr[:, :, 0:nh], ACT.Sqrt).then_inc(rstd_ready, 1)

            def hi_parts(n, dst):
                for p in range(NT // 2):
                    act.wait_ge(tp_done, n * (NT // 2) + p + 1)
                    act.activation(dst[:, :, p * 2 * P:(p + 1) * 2 * P].rearrange("p k (t c) -> p t k c", t=2),
                                   bank(p).rearrange("p (t k c) -> p t k c", t=2, k=KD), ACT.Copy).then_inc(hi_done, 1)

            def layernorm(n, dst):
                warm(ACT.Sqrt)
                act.wait_ge(ln_var, n + 1)
                act.activation(rstd[:], rv[:], ACT.Sqrt).then_inc(ln_rstd, 1)
                act.wait_ge(ln_bias, n + 1)
                for t in range(NT):
                    if t // 2 % 2:
                        act.activation(dst[:, t, :], bank(4 + t // 2)[:, (t % 2) * D:(t % 2 + 1) * D], ACT.Identity,
                                       bias=nb[:, t:t + 1], scale=rstd[:, t:t + 1]).then_inc(x_act, 1)
                warm(ACT.Exp)

            def evacuate_logits(n):
                act.wait_ge(rt_mm, 3 * n + 1)
                act.activation(LT[:, 0:BANK], bank(0)[0:2 * WRC, :], ACT.Copy).then_inc(lt_read, 1)

            def router_exp(n, E):
                act.wait_ge(rt_max, n + 1)
                act.activation(PR[:, :, 0:E], LG[:, :, 0:E], ACT.Exp).then_inc(rt_exp, 1)
                warm(ACT.Silu)

            def moe_act(m):
                IP, I = m.IP, m.I

                def silu(pos, u):
                    s = pos % 2
                    act.wait_ge(gu_done, u + 1)
                    wait_past(act, h_ready, u - 1)
                    act.activation(SIL[:, s, 0:I], bank(s)[:, 0:I], ACT.Silu).then_inc(sil_done, 1)

                def hi(pos, u):
                    s = pos % 2
                    act.wait_ge(ht_done, u + 1)
                    wait_past(act, dn_done, u - 1)
                    act.activation(EHH[0:IP, s, :], bank(2 + s)[0:IP, 0:256], ACT.Copy).then_inc(hhi_done, 1)

                run_units(act, m, silu, [(hi, 1)])

            head_rstd(0, NH0)
            hi_parts(0, HTH)
            layernorm(0, XB)
            hi_parts(1, XH)
            evacuate_logits(0)
            router_exp(0, E0)
            moe_act(MOES[0])
            layernorm(1, XA)
            hi_parts(2, XH)

            for hf in range(2):
                act.wait_ge(g_mm, hf + 1)
                act.activation(KGL[0:16, hf * BANK:(hf + 1) * BANK], bank(4 + hf)[0:16, :], ACT.Copy).then_inc(z_ready, 1)

            def value_hi(k, b0):
                for hf in range(2):
                    act.wait_ge(vt_mm, 2 * k + hf + 1)
                    act.activation(VTH[:, k, hf * BANK:(hf + 1) * BANK], bank(b0 + hf), ACT.Copy).then_inc(vt_hi, 1)

            value_hi(0, 0)
            halves = [slice(hf * BANK, (hf + 1) * BANK) for hf in range(2)]
            for hf in range(2):
                act.wait_ge(kg_abs, hf + 1)
                exps = ch.mark(act.activation(KGL[:, halves[hf]], KGL[:, halves[hf]], ACT.Exp, scale=-1.0))
            ch.need(exps)
            for hf in range(2):
                act.activation(KGL[:, halves[hf]], KGL[:, halves[hf]], ACT.Ln, bias=1.0).then_inc(kg_ln, 1)
            warm(ACT.Exp)
            for hf in range(2):
                act.wait_ge(g_mm, 5 + hf)
                act.activation(KT[:, hf * BANK:(hf + 1) * BANK], bank(2 + hf), ACT.Copy, scale=KSCALE).then_inc(k_ready, 1)
            for hf in range(2):
                act.wait_ge(kg_log_sigmoid, hf + 1)
                act.activation(DEC[:, halves[hf]], KG[:, halves[hf]], ACT.Exp, scale=1.0 / GATE_NORM
                               ).then_inc(dec_ready, 1)
            for hf in range(2):
                act.wait_ge(g_mm, 7 + hf)
                act.activation(QT[:, hf * BANK:(hf + 1) * BANK], bank(4 + hf), ACT.Copy).then_inc(q_ready, 1)
            value_hi(1, 6)
            for p in range(NT // 2):
                act.wait_ge(og_mm, p + 1)
                act.activation(OGATE[:, 2 * p:2 * p + 2, :], bank(6 + p % 2).rearrange("p (t d) -> p t d", t=2),
                               ACT.Silu).then_inc(og_silu, 1)
            for hf in range(2):
                act.wait_ge(qs_used, DV1 // 2)
                act.activation(OT[:, 0, hf * BANK:(hf + 1) * BANK], bank(4 + hf), ACT.Copy).then_inc(ot_evac, 1)
            act.wait_ge(qs_used, DV1)
            act.activation(OT[:, 1, 0:BANK], bank(6), ACT.Copy).then_inc(ot_evac, 1)
            for p in range(NT // 2):
                act.wait_ge(o_mm, p + 1)
                if 2 * p >= 4:
                    act.wait_ge(sq_read, NT + 2 * p - 2)
                o = bank(p).rearrange("p (t v h) -> p t h v", t=2, v=DV1)
                for t in range(2):
                    act.activation(SQ[:, (2 * p + t) % 4, :].rearrange("p (h v) -> p h v", h=NH1), o[:, t],
                                   ACT.Square).then_inc(sq_done, 1)
            head_rstd(1, NH1)
            hi_parts(3, HTH)
            layernorm(2, XB)
            hi_parts(4, XH)
            evacuate_logits(1)
            router_exp(1, E1)
            moe_act(MOES[1])
            layernorm(3, XA)

        @block.vector
        def _(dve):
            ch = Counter(dve, dve_chain)
            dve.memset(zb[:], 0.0).then_inc(zb_set, 1)
            dve.wait_ge(ld_xt, 16)
            dve.wait_ge(ld_w0, 16)
            dve.memset(VX[:, :, :, DV0:DV0 + 1], 1.0)
            dve.memset(VXF[:, VXC:VXC + DV0], 1.0).then_inc(ones_set, 1)
            dve.wait_ge(ld_const, 16 * 15)
            dve.tensor_scalar(gate_bs[:], gate_b[:], 1.0 / CAP, None, ALU.mult).then_inc(gate_bias, 1)
            def centre_values(view, shape):
                nh = shape[1]
                acc = hn[:, 0:KD, 0:nh]
                for k in range(KD):
                    ins = dve.tensor_reduce(hn[:, k, 0:nh], view(k), AX_X, ALU.add)
                ch.link(ins)
                ch.link(dve.tensor_scalar(acc, acc, -1.0 / (D // nh), None, ALU.mult))
                for k in range(KD):
                    ins = dve.tensor_tensor(view(k), view(k), col(hn[:, k, 0:nh], D // nh), ALU.add)
                return ins
            centre_values(lambda k: W0T[:, k, V0:V0 + D].rearrange("p (h v) -> p h v", h=NH0), (P, NH0)
                          ).then_inc(v_centred, 1)
            for k in range(KD):
                dve.wait_ge(xt_hi, k + 1)
                dve.tensor_tensor(XL[:, k, :], XT[:, k, :], XH[:, k, :].bitcast(F32), ALU.subtract)
            for c0, cn, done, i in ((Q0, 2 * P, w0_hi, 1), (O0, D, w0_hi, 2), (V0, D, w0v_hi, 1)):
                dve.wait_ge(done, i)
                dve.tensor_tensor(W0L[:, :, c0:c0 + cn], W0T[:, :, c0:c0 + cn],
                                  W0H[:, :, c0:c0 + cn].bitcast(F32), ALU.subtract).then_inc(x0_split, 1)
            dve.wait_ge(qk_mm, 4)
            for hf in range(2):
                dve.tensor_scalar(KTE[:, hf * BANK:(hf + 1) * BANK], bank(4 + hf), head_masks[:, 0:1], None, ALU.mult)
                dve.tensor_scalar(KTO[:, hf * BANK:(hf + 1) * BANK], bank(4 + hf), head_masks[:, 1:2], None,
                                  ALU.mult).then_inc(k_ready, 1)
            dve.wait_ge(soft_done, 1)
            ch.link(dve.tensor_tensor_scan(NL[:], GF[:], GF[:], 0.0, ALU.add, ALU.max))
            dve.wait_ge(tanh_done, 1)
            ch.link(dve.scalar_tensor_tensor(out=AS[:], in0=GI[:], scalar=CAP, in1=NL[:], op0=ALU.mult, op1=ALU.add))
            ch.link(dve.tensor_tensor_scan(MX[:], AS[:], AS[:], 0.0, ALU.max, ALU.max))
            dve.tensor_tensor(NL[:], NL[:], MX[:], ALU.subtract).then_inc(nl_ready, 1)
            ch.link(dve.tensor_scalar(MX[:], MX[:], -1.0, None, ALU.mult))
            ch.link(dve.tensor_copy(NMH[:], MX[:]))
            ch.link(dve.tensor_tensor(NML[:], MX[:], NMH[:].bitcast(F32), ALU.subtract))
            ch.link(dve.tensor_scalar(NML[:], NML[:], head_masks[:, 3:4], None, ALU.mult))
            for dst, src in ((slice(0, S), slice(0, S)), (slice(S, S + P), slice(P, S))):
                dve.scalar_tensor_tensor(out=NMD[:, dst], in0=NMH[:, src].bitcast(F32), scalar=head_masks[:, 2:3],
                                         in1=NML[:, src], op0=ALU.mult, op1=ALU.add).then_inc(nm_ready, 1)
            dve.wait_ge(ld_w1, 16)
            centre_values(lambda k: W1T[:, k, V1:V1 + D].rearrange("p (v h) -> p h v", h=NH1), (P, NH1)
                          ).then_inc(v_centred, 1)
            dve.wait_ge(gt_mm, 1)
            dve.tensor_copy(ATF[:, 0].rearrange("p t c -> p (t c)"), bank(4)[:, 0:S]).then_inc(at_ready, 1)

            def mlstm_heads(t):
                b, tt = t // TB, t % TB
                ao = bank(6 + tt).rearrange("p (h v) -> p h v", h=NH0)
                qn = ao[:, :, DV0]
                if t == 0:
                    dve.wait_ge(at_ready, 2)
                    dve.wait_ge(w_split, 4)
                dve.wait_ge(ao_tokens, t + 1)
                ch.link(dve.scalar_tensor_tensor(out=den[:, 0, :], in0=qn, scalar=-1.0,
                                                 in1=ATF[:, 1, tt, 32 * b:32 * b + NH0], op0=ALU.mult, op1=ALU.max))
                ch.link(dve.tensor_tensor(den[:, 1, :], qn, den[:, 0, :], ALU.max))
                ch.link(dve.tensor_scalar(den[:, 1, :], den[:, 1, :], EPS_M, None, ALU.add))
                ch.link(dve.reciprocal(den[:, 2, :], den[:, 1, :]))
                dve.tensor_tensor(HC[:, t, :].rearrange("p (h v) -> p h v", h=NH0), ao[:, :, 0:DV0],
                                  col(den[:, 2, :], DV0), ALU.mult).then_inc(hc_ready, 1)

            def head_sums(n, t, nh):
                dve.wait_ge(sq_done, n * NT + t + 1)
                dve.tensor_reduce(hs[:, t, 0:nh], SQ[:, t % 4, :].rearrange("p (h v) -> p h v", h=nh), AX_X, ALU.add
                                  ).then_inc(sq_read, 1)

            def head_var(n, nh, eps):
                dve.wait_ge(sq_read, (n + 1) * NT)
                ch.link(dve.tensor_scalar(hs[:, :, 0:nh], hs[:, :, 0:nh], nh / D, eps, ALU.mult, ALU.add))
                dve.reciprocal(hr[:, :, 0:nh], hs[:, :, 0:nh]).then_inc(var_ready, 1)

            for u in range((B + 1) * NH0):
                b, h = u // NH0, u % NH0
                if b < B:
                    dve.wait_ge(e_ready, u + 1)
                    dve.wait_ge(qk_ready, u + 1)
                    if u >= 3:
                        dve.wait_ge(av_done, u - 2)
                    dve.tensor_tensor(WW[:, u % 3, :], EW[:, u % 2, :], bank(2 + u % 2)[:, 0:3 * P],
                                      ALU.mult).then_inc(w_ready, 1)
                if u == FLOOR_AT:
                    dve.wait_ge(gt_mm, 2)
                    dve.tensor_copy(ATF[:, 1].rearrange("p t c -> p (t c)"), bank(7)[:, 0:S]).then_inc(at_ready, 1)
                if b >= 1 and h == EVAC_AT:
                    dve.wait_ge(av_done, b * NH0)
                    if b >= 2:
                        dve.wait_ge(ao_tokens, (b - 1) * TB)
                    dve.tensor_copy(AOT[:, 1, :], bank(5)).then_inc(ao_evac, 1)
                if b >= 1 and h in HEADS_AT:
                    mlstm_heads((b - 1) * TB + HEADS_AT.index(h))
                if b >= 1 and h in SUMS_AT:
                    head_sums(0, (b - 1) * TB + SUMS_AT.index(h), NH0)
            head_var(0, NH0, EPS_M)

            def apply_rstd(n, nh):
                dve.wait_ge(rstd_ready, n + 1)
                dve.wait_ge(og_ready, (n + 1) * NT)
                for t in range(NT):
                    dve.tensor_tensor(HC[:, t, :].rearrange("p (h v) -> p h v", h=nh),
                                      OGATE[:, t, :].rearrange("p (h v) -> p h v", h=nh),
                                      col(hr[:, t, 0:nh], D // nh), ALU.mult).then_inc(gated, 1)

            def lo_parts(n, dst, hi):
                for p in range(NT // 2):
                    dve.wait_ge(hi_done, n * (NT // 2) + p + 1)
                    ap = lambda x: x[:, :, p * 2 * P:(p + 1) * 2 * P].rearrange("p k (t c) -> p t k c", t=2)
                    for t in range(2):
                        ins = dve.tensor_tensor(ap(dst)[:, t], bank(p).rearrange("p (t k c) -> p t k c", t=2, k=KD)[:, t],
                                                ap(hi).bitcast(F32)[:, t], ALU.subtract)
                    ins.then_inc(lo_done, 1)

            def layernorm(n, dst, y, count):
                for p in range(NT // 2):
                    dve.wait_ge(y, count(p))
                    for t in (2 * p, 2 * p + 1):
                        stats = ch.mark(dve.bn_stats(st[:, t, :], bank(4 + p)[:, (t % 2) * D:(t % 2 + 1) * D]))
                ch.need(stats)
                for t in range(NT):
                    ins = dve.bn_aggr(mv[:, t, :], st[:, t, :])
                ch.link(ins)
                ch.link(dve.tensor_scalar(rv[:], mv[:, :, 1], EPS_LN, None, ALU.add))
                dve.reciprocal(rv[:], rv[:]).then_inc(ln_var, 1)
                dve.wait_ge(ln_rstd, n + 1)
                dve.scalar_tensor_tensor(out=nb[:], in0=mv[:, :, 0], scalar=-1.0, in1=rstd[:], op0=ALU.mult,
                                         op1=ALU.mult).then_inc(ln_bias, 1)
                for t in range(NT):
                    if t // 2 % 2 == 0:
                        dve.tensor_scalar(dst[:, t, :], bank(4 + t // 2)[:, (t % 2) * D:(t % 2 + 1) * D],
                                          mv[:, t, 0:1], rstd[:, t:t + 1], ALU.subtract, ALU.mult).then_inc(x_dve, 1)

            def softmax(n, E, bias):
                lg, pr = LG[:, :, 0:E], PR[:, :, 0:E]
                dve.wait_ge(rt_mm, 3 * n + 2)
                dve.tensor_copy(LT[:, BANK:2 * BANK], bank(1)[0:2 * WRC, :]).then_inc(lt_read, 1)
                dve.wait_ge(rt_mm, 3 * n + 3)
                src = bank(2)[:, 0:NT * E].rearrange("p (t e) -> p t e", t=NT)
                if bias is not None:
                    ch.link(dve.tensor_tensor(lg, src, bias.unsqueeze(1).broadcast_to([P, NT, E]), ALU.add))
                    src = lg
                ch.link(dve.tensor_reduce(rsum[:], src, AX_X, ALU.max))
                dve.tensor_tensor(lg, src, col(rsum[:], E), ALU.subtract).then_inc(rt_max, 1)
                dve.wait_ge(rt_exp, n + 1)
                for t in range(NT):
                    ins = dve.max(top[:, t, :], PR[:, t, 0:E])
                largest = ch.mark(ins)
                summed = ch.mark(dve.tensor_reduce(rsum[:], pr, AX_X, ALU.add))
                ch.need(largest)
                for t in range(NT):
                    ins = dve.max_index(tix[:, t, :], top[:, t, :], PR[:, t, 0:E])
                found = ch.mark(ins)
                ch.need(summed)
                inverse = ch.mark(dve.reciprocal(rsum[:], rsum[:]))
                ch.need(found)
                dve.tensor_copy(tif[:], tix[:])
                ch.need(inverse)
                ch.link(dve.tensor_tensor(top[:], top[:], col(rsum[:], 8), ALU.mult))

            def normalise(dst, src, k, floor):
                ch.link(dve.tensor_reduce(rsum[:], src[:, :, 0:k], AX_X, ALU.add))
                if floor is not None:
                    ch.link(dve.tensor_scalar(rsum[:], rsum[:], floor, None, ALU.max))
                ch.link(dve.reciprocal(rsum[:], rsum[:]))
                return dve.tensor_tensor(dst[:, :, 0:k], src[:, :, 0:k], col(rsum[:], k), ALU.mult)

            def route1():
                ch.link(normalise(t1, top, 8, 1e-12))
                ch.link(dve.tensor_scalar(t2[:], t1[:], alpha[:, 0:1], None, ALU.mult))
                ch.link(dve.tensor_reduce(rsum[:], t2[:], AX_X, ALU.max))
                ch.link(dve.tensor_tensor(t3[:], t2[:], col(rsum[:], 8), ALU.is_equal))
                f8 = first8[:].unsqueeze(1).broadcast_to([P, NT, 8])
                ch.link(dve.tensor_tensor(t3[:], t3[:], f8, ALU.mult))
                ch.link(dve.tensor_reduce(rbest[:], t3[:], AX_X, ALU.max))
                ch.link(dve.scalar_tensor_tensor(out=rbest[:], in0=rsum[:], scalar=TAU, in1=rbest[:],
                                                 op0=ALU.is_lt, op1=ALU.mult))
                ch.link(dve.tensor_tensor(t3[:], f8, col(rbest[:], 8), ALU.is_equal))
                ch.link(dve.scalar_tensor_tensor(out=t2[:], in0=t2[:], scalar=TAU, in1=t3[:], op0=ALU.is_ge,
                                                 op1=ALU.max))
                ch.link(dve.tensor_tensor(t1[:], t1[:], t2[:], ALU.mult))

            def combine(m, i):
                k, first = m.top, 2 * m.pair
                size = E1 // k
                e0, e1 = (0, first) if i < 3 else (first + size * (i // 3 - 1), first + size * (i // 3))
                e1 = min(e1, m.E * m.pair)
                if e0 >= e1:
                    return
                shape = [P, NT, e1 - e0, k]
                each = lambda x: x[:, :, 0:k].unsqueeze(2).broadcast_to(shape)
                eq = EQ[:].rearrange("p t e -> p (t e)")[:, 0:NT * (e1 - e0) * k].rearrange(
                    "p (t e k) -> p t e k", t=NT, k=k)
                if i > 0:
                    ch.need(combined[0])
                if i % 3 == 0:
                    ins = dve.tensor_tensor(eq, iota_e[:, e0:e1].unsqueeze(1).unsqueeze(3).broadcast_to(shape),
                                            each(tif[:]), ALU.is_equal)
                elif i % 3 == 1:
                    ins = dve.tensor_tensor(eq, eq, each(t2[:]), ALU.mult)
                else:
                    ins = dve.tensor_reduce(CW[:, :, e0:e1], eq, AX_X, ALU.add)
                combined[0] = ch.mark(ins)

            combined = [0]

            def moe_dve(m):
                I, IP = m.I, m.IP
                W = I // m.pair

                def gate_up(pos, u):
                    s = pos % 2
                    dve.wait_ge(sil_done, u + 1)
                    wait_past(dve, ht_done, u - 1)
                    t, first = pos % m.units, pos // m.units
                    for j in range(m.pair):
                        if isinstance(u, int):
                            c = CW[:, t, first * m.pair + j:first * m.pair + j + 1]
                        else:
                            round_ = (u - (UB[m.n] + pos)) // m.units
                            c = CW[:, t, bass.ds(round_ * m.pair + (first * m.pair + j), 1)]
                        ins = dve.scalar_tensor_tensor(
                            out=HH[:, s, j * W:(j + 1) * W], in0=SIL[:, s, j * W:(j + 1) * W], scalar=c,
                            in1=bank(s)[:, I + j * W:I + (j + 1) * W], op0=ALU.mult, op1=ALU.mult)
                    ins.then_inc(h_ready, 1)

                def lo(pos, u):
                    s = pos % 2
                    dve.wait_ge(hhi_done, u + 1)
                    dve.tensor_tensor(EHL[0:IP, s, :], bank(2 + s)[0:IP, 0:256], EHH[0:IP, s, :].bitcast(F32),
                                      ALU.subtract).then_inc(hlo_done, 1)

                run_units(dve, m, gate_up, [(lo, 1)], lambda slot: combine(m, 3 + slot))
                ch.need(combined[0])

            apply_rstd(0, NH0)
            lo_parts(0, HTL, HTH)
            dve.wait_ge(w_split, 3)
            layernorm(0, XB, y_done, lambda p: 2 * p + 2)
            lo_parts(1, XL, XH)
            softmax(0, E0, bias_r0[:])
            normalise(t2, top, 4, None).then_inc(weights_ready, 1)
            dve.wait_ge(weights_ready, 1)
            for i in range(3):
                combine(MOES[0], i)
            ch.need(combined[0])
            moe_dve(MOES[0])
            layernorm(1, XA, dn_done, lambda p: UB[1] - NT + 2 * p + 2)
            lo_parts(2, XL, XH)

            for hf in range(2):
                dve.wait_ge(g_mm, 3 + hf)
                dve.tensor_scalar(KG[:, hf * BANK:(hf + 1) * BANK], bank(6 + hf), bkg[:, 0:1], None,
                                  ALU.add).then_inc(g_read, 1)
            halves = [slice(hf * BANK, (hf + 1) * BANK) for hf in range(2)]
            for hf in range(2):
                dve.wait_ge(g_read, hf + 1)
                kg = KG[:, halves[hf]]
                dve.scalar_tensor_tensor(out=KGL[:, halves[hf]], in0=kg, scalar=-1.0, in1=kg, op0=ALU.mult,
                                         op1=ALU.max).then_inc(kg_abs, 1)

            def value_lo(k, b0):
                for hf in range(2):
                    dve.wait_ge(vt_hi, 2 * k + hf + 1)
                    c = slice(hf * BANK, (hf + 1) * BANK)
                    dve.tensor_tensor(VTL[:, k, c], bank(b0 + hf), VTH[:, k, c].bitcast(F32), ALU.subtract
                                      ).then_inc(vt_lo, 1)

            value_lo(0, 0)
            for hf in range(2):
                dve.wait_ge(kg_ln, hf + 1)
                kg = KG[:, halves[hf]]
                dve.scalar_tensor_tensor(out=kg, in0=kg, scalar=0.0, in1=KGL[:, halves[hf]], op0=ALU.min,
                                         op1=ALU.subtract).then_inc(kg_log_sigmoid, 1)
            def kv_product(v):
                dve.wait_ge(vr_mm, v + 1)
                dve.tensor_tensor(spread_v(v), KT, spread_v(v), ALU.mult).then_inc(d1_done, 1)

            spread_v = lambda v: PS[:, 2 * (v % 2):2 * (v % 2) + 2, :].rearrange("p k c -> p (k c)")
            dve.wait_ge(k_ready, 4)
            kv_product(0)
            dve.wait_ge(dec_ready, 2)
            ch.link(dve.memset(DEC.rearrange("p (b s) -> p b s", b=B)[:, :, 0:1], 0.0))
            for v in range(DV1):
                if v > 0:
                    kv_product(v)
                if v == LATE_VALUES_AT:
                    value_lo(1, 6)
                dve.wait_ge(d1_done, v + 1)
                if v >= 2:
                    dve.wait_ge(qs_done, v - 1)
                dve.tensor_tensor_scan(STATE[:, v % 2, :], DEC, spread_v(v), 0.0, ALU.mult, ALU.add
                                       ).then_inc(s_done, 1)
            dve.wait_ge(s_done, DV1)
            dve.wait_ge(qs_used, DV1 - 2)
            dve.tensor_tensor(QS[:, (DV1 - 1) % 2, 0:BANK], STATE[:, (DV1 - 1) % 2, 0:BANK], QT[:, 0:BANK], ALU.mult
                              ).then_inc(qs_last, 1)
            dve.wait_ge(qs_used, DV1)
            dve.tensor_copy(OT[:, 1, BANK:2 * BANK], bank(7)).then_inc(ot_evac, 1)
            for p in range(NT // 2):
                dve.wait_ge(o_mm, p + 1)
                dve.wait_ge(sq_done, NT + 2 * p + 2)
                o = bank(p).rearrange("p (t v h) -> p t h v", t=2, v=DV1)
                for t in range(2):
                    ins = dve.tensor_tensor(OGATE[:, 2 * p + t, :].rearrange("p (h v) -> p h v", h=NH1), o[:, t],
                                            OGATE[:, 2 * p + t, :].rearrange("p (h v) -> p h v", h=NH1), ALU.mult)
                    ins.then_inc(og_ready, 1)
                for t in range(2):
                    head_sums(1, 2 * p + t, NH1)
            head_var(1, NH1, EPS_G)
            apply_rstd(1, NH1)
            lo_parts(3, HTL, HTH)
            layernorm(2, XB, y_done, lambda p: NT + 2 * p + 2)
            lo_parts(4, XL, XH)
            softmax(1, E1, None)
            route1()
            normalise(t2, t1, 8, 1e-12).then_inc(weights_ready, 1)
            dve.wait_ge(weights_ready, 2)
            for i in range(3):
                combine(MOES[1], i)
            ch.need(combined[0])
            moe_dve(MOES[1])
            layernorm(3, XA, dn_done, lambda p: UB[2] - NT + 2 * p + 2)

        @block.tensor
        def _(pe):
            def mm3(o, lhs, rhs, start, stop):
                n = 3 * len(lhs)
                i = 0
                for (lh, ll), (rh, rl) in zip(lhs, rhs):
                    for l, r in ((lh, rh), (lh, rl), (ll, rh)):
                        ins = pe.matmul(o, l, r, start=start and i == 0, stop=stop and i == n - 1,
                                        skip_group_check=True)
                        i += 1
                return ins

            def xs(t):
                return [(XH[:, k, t * P:(t + 1) * P], XL[:, k, t * P:(t + 1) * P]) for k in range(KD)]

            def xm(hf):
                return [(XH[:, k, hf * BANK:(hf + 1) * BANK], XL[:, k, hf * BANK:(hf + 1) * BANK]) for k in range(KD)]

            def ws(wh, wl, c, n):
                return [(wh[:, k, c:c + n], wl[:, k, c:c + n]) for k in range(KD)]

            pe.wait_ge(zb_set, 1)

            def keep_warm(n, b):
                for _ in range(n):
                    pe.matmul(bank(b), zb[:, 0:P], zb[:], start=True, stop=True, skip_group_check=True)

            keep_warm(18, 7)
            pe.wait_ge(ld_xt, 16)
            pe.wait_ge(ld_w0, 16)
            for g, c in ((0, IG0), (1, FG0)):
                for b in range(B):
                    for k in range(KD):
                        ins = pe.matmul(bank(g)[32 * b:32 * b + 32, 0:S], W0T[:, k, c:c + 32],
                                        XT[:, k, b * S:(b + 1) * S], start=(k == 0), stop=(k == KD - 1))
            ins.then_inc(gate_mm, 1)
            keep_warm(8, 7)
            pe.wait_ge(x0_split, 1)
            for g, c in ((2, Q0), (4, K0)):
                for hf in range(2):
                    mm3(bank(g + hf), ws(W0H, W0L, c, P), xm(hf), True, True).then_inc(qk_mm, 1)
            pe.wait_ge(x0_split, 3)
            for t in range(NT):
                if t >= 2:
                    pe.wait_ge(vo_done, t - 1)
                mm3(bank(6 + t % 2), xs(t), ws(W0H, W0L, 0, 2 * D), True, True).then_inc(vo_mm, 1)
            def gates_to_tokens(src, dst):
                for tt in range(TB):
                    ins = pe.transpose(dst[:, tt * P:(tt + 1) * P], src[:, tt * P:(tt + 1) * P], ident[:])
                ins.then_inc(gt_mm, 1)

            pe.wait_ge(ld_const, 16 * 15)
            pe.wait_ge(k_ready, 2)
            pe.wait_ge(nm_ready, 2)
            gates_to_tokens(AS, bank(4))

            def scores(u):
                b, h = u // NH0, u % NH0
                r, q = bank(u % 2), bank(2 + u % 2)
                if u >= 2:
                    pe.wait_ge(e_ready, u - 1)
                sel = sel0[:, u:u + 1].broadcast_to([P, P])
                pe.matmul(r[:, 0:3 * P], sel, NMD[:], start=True, stop=False, skip_group_check=True)
                own = r.rearrange("p (n c) -> p n c", c=P)[:, 0:3:2, :]
                pe.matmul(own, identb[:], futb[:].unsqueeze(1).broadcast_to([P, 2, P]), start=False, stop=True,
                          skip_group_check=True).then_inc(r_ready, 1)
                if u >= 2:
                    pe.wait_ge(w_ready, u - 1)
                rows = slice(32 * (h // 2), 32 * (h // 2) + 32)
                kt = KTE if h % 2 == 0 else KTO
                pe.matmul(q[:, 0:S], kt[rows, b * S:b * S + P], QT[rows, b * S:(b + 1) * S],
                          start=True, stop=False, skip_group_check=True)
                pe.matmul(q[:, S:S + P], kt[rows, b * S + P:b * S + 2 * P], QT[rows, b * S + P:b * S + 2 * P],
                          start=False, stop=True, skip_group_check=True).then_inc(qk_ready, 1)

            def values(u):
                b, h = u // NH0, u % NH0
                if u == 0:
                    pe.wait_ge(at_ready, 1)
                if h == 0 and b >= 1:
                    pe.wait_ge(ao_evac, 2 * b)
                pe.wait_ge(w_ready, u + 1)
                w = WW[:, u % 3, :]
                o = bank(4 + h // 4)[64 * (h % 2):64 * (h % 2) + 64, :]
                c = S * (h // 2 % 2)
                for tt, (w0, w1) in enumerate(((0, S), (S, S + P))):
                    v0 = ((TB * b + tt) * NH0 + h) * (DV0 + 1)
                    ins = pe.matmul(o[:, c + tt * P:c + S], VXF[:, v0:v0 + 64], w[:, w0:w1],
                                    start=(tt == 0 and c == 0), stop=(tt == 1), skip_group_check=True)
                ins.then_inc(av_done, 1)

            def heads_to_tokens(b):
                pe.wait_ge(ao_evac, 2 * (b + 1))
                pe.wait_ge(at_ready, 2)
                if b >= 1:
                    pe.wait_ge(hc_ready, b * TB)
                for tt in range(TB):
                    for p in range(NH0 // 2):
                        c = S * (p % 2) + tt * P
                        ins = pe.transpose(bank(6 + tt)[:, p * P:(p + 1) * P], AOT[:, p // 2, c:c + P], ident[:])
                    ins.then_inc(ao_tokens, 1)

            pe.wait_ge(ld_sel, 32)
            pe.wait_ge(q_ready, 2)
            pe.wait_ge(tanh_done, 1)
            pe.wait_ge(vo_done, NT)
            for u in range((B + 1) * NH0):
                if u < B * NH0:
                    scores(u)
                if 2 <= u < B * NH0 + 2:
                    values(u - 2)
                if u == FLOOR_AT:
                    pe.wait_ge(floor_ready, 1)
                    gates_to_tokens(NL, bank(7))
                if u >= NH0 and u % NH0 == TOKENS_AT:
                    heads_to_tokens(u // NH0 - 1)

            def transposes(n, src, wait_tile):
                for p in range(NT // 2):
                    for t in range(2):
                        wait_tile(2 * p + t)
                    for t in range(2):
                        for k in range(KD):
                            ins = pe.transpose(bank(p)[:, (2 * t + k) * P:(2 * t + k + 1) * P],
                                               src[:, 2 * p + t, k * P:(k + 1) * P], ident[:])
                    ins.then_inc(tp_done, 1)

            def project(n, wh, wl):
                for t in range(NT):
                    if t % 2 == 0:
                        pe.wait_ge(lo_done, n * (NT // 2) + t // 2 + 1)
                    lhs = [(HTH[:, k, t * P:(t + 1) * P], HTL[:, k, t * P:(t + 1) * P]) for k in range(KD)]
                    mm3(bank(4 + t // 2)[:, (t % 2) * D:(t % 2 + 1) * D], lhs, ws(wh, wl, 0, D),
                        False, True).then_inc(y_done, 1)

            def router(n, tp, c, E):
                for hf in range(2):
                    pe.wait_ge(lo_done, tp * (NT // 2) + 2 * (hf + 1))
                    for i in range(2 * KD):
                        ins = pe.matmul(bank(hf)[0:2 * WRC, :], WRS[:, i // 2, :],
                                        (XH, XL)[i % 2][:, i // 2, hf * BANK:(hf + 1) * BANK],
                                        start=(i == 0), stop=(i == 2 * KD - 1))
                    ins.then_inc(rt_mm, 1)
                pe.wait_ge(lt_read, 2 * n + 2)
                for t in range(NT):
                    ins = pe.matmul(bank(2)[:, t * E:(t + 1) * E], LT[:, t * P:(t + 1) * P],
                                    wr_sum[0:2 * WRC, c:c + E], start=(t == 0), stop=True, skip_group_check=True)
                ins.then_inc(rt_mm, 1)

            def residual(src):
                for t in range(NT):
                    pe.matmul(bank(4 + t // 2)[:, (t % 2) * D:(t % 2 + 1) * D], ident[:], src[:, t, :],
                              start=(t % 2 == 0), stop=True, skip_group_check=True)

            def moe_pe(m):
                I, IP, IC = m.I, m.IP, m.IC
                base = UB[m.n]
                residual(XB)
                pe.wait_ge(rt_max, m.n + 1)

                def gate_up(pos, u):
                    s, par = pos % 2, pos // m.units
                    if pos % m.units == 0:
                        first = (u - (base + pos)) // m.units if not isinstance(u, int) else 0
                        pe.wait_ge(exp_split, first + (EB[m.n] + par + 1))
                    wait_past(pe, h_ready, u - 1)
                    w = [EG_.rearrange("p (k c) -> p k c", k=KD) for EG_ in (EGH[:, par, 0:m.gcols], EGL[:, par, 0:m.gcols])]
                    ins = mm3(bank(s)[:, 0:2 * I], xs(pos % m.units), [(w[0][:, k, :], w[1][:, k, :]) for k in range(KD)],
                              True, True)
                    ins.then_inc(gu_done, 1)

                def turn(pos, u):
                    s = pos % 2
                    pe.wait_ge(h_ready, u + 1)
                    wait_past(pe, hlo_done, u - 1)
                    for j in range(2):
                        ins = pe.transpose(bank(2 + s)[0:IP, j * P:(j + 1) * P], HH[:, s, j * IP:(j + 1) * IP], ident[:])
                    ins.then_inc(ht_done, 1)

                def down(pos, u):
                    s, par = pos % 2, pos // m.units
                    pe.wait_ge(hlo_done, u + 1)
                    t = pos % m.units
                    lhs = [(EHH[0:IP, s, c * P:(c + 1) * P], EHL[0:IP, s, c * P:(c + 1) * P]) for c in range(IC)]
                    rhs = [(EDH[0:IP, par, c * D:(c + 1) * D], EDL[0:IP, par, c * D:(c + 1) * D]) for c in range(IC)]
                    ins = mm3(bank(4 + t // 2)[:, (t % 2) * D:(t % 2 + 1) * D], lhs, rhs, False, True)
                    ins.then_inc(dn_done, 1)

                run_units(pe, m, gate_up, [(turn, 1), (down, 2)])
                pe.wait_ge(dn_done, base + m.total)

            pe.wait_ge(hc_ready, NT)
            pe.wait_ge(ld_x, 16)
            residual(XA)
            transposes(0, HC, lambda t: pe.wait_ge(gated, t + 1))
            pe.wait_ge(w_split, 1)
            project(0, WO0H, WO0L)
            transposes(1, XB, lambda t: wait_x(pe, 0, t))
            pe.wait_ge(w_split, 2)
            router(0, 1, 0, E0)
            moe_pe(MOES[0])
            transposes(2, XA, lambda t: wait_x(pe, 1, t))

            pe.wait_ge(w_split, 4)

            def feature_major(b0, c, done, after=None):
                for hf in range(2):
                    if after is not None:
                        pe.wait_ge(*after(hf))
                    mm3(bank(b0 + hf), ws(W1H, W1L, c, P), xm(hf), True, True).then_inc(done, 1)

            feature_major(4, Z1, g_mm, lambda hf: (lo_done, 2 * (NT // 2) + 2 * (hf + 1)))
            for hf in range(2):
                mm3(bank(hf), ws(W1H, W1L, V1, P), xm(hf), True, True).then_inc(vt_mm, 1)
                if hf == 0:
                    for h2 in range(2):
                        pe.wait_ge(z_ready, h2 + 1)
                        pe.matmul(bank(6 + h2), wkg2[:], KGL[0:16, h2 * BANK:(h2 + 1) * BANK], start=True, stop=True
                                  ).then_inc(g_mm, 1)
            feature_major(2, K1, g_mm)
            feature_major(4, Q1, g_mm)
            def spread(v):
                s = v % 2
                if v >= 2:
                    pe.wait_ge(s_done, v - 1)
                for hf in range(2):
                    for i, part in enumerate((VTH, VTL)):
                        ins = pe.matmul(bank(2 * s + hf), rep1[:, v % 8, :], part[:, v // 8, hf * BANK:(hf + 1) * BANK],
                                        start=(i == 0), stop=(i == 1))
                ins.then_inc(vr_mm, 1)

            def gather_o(v):
                pe.wait_ge(qs_done, v + 1)
                if v == DV1 - 1:
                    pe.wait_ge(qs_last, 1)
                q = 32 * ((v % 8) // 2)
                for hf in range(2):
                    ins = pe.matmul(bank(4 + 2 * (v // 8) + hf)[q:q + 32, :], block2[:, v % 2, :],
                                    QS[:, v % 2, hf * BANK:(hf + 1) * BANK], start=(v % 2 == 0), stop=(v % 2 == 1))
                ins.then_inc(qs_used, 1)

            pe.wait_ge(vt_lo, 2)
            spread(0)
            pe.wait_ge(k_ready, 4)
            spread(1)

            def late_values(hf):
                pe.wait_ge(g_read, hf + 1)
                mm3(bank(6 + hf), ws(W1H, W1L, V1 + P, P), xm(hf), True, True).then_inc(vt_mm, 1)

            def output_gate(t):
                p = t // 2
                if t == 0:
                    pe.wait_ge(vt_lo, 4)
                    pe.wait_ge(w_split, 5)
                if t % 2 == 0 and p >= 2:
                    pe.wait_ge(og_silu, p - 1)
                b = bank(6 + p % 2)
                mm3(b[:, (t % 2) * D:(t % 2 + 1) * D], xs(t), ws(W1H, W1L, G1, D), t % 2 == 0, True)
                if t % 2:
                    for part in (BGH, BGL):
                        ins = pe.matmul(b, rep1[0:1, 0, 0:1].broadcast_to([1, P]),
                                        part.unsqueeze(1).broadcast_to([1, 2, D]), start=False, stop=True,
                                        skip_group_check=True)
                    ins.then_inc(og_mm, 1)

            pe.wait_ge(q_ready, 4)
            late_values(0)
            late_values(1)
            gate_tiles = {3: (0, 1), 4: (2, 3), 5: (4, 5), 6: (6, 7)}
            for v in range(DV1):
                if v + 2 < DV1:
                    if v + 2 == DV1 // 2:
                        pe.wait_ge(vt_lo, 4)
                    spread(v + 2)
                for t in gate_tiles.get(v, ()):
                    output_gate(t)
                if v == DV1 // 2:
                    pe.wait_ge(og_silu, NT // 2)
                gather_o(v)
            pe.wait_ge(ot_evac, 4)
            for p in range(NT // 2):
                for t in range(2):
                    for k in range(KD):
                        ins = pe.transpose(bank(p)[:, (2 * t + k) * P:(2 * t + k + 1) * P],
                                           OT[:, k, (2 * p + t) * P:(2 * p + t + 1) * P], ident[:])
                ins.then_inc(o_mm, 1)
            residual(XA)
            transposes(3, HC, lambda t: pe.wait_ge(gated, NT + t + 1))
            project(3, WO1H, WO1L)
            transposes(4, XB, lambda t: wait_x(pe, 2, t))
            router(1, 4, E0, E1)
            moe_pe(MOES[1])


def kernel(**inputs):
    import numpy as np
    import concourse.bacc as bacc
    from concourse.bass_utils import run_bass_kernel_spmd

    g = {k: np.asarray(v) for k, v in inputs.items()}
    B, S, D = g["L0_attn_x"].shape
    P = 128
    NH0, NH1 = 8, 16
    DV1, DK1 = D // NH1, P // NH1
    f32 = np.float32
    eye = np.eye(P, dtype=f32)
    rows = np.arange(P)

    odd = (rows // (P // NH0)) % 2
    rep = (rows % 32) // NH0
    sc = f32((P // NH0) ** -0.5)
    head_masks = np.stack([(odd == 0) * sc, (odd == 1) * sc, rep == 0, rep == 1], 1).astype(f32)
    sel0 = np.zeros((P, B * NH0), f32)
    for b in range(B):
        for h in range(NH0):
            sel0[32 * b + h, b * NH0 + h] = 1
            sel0[32 * b + NH0 + h, b * NH0 + h] = 1
    rep1 = np.zeros((P, 8, P), f32)
    for v in range(8):
        for h in range(NH1):
            rep1[v * NH1 + h, v, h * DK1:(h + 1) * DK1] = 1
    import ml_dtypes
    bf = ml_dtypes.bfloat16
    futb = np.where(rows[:, None] > rows[None, :], -1e30, 0.0).astype(bf)

    block2 = np.zeros((P, 2, 2 * NH1), f32)
    for i in range(2):
        block2[rows, i, i * NH1 + rows // DK1] = 1

    wr_sum = np.tile(np.eye(48, dtype=f32), (3, 1))[0:P]

    def rowsof(v):
        return np.ascontiguousarray(np.broadcast_to(v, (P,) + v.shape))
    wv1 = g["L1_attn_Wv"].reshape(NH1, DV1, D).transpose(1, 0, 2).reshape(D, D)
    arrays = {
        "x": g["L0_attn_x"],
        "xT": g["L0_attn_x"].reshape(B * S, D).T,
        "w0T": np.concatenate([g["L0_attn_Wv"], g["L0_attn_Wog"], g["L0_attn_Wq"], g["L0_attn_Wk"],
                               np.tile(g["L0_attn_Wig"], (4, 1)), np.tile(g["L0_attn_Wfg"], (4, 1))]).T,
        "wo0T": g["L0_attn_Wout"].T,
        "w1T": np.concatenate([wv1, g["L1_attn_Wg"], g["L1_attn_Wq"], g["L1_attn_Wk"],
                               np.tile(g["L1_attn_Wkg1"], (8, 1))]).T,
        "wo1T": g["L1_attn_Wo"].T,
        "wrT": np.concatenate([g["L0_ffn_router_w"], g["L1_ffn_gate_weight"]]).T,
        "gate_b": np.stack([np.tile(g["L0_attn_big"], P // NH0), np.tile(g["L0_attn_bfg"], P // NH0)], 1),
        "gamma": g["L0_attn_gamma"].reshape(D // P, P).T,
        "bias_r0": rowsof(g["L0_ffn_expert_bias"]),
        "alpha": rowsof(g["L1_ffn_layer_alpha"].reshape(1)),
        "bkg": g["L1_attn_bkg2"].reshape(P, 1),
        "bg": g["L1_attn_bg"].reshape(1, D),
        "wkg2T": g["L1_attn_Wkg2"].T,
        "gateup0": np.concatenate([g["L0_ffn_gate_proj"], g["L0_ffn_up_proj"]], 2),
        "down0": g["L0_ffn_down_proj"],
        "gateup1": g["L1_ffn_gate_up_proj"].reshape(16, 2, 2, 96, D).transpose(0, 4, 2, 1, 3).reshape(16, D, 384),
        "down1": g["L1_ffn_down_proj"].transpose(0, 2, 1).reshape(16, 192, D),
        "ident": eye,
        "identb": eye.astype(bf),
        "futb": futb,
        "head_masks": head_masks,
        "sel0": sel0,
        "rep1": rep1,
        "iota_e": rowsof(np.arange(32, dtype=f32)),
        "first8": rowsof(np.arange(8, 0, -1).astype(f32)),
        "block2": block2,
        "wr_sum": wr_sum,
    }
    nc = bacc.Bacc("TRN2", target_bir_lowering=False, num_devices=1)
    feeds, aps = {}, {}
    for name, v in arrays.items():
        v = np.ascontiguousarray(v)
        feeds[f"in_{name}"] = v
        aps[name] = nc.dram_tensor(f"in_{name}", v.shape, mybir.dt.from_np(v.dtype), kind="ExternalInput").ap()
    out = nc.dram_tensor("out_y", (B, S, D), F32, kind="ExternalOutput").ap()
    build_kernel(nc, aps, out)
    r = run_bass_kernel_spmd(nc, [feeds], core_ids=[0])
    return r.results[0]["out_y"]
```
